# Optimizing a Trainium2 kernel written in Bass

```python
import numpy as np
import jax
import jax.numpy as jnp

def _softmax(x, axis=-1):
    return jax.nn.softmax(x, axis=axis)

def _gelu(x):
    return jax.nn.gelu(x, approximate=True)

def _silu(x):
    return jax.nn.silu(x)

def _sigmoid(x):
    return jax.nn.sigmoid(x)

def _layernorm(x, axis=-1, eps=1e-05):
    m = jnp.mean(x, axis=axis, keepdims=True)
    v = jnp.var(x, axis=axis, keepdims=True)
    return (x - m) / jnp.sqrt(v + eps)

def _scatter_add(tgt, idx, src, axis=0):
    return tgt.at[idx].add(src)

def _segment_sum(src, seg, n):
    return jax.ops.segment_sum(src, seg, n)
kernel_name = 'mk_gnn_preln_d2_gnn_r32_f0a046'

def setup_inputs(seed: int=0):
    np.random.seed(seed)
    _w = jnp.asarray

    def _rec_inputs():
        import jax
        import jax.numpy as jnp
        _gk = jax.random.key(seed)
        x = -0.000202 + 1 * jax.random.normal(jax.random.fold_in(_gk, 1), (3125, 128), jnp.float32)
        _s = jax.random.randint(jax.random.fold_in(_gk, 2), (25000,), 0, 3125, jnp.int32)
        _d = jax.random.randint(jax.random.fold_in(_gk, 3), (25000,), 0, 3125, jnp.int32)
        _loop = jnp.arange(3125, dtype=jnp.int32)
        src = jnp.concatenate([_s, _d, _loop])
        dst = jnp.concatenate([_d, _s, _loop])
        _o = jnp.argsort(dst, stable=True)
        src = src[_o]
        dst = dst[_o]
        return (x, src, dst)
    x, src, dst = _rec_inputs()

    def _L0_gnn_setup():
        import jax, jax.numpy as jnp
        import numpy as np
        N, E, F, H, L = (50000, 18750, 128, 128, 5)
        key = jax.random.key(seed)
        ks = jax.random.split(key, 16)
        s = 1.0 / np.sqrt(H)
        u = lambda k, shape: jax.random.uniform(k, shape, jnp.float32, -s, s)
        return {'x': jax.random.normal(ks[0], (N, F), jnp.float32), 'edge_index': jax.random.randint(ks[1], (2, E), 0, N, jnp.int64), 'enc_w1': u(ks[2], (H, F)), 'enc_b1': u(ks[3], (H,)), 'enc_w2': u(ks[4], (H, H)), 'enc_b2': u(ks[5], (H,)), 'conv_w': u(ks[6], (L, H, H)), 'gru_wih': u(ks[7], (3 * H, H)), 'gru_whh': u(ks[8], (3 * H, H)), 'gru_bih': u(ks[9], (3 * H,)), 'gru_bhh': u(ks[10], (3 * H,)), 'dec_w1': u(ks[11], (H, H)), 'dec_b1': u(ks[12], (H,)), 'dec_w2': u(ks[13], (F, H)), 'dec_b2': u(ks[14], (F,))}
    _L0_gnn_all = _L0_gnn_setup()
    _L0_gnn_in = {k: v for k, v in _L0_gnn_all.items() if k in ('enc_w1', 'enc_b1', 'enc_w2', 'enc_b2', 'conv_w', 'gru_wih', 'gru_whh', 'gru_bih', 'gru_bhh', 'dec_w1', 'dec_b1', 'dec_w2', 'dec_b2')}
    del _L0_gnn_all

    def _L1_gnn_setup():
        import jax, jax.numpy as jnp
        import numpy as np
        N_NODES = 50000

        def _norm_adj(num_nodes, edge_index):
            row, col = (edge_index[0], edge_index[1])
            loop = jnp.arange(num_nodes, dtype=edge_index.dtype)
            row = jnp.concatenate([row, loop])
            col = jnp.concatenate([col, loop])
            ones = jnp.ones(row.shape[0], dtype=jnp.float32)
            deg = jax.ops.segment_sum(ones, row, num_segments=num_nodes)
            dinv = jnp.clip(deg, 1.0) ** (-0.5)
            v = dinv[row] * dinv[col]
            return (row, col, v)

        def _spmm(row, col, v, x, num_nodes):
            return jax.ops.segment_sum(v[:, None] * x[col], row, num_segments=num_nodes)
        key = jax.random.key(seed)
        ks = jax.random.split(key, 6)
        in_dim, hidden_dim, out_dim = (128, 256, 128)
        n_edges = 25000
        x = jax.random.normal(ks[0], (N_NODES, in_dim), dtype=jnp.float32)
        edge_index = jax.random.randint(ks[1], (2, n_edges), 0, N_NODES, dtype=jnp.int32)
        W1 = jax.random.normal(ks[2], (hidden_dim, in_dim), dtype=jnp.float32) * (1.0 / np.sqrt(in_dim))
        b1 = jax.random.normal(ks[3], (hidden_dim,), dtype=jnp.float32) * 0.01
        W2 = jax.random.normal(ks[4], (out_dim, hidden_dim), dtype=jnp.float32) * (1.0 / np.sqrt(hidden_dim))
        b2 = jax.random.normal(ks[5], (out_dim,), dtype=jnp.float32) * 0.01
        return {'x': x, 'edge_index': edge_index, 'W1': W1, 'b1': b1, 'W2': W2, 'b2': b2}
    _L1_gnn_all = _L1_gnn_setup()
    _L1_gnn_in = {k: v for k, v in _L1_gnn_all.items() if k in ('W1', 'b1', 'W2', 'b2')}
    del _L1_gnn_all
    return {'x': x, 'src': src, 'dst': dst, 'L0_gnn_enc_w1': _L0_gnn_in['enc_w1'], 'L0_gnn_enc_b1': _L0_gnn_in['enc_b1'], 'L0_gnn_enc_w2': _L0_gnn_in['enc_w2'], 'L0_gnn_enc_b2': _L0_gnn_in['enc_b2'], 'L0_gnn_conv_w': _L0_gnn_in['conv_w'], 'L0_gnn_gru_wih': _L0_gnn_in['gru_wih'], 'L0_gnn_gru_whh': _L0_gnn_in['gru_whh'], 'L0_gnn_gru_bih': _L0_gnn_in['gru_bih'], 'L0_gnn_gru_bhh': _L0_gnn_in['gru_bhh'], 'L0_gnn_dec_w1': _L0_gnn_in['dec_w1'], 'L0_gnn_dec_b1': _L0_gnn_in['dec_b1'], 'L0_gnn_dec_w2': _L0_gnn_in['dec_w2'], 'L0_gnn_dec_b2': _L0_gnn_in['dec_b2'], 'L1_gnn_W1': _L1_gnn_in['W1'], 'L1_gnn_b1': _L1_gnn_in['b1'], 'L1_gnn_W2': _L1_gnn_in['W2'], 'L1_gnn_b2': _L1_gnn_in['b2']}

def reference(x, src, dst, L0_gnn_enc_w1, L0_gnn_enc_b1, L0_gnn_enc_w2, L0_gnn_enc_b2, L0_gnn_conv_w, L0_gnn_gru_wih, L0_gnn_gru_whh, L0_gnn_gru_bih, L0_gnn_gru_bhh, L0_gnn_dec_w1, L0_gnn_dec_b1, L0_gnn_dec_w2, L0_gnn_dec_b2, L1_gnn_W1, L1_gnn_b1, L1_gnn_W2, L1_gnn_b2):
    import jax
    import jax.numpy as jnp

    def _L0_gnn_ref(x, edge_index, enc_w1, enc_b1, enc_w2, enc_b2, conv_w, gru_wih, gru_whh, gru_bih, gru_bhh, dec_w1, dec_b1, dec_w2, dec_b2):
        import jax, jax.numpy as jnp
        import numpy as np
        N, E, F, H, L = (50000, 18750, 128, 128, 5)
        src, dst = (edge_index[0], edge_index[1])
        n_nodes = x.shape[0]
        h = jnp.maximum(x @ enc_w1.T + enc_b1, 0.0) @ enc_w2.T + enc_b2

        def step(h, w):
            m = h @ w
            agg = jax.ops.segment_sum(m[src], dst, num_segments=n_nodes)
            gi = agg @ gru_wih.T + gru_bih
            gh = h @ gru_whh.T + gru_bhh
            ir, iz, i_n = jnp.split(gi, 3, axis=1)
            hr, hz, h_n = jnp.split(gh, 3, axis=1)
            r = jax.nn.sigmoid(ir + hr)
            z = jax.nn.sigmoid(iz + hz)
            n = jnp.tanh(i_n + r * h_n)
            return ((1.0 - z) * n + z * h, None)
        h, _ = jax.lax.scan(step, h, conv_w)
        h = jnp.maximum(h, 0.0)
        out = jnp.maximum(h @ dec_w1.T + dec_b1, 0.0) @ dec_w2.T + dec_b2
        return jax.nn.sigmoid(out)

    def _L1_gnn_ref(x, edge_index, W1, b1, W2, b2):
        import jax, jax.numpy as jnp
        import numpy as np
        N_NODES = 50000

        def _norm_adj(num_nodes, edge_index):
            row, col = (edge_index[0], edge_index[1])
            loop = jnp.arange(num_nodes, dtype=edge_index.dtype)
            row = jnp.concatenate([row, loop])
            col = jnp.concatenate([col, loop])
            ones = jnp.ones(row.shape[0], dtype=jnp.float32)
            deg = jax.ops.segment_sum(ones, row, num_segments=num_nodes)
            dinv = jnp.clip(deg, 1.0) ** (-0.5)
            v = dinv[row] * dinv[col]
            return (row, col, v)

        def _spmm(row, col, v, x, num_nodes):
            return jax.ops.segment_sum(v[:, None] * x[col], row, num_segments=num_nodes)
        n = x.shape[0]
        row, col, v = _norm_adj(n, edge_index)
        h = _spmm(row, col, v, x, n)
        h = jax.nn.relu(h @ W1.T + b1)
        h = _spmm(row, col, v, h, n)
        return h @ W2.T + b2
    edge_index = jnp.stack([src, dst])
    h = jnp.maximum(_layernorm(x, axis=-1), 0.0)
    x = x + _L0_gnn_ref(h, edge_index, L0_gnn_enc_w1, L0_gnn_enc_b1, L0_gnn_enc_w2, L0_gnn_enc_b2, L0_gnn_conv_w, L0_gnn_gru_wih, L0_gnn_gru_whh, L0_gnn_gru_bih, L0_gnn_gru_bhh, L0_gnn_dec_w1, L0_gnn_dec_b1, L0_gnn_dec_w2, L0_gnn_dec_b2)
    h = jnp.maximum(_layernorm(x, axis=-1), 0.0)
    x = x + _L1_gnn_ref(h, edge_index, L1_gnn_W1, L1_gnn_b1, L1_gnn_W2, L1_gnn_b2)
    return x

_drawn_inputs = setup_inputs


def setup_inputs(seed=0):
    import zlib

    import numpy as np

    out = dict(_drawn_inputs(seed))
    spreads = {}
    factors = {'L0_gnn_enc_w1': 3.483,
     'L0_gnn_enc_b1': 5.794,
     'L0_gnn_enc_w2': 3.378,
     'L0_gnn_enc_b2': 8.987,
     'L0_gnn_conv_w': 3.669,
     'L0_gnn_gru_wih': 2.794,
     'L0_gnn_gru_whh': 21.931,
     'L0_gnn_gru_bih': 200.0,
     'L0_gnn_gru_bhh': 200.0,
     'L0_gnn_dec_b1': 8.0,
     'L0_gnn_dec_b2': 5.099,
     'L1_gnn_b1': 8.0,
     'L1_gnn_b2': 5.617}
    for name, (base, spread) in spreads.items():
        noise = np.random.default_rng([zlib.crc32(name.encode()), seed]).standard_normal(out[name].shape)
        drawn = base * np.exp(spread * noise) if base else spread * noise
        out[name] = jnp.asarray(drawn.astype(out[name].dtype))
    for name, factor in factors.items():
        out[name] = (out[name] * factor).astype(out[name].dtype)
    return out
```

```python
import concourse.bass as bass
from concourse import mybir
from contextlib import ExitStack


def gnn_kernel(nc, x, src, dst, enc_w1T, enc_b1, enc_w2T, enc_b2, conv_wT, gru_wihT, gru_whhT,
               gru_bih, gru_bhh, dec_w1T, dec_b1, dec_w2T, dec_b2, l1_w1T, l1_b1, l1_w2T, l1_b2, out):
    F32, F16, BF16, I32 = mybir.dt.float32, mybir.dt.float16, mybir.dt.bfloat16, mybir.dt.int32
    FP8 = mybir.dt.float8e3
    ALU, ACT, AX = mybir.AluOpType, mybir.ActivationFunctionType, mybir.AxisListType

    N, F = x.shape
    E = src.shape[0]
    L = conv_wT.shape[0]
    G = 3 * F
    HID = l1_w1T.shape[1]
    P = 125
    T = N // P
    assert T * P == N
    W = 9
    KW = 3
    PW = 116
    assert KW * PW * W >= N
    DP = KW * PW * W
    RL = 25
    NR = E // RL
    assert NR * RL == E
    SL = 2 * P
    TR = NR - SL // RL + 1
    NS = NR // P
    assert NS * P == NR
    LIMIT = 1000.0
    MAGIC = 12582912.0
    TC = 4
    CH = [(t, min(TC, T - t)) for t in range(0, T, TC)]
    NC = len(CH)
    S0 = 64.0
    S1 = 1024.0

    src_t, dst_t = src.tensor, dst.tensor
    table = nc.dram_tensor("edge_table", (TR, 2 * SL), I32, kind="Internal").ap()
    comb_dram = nc.dram_tensor("comb_scratch", (L, F, G), F32, kind="Internal").ap()

    ctx = ExitStack()
    with ctx:
        def sb(name, shape, dt):
            return ctx.enter_context(nc.sbuf_tensor(name, shape, dt))

        def sem(name):
            return ctx.enter_context(nc.semaphore(name))

        def carve(region, at, shape, dt):
            size = {F32: 4, I32: 4, F16: 2, BF16: 2}[dt]
            n = size
            for s in shape[1:]:
                n *= s
            v = region[0:shape[0], at:at + n].bitcast(dt)
            if len(shape) == 3:
                v = v.rearrange("p (a b) -> p a b", a=shape[1])
            if len(shape) == 4:
                v = v.rearrange("p (a b c) -> p a b c", a=shape[1], b=shape[2])
            return v

        AT = sb("AT", [128, T * DP], FP8)
        CT = sb("CT", [128, T * N + 3], FP8)
        HT = sb("HT", [128, N], F32)
        H16 = sb("H16", [128, 2, T, 2, F], F16)
        AT3 = AT[:, :].rearrange("p (t d) -> p t d", t=T)
        CT3 = CT[:, 0:T * N].rearrange("p (t s) -> p t s", t=T)
        ident = sb("ident", [128, 128], F32)
        ident16 = sb("ident16", [128, 128], F16)
        comb = sb("comb", [128, 2, G], F32)
        whh = sb("whh", [128, G], F32)
        aggS = sb("aggS", [128, TC * P], F32)
        rS = sb("rS", [128, TC * P], F32)
        zS = sb("zS", [128, TC * P], F32)
        nS = sb("nS", [128, TC * P], F32)
        bias = sb("bias", [128, 16], F32)
        dec1 = sb("dec1", [128, F], F32)
        dec2 = sb("dec2", [128, F], F32)
        dec2b = sb("dec2b", [128, F], F32)
        yS = sb("yS", [128, TC * F], F32)
        deg = sb("deg", [128, T], F32)
        dinv = sb("dinv", [128, T], F32)
        dinvs = sb("dinvs", [128, T], F32)
        stat = sb("stat", [128, TC, 6], F32)
        mv = sb("mv", [128, T, 2], F32)
        lnsc = sb("lnsc", [128, T], F32)
        chk = sb("chk", [128, 4], F32)
        flag_f = sb("flag_f", [1, 4], F32)
        flag = sb("flag", [1, 1], I32)
        mhalf = sb("mhalf", [128, T], F32)
        lnb = sb("lnb", [128, T], F32)
        X32 = H16[:, 1, :, :, :].rearrange("p t h f -> p (t h f)").bitcast(F32).rearrange("p (t f) -> p t f", t=T)
        (B_R, B_Z, B_HN, B_IN, B_E1, B_E2, B_D1, B_L1) = range(8)

        PS = [ctx.enter_context(nc.psum_tensor(f"PS{i}", [128, 512], F32)) for i in range(8)]

        o = [0]

        def early(shape, dt):
            size = {F32: 4, I32: 4, F16: 2, BF16: 2}[dt]
            n = size
            for s in shape[1:]:
                n *= s
            v = carve(CT, o[0], shape, dt)
            o[0] += (n + 31) // 32 * 32
            return v

        ones = early([128, 128], F32)
        samp_i = early([P, NS, RL], I32)
        samp = early([P, NS], F32)
        diag = early([P, NS, P], F32)
        junk = early([P, NS * P], F32)
        wstart = early([PW, KW], F32)
        wstart1 = early([PW, KW], F32)
        cnt = early([PW, KW], F32)
        idx = early([PW, KW], I32)
        Gt = early([PW, KW, 2 * SL], I32)
        tf = early([PW, KW, SL], F32)
        pf = early([PW, KW, SL], F32)
        kf = early([PW, KW, SL], F32)
        pT = early([P, 2 * KW, PW], F32)
        kT = early([P, 2 * KW, PW], F32)
        iotaP = early([P, 128], BF16)
        iotaK = early([P, 226], BF16)
        NG = 6
        ohP = early([P, NG * 4, 126], BF16)
        ohK = early([P, NG * 4, 226], BF16)
        enc1 = early([128, F], F32)
        enc2 = early([128, F], F32)
        convT = early([128, L, F], F32)
        wih = early([128, G], F32)
        combS = early([128, L, G], F32)
        assert o[0] <= T * N, o[0]

        p2 = [0]

        def late(shape, dt):
            size = {F32: 4, I32: 4, F16: 2, BF16: 2}[dt]
            n = size
            for d in shape[1:]:
                n *= d
            v = carve(AT, p2[0], shape, dt)
            p2[0] += (n + 31) // 32 * 32
            return v

        w1 = late([128, HID], F32)
        w2 = late([128, HID // F, F], F32)
        l1b2 = late([128, F], F32)
        onesL = late([128, 128], F32)
        dinvB = late([128, N], F32)
        diagD = late([P, T, P], F32)
        U32 = late([P, T, F], F32)
        OUT = late([P, T, F], F32)
        V16 = H16[:, 0, :, :, :]
        Z16 = late([P, T, 2 * F], F16).rearrange("p t (h f) -> p t h f", h=2)
        assert p2[0] <= T * DP

        gp = [0, 0]

        def spare(r, shape, dt):
            n = 2 if dt == F16 else 4
            for d in shape[1:]:
                n *= d
            v = carve((AT, CT)[r], gp[r], shape, dt)
            gp[r] += (n + 31) // 32 * 32
            return v

        gH, gA, gB, gD, gH1, gH2 = [spare(0, [128, N], F32) for _ in range(6)]
        gX, gU = [spare(1, [P, T, F], F32) for _ in range(2)]
        EC = E // T
        ebuf = spare(1, [1, 2, EC], I32)
        genc1, genc2 = [spare(1, [128, F], F32) for _ in range(2)]
        gcw = spare(1, [128, G], F32)
        gw1 = spare(1, [128, HID], F32)
        gw2 = spare(1, [128, HID // F, F], F32)
        gb2 = spare(1, [128, 1], F32)
        assert gp[0] <= T * DP and gp[1] <= T * N

        AGG, RB, ZB, NB, IB, TB, CB = (0, 1), 2, 3, 4, 5, 6, 7
        NBLK = T * T
        NCG = (NBLK + 3) // 4
        CPS = 6
        SPOT = [3, 7, 11, 15, 19, 23]
        cgroups = lambda q: [m for m in range(CPS * q, CPS * q + CPS) if m < NCG]

        s_tab = sem("s_tab"); s_samp = sem("s_samp"); s_idxl = sem("s_idxl")
        s_id = sem("s_id"); s_ones = sem("s_ones"); s_ws = sem("s_ws"); s_iota = sem("s_iota")
        s_diag = sem("s_diag"); s_bc = sem("s_bc"); s_idx = sem("s_idx")
        s_gath = [sem(f"s_gath{k}") for k in range(KW)]
        s_keys = sem("s_keys"); s_ktr = sem("s_ktr"); s_kt = sem("s_kt")
        s_oh = sem("s_oh"); s_win = sem("s_win"); s_winfree = sem("s_winfree")
        s_wts = sem("s_wts"); s_mhalf = sem("s_mhalf"); s_mv = sem("s_mv"); s_rs = sem("s_rs"); s_deg = sem("s_deg"); s_x = sem("s_x"); s_x2 = sem("s_x2"); s_wts1 = sem("s_wts1")
        s_ln = sem("s_ln"); s_xn = sem("s_xn"); s_eX = sem("s_eX"); s_eXs = sem("s_eXs"); s_e1 = sem("s_e1")
        s_e1s = sem("s_e1s"); s_e2 = sem("s_e2"); s_eh = sem("s_eh"); s_eT = sem("s_eT"); s_eTs = sem("s_eTs")
        s_ehi = sem("s_ehi"); s_elo = sem("s_elo"); s_bcused = sem("s_bcused"); s_bias = sem("s_bias")
        s_id16 = sem("s_id16"); s_cm = sem("s_cm"); s_cms = sem("s_cms"); s_combst = sem("s_combst")
        s_comb = [sem("s_comb0"), sem("s_comb1")]
        s_S = sem("s_S"); s_agg = sem("s_agg"); s_gN = sem("s_gN"); s_gR = sem("s_gR"); s_gZ = sem("s_gZ")
        s_gI = sem("s_gI"); s_r = sem("s_r"); s_z = sem("s_z"); s_n = sem("s_n"); s_t1 = sem("s_t1"); s_t2 = sem("s_t2")
        s_h = sem("s_h"); s_tr = sem("s_tr"); s_hi = sem("s_hi"); s_lo = sem("s_lo"); s_cfull = sem("s_cfull")
        s_cev = [sem("s_cevd"), sem("s_ceva")]
        s_d1 = sem("s_d1"); s_d1s = sem("s_d1s"); s_d2 = sem("s_d2"); s_d2b = sem("s_d2b"); s_sg = sem("s_sg")
        s_x1 = sem("s_x1"); s_lsc = sem("s_lsc"); s_diagD = sem("s_diagD"); s_dB = sem("s_dB"); s_dBs = sem("s_dBs")
        s_u = sem("s_u"); s_uhl = sem("s_uhl"); s_1S = sem("s_1S"); s_1a = sem("s_1a"); s_1g = sem("s_1g")
        s_1h = sem("s_1h"); s_1p = sem("s_1p"); s_1hi = sem("s_1hi"); s_1lo = sem("s_1lo")
        s_2S = sem("s_2S"); s_2a = sem("s_2a"); s_2t = sem("s_2t"); s_2o = sem("s_2o"); s_onesL = sem("s_onesL")
        s_chk = sem("s_chk"); s_chksum = sem("s_chksum"); s_flag = sem("s_flag")
        g_x = sem("g_x"); g_w = sem("g_w"); g_mv = sem("g_mv"); g_rs = sem("g_rs"); g_ln = sem("g_ln")
        g_un = sem("g_un"); g_ut = sem("g_ut"); g_utc = sem("g_utc"); g_e1 = sem("g_e1"); g_e1s = sem("g_e1s")
        g_e2 = sem("g_e2"); g_h0 = sem("g_h0"); g_cw = sem("g_cw"); g_agg = sem("g_agg"); g_gt = sem("g_gt")
        g_rz = sem("g_rz"); g_t2 = sem("g_t2"); g_tn = sem("g_tn"); g_hn = sem("g_hn"); g_rh = sem("g_rh")
        g_d1 = sem("g_d1"); g_d1s = sem("g_d1s"); g_d2 = sem("g_d2"); g_d2b = sem("g_d2b"); g_sg = sem("g_sg")
        g_x1 = sem("g_x1"); g_deg = sem("g_deg"); g_dinv = sem("g_dinv"); g_a1 = sem("g_a1"); g_w1 = sem("g_w1")
        g_w1s = sem("g_w1s"); g_w2 = sem("g_w2"); g_w2s = sem("g_w2s"); g_a2 = sem("g_a2"); g_ot = sem("g_ot")
        g_o = sem("g_o"); g_out = sem("g_out"); g_eb = sem("g_eb"); g_ebfree = sem("g_ebfree"); g_edge = sem("g_edge"); g_tick = sem("g_tick")
        g_chain = sem("g_chain")
        s_chain = sem("s_chain"); s_out = sem("s_out"); s_built = sem("s_built")

        block = ctx.enter_context(nc.Block())

        def evac_block_group(eng, m):
            b0, nb = 4 * m, min(4, NBLK - 4 * m)
            eng.wait_ge(s_cfull, m + 1)
            if 4 * m + nb > T * (T - 1):
                eng.wait_ge(s_deg, T)
            if m < 2:
                eng.wait_ge(s_combst, 16)
            o_, i_ = CT[0:P, b0 * P:(b0 + nb) * P], PS[CB][0:P, 0:nb * P]
            if m % 2 == 0:
                nc.vector.tensor_copy(o_, i_, saturate=False).then_inc(s_cev[0], 1)
            else:
                nc.scalar.activation(o_, i_, ACT.Copy, saturate=False).then_inc(s_cev[1], 1)

        def general_vector(dve):
            n = [0]

            def link(ins):
                n[0] += 1
                ins.then_inc(g_chain, 1)
                dve.wait_ge(g_chain, n[0])

            def norm(k):
                for t in range(T):
                    link(nc.vector.bn_stats(stat[0:P, 0, :], gX[:, t, :]))
                    link(nc.vector.bn_aggr(mv[0:P, t, :], stat[0:P, 0, :]))
                nc.vector.tensor_scalar(mv[0:P, :, 1], mv[0:P, :, 1], 1e-5, None, ALU.add).then_inc(g_mv, 1)
                dve.wait_ge(g_rs, k + 1)
                nc.vector.scalar_tensor_tensor(lnb[0:P, :], mv[0:P, :, 0], -1.0, lnsc[0:P, :], ALU.mult, ALU.mult
                                               ).then_inc(g_ln, 1)

            def edges(first, to, frm, fi, ti):
                with dve.Fori(0, T) as k:
                    dve.wait_ge(g_eb, (first + k + 1) * 32)
                    dve.sem_inc(g_tick, 1)
                    with dve.Fori(0, EC) as i:
                        a = dve.value_load(ebuf[0:1, ti, bass.ds(i, 1)], min_val=0, max_val=N - 1)
                        if frm is None:
                            ins = nc.vector.tensor_scalar(to[:, bass.ds(a, 1)], to[:, bass.ds(a, 1)], 1.0, None, ALU.add)
                        else:
                            b = dve.value_load(ebuf[0:1, fi, bass.ds(i, 1)], min_val=0, max_val=N - 1)
                            ins = nc.vector.tensor_tensor(to[:, bass.ds(a, 1)], to[:, bass.ds(a, 1)],
                                                          frm[:, bass.ds(b, 1)], ALU.add)
                        ins.then_inc(g_edge, 1)
                        dve.wait_ge(g_edge, i + 1)
                    dve.sem_clear(g_edge)
                    dve.sem_inc(g_ebfree, 1)

            dve.sem_inc(g_ebfree, 1)
            dve.wait_ge(g_x, 16)
            norm(0)
            dve.wait_ge(g_h0, NC)
            with dve.Fori(0, L) as l:
                nc.vector.memset(gA, 0.0).then_inc(g_agg, 1)
                dve.wait_ge(g_agg, l * 2 + 1)
                dve.sem_inc(g_tick, 1)
                edges(l * T, gA, gH, 0, 1)
                dve.sem_inc(g_agg, 1)
                for c, (t0, nt) in enumerate(CH):
                    w = nt * P
                    H = gH[:, t0 * P:t0 * P + w]
                    dve.wait_ge(g_rz, l * NC + (c + 1))
                    nc.vector.scalar_tensor_tensor(rS[:, 0:w], PS[NB][:, 0:w], bias[:, B_HN:B_HN + 1], rS[:, 0:w],
                                                   ALU.add, ALU.mult).then_inc(g_t2, 1)
                    dve.wait_ge(g_t2, l * (2 * NC) + (2 * c + 1))
                    nc.vector.tensor_tensor(rS[:, 0:w], PS[IB][:, 0:w], rS[:, 0:w], ALU.add).then_inc(g_t2, 1)
                    dve.wait_ge(g_tn, l * (3 * NC) + (3 * c + 1))
                    nc.vector.tensor_tensor(H, H, nS[:, 0:w], ALU.subtract).then_inc(g_tn, 1)
                    dve.wait_ge(g_tn, l * (3 * NC) + (3 * c + 2))
                    nc.vector.tensor_tensor(H, H, zS[:, 0:w], ALU.mult).then_inc(g_tn, 1)
                    dve.wait_ge(g_tn, l * (3 * NC) + (3 * c + 3))
                    nc.vector.tensor_tensor(H, H, nS[:, 0:w], ALU.add).then_inc(g_hn, 1)
            dve.wait_ge(g_hn, L * NC)
            nc.vector.tensor_scalar(gH, gH, 0.0, None, ALU.max).then_inc(g_rh, 1)
            for c, (t0, nt) in enumerate(CH):
                y = yS[0:P, 0:nt * F].rearrange("p (t f) -> p t f", t=nt)
                dve.wait_ge(g_d2, c + 1)
                nc.vector.tensor_tensor(y, PS[CB][0:P, 0:nt * F].rearrange("p (t f) -> p t f", t=nt),
                                        dec2b[0:P, :].unsqueeze(1).to_broadcast([P, nt, F]), ALU.add).then_inc(g_d2b, 1)
                dve.wait_ge(g_sg, c + 1)
                nc.vector.tensor_tensor(gX[:, t0:t0 + nt, :], gX[:, t0:t0 + nt, :], y, ALU.add).then_inc(g_x1, 1)
                dve.wait_ge(g_x1, c + 1)
            norm(1)
            link(nc.vector.memset(gD, 1.0))
            edges(L * T, gD, None, 0, 0)
            dve.sem_inc(g_deg, 1)
            dve.wait_ge(g_utc, 2 * NC)
            dve.wait_ge(g_dinv, 1)
            link(nc.vector.tensor_tensor(gB, gB, gD, ALU.mult))
            link(nc.vector.tensor_copy(gA, gB))
            edges((L + 1) * T, gA, gB, 1, 0)
            nc.vector.tensor_tensor(gA, gA, gD, ALU.mult).then_inc(g_a1, 1)
            for c, (t0, nt) in enumerate(CH):
                cs = slice(t0 * P, (t0 + nt) * P)
                dve.wait_ge(g_w2, c + 1)
                nc.vector.tensor_tensor(gB[:, cs], PS[NB][:, 0:nt * P], gD[:, cs], ALU.mult).then_inc(g_w2s, 1)
            dve.wait_ge(g_w2s, NC)
            link(nc.vector.tensor_copy(gA, gB))
            edges((L + 2) * T, gA, gB, 1, 0)
            dve.wait_ge(g_w, 16 * 5)
            link(nc.vector.tensor_tensor(gA, gA, gD, ALU.mult))
            nc.vector.tensor_scalar(gA, gA, gb2[:, 0:1], None, ALU.add).then_inc(g_a2, 1)
            for c, (t0, nt) in enumerate(CH):
                dve.wait_ge(g_ot, c + 1)
                nc.vector.tensor_tensor(gX[:, t0:t0 + nt, :], gX[:, t0:t0 + nt, :],
                                        PS[TB][0:P, 0:nt * F].rearrange("p (t f) -> p t f", t=nt), ALU.add
                                        ).then_inc(g_o, 1)

        def general_tensor(pe):
            def to_features(k):
                for c, (t0, nt) in enumerate(CH):
                    pe.wait_ge(g_un, k * T + t0 + nt)
                    if k * NC + c >= 1:
                        pe.wait_ge(g_utc, k * NC + c)
                    for j in range(nt):
                        last = nc.tensor.transpose(PS[TB][:, j * P:(j + 1) * P], gU[:, t0 + j, :], ident[0:P, 0:P])
                    last.then_inc(g_ut, 1)

            to_features(0)
            pe.wait_ge(g_w, 16 * 5)
            for c, (t0, nt) in enumerate(CH):
                cs = slice(t0 * P, (t0 + nt) * P)
                pe.wait_ge(g_utc, c + 1)
                nc.tensor.matmul(PS[RB][:, 0:nt * P], genc1, gB[:, cs], start=True, stop=True).then_inc(g_e1, 1)
                pe.wait_ge(g_e1s, c + 1)
                nc.tensor.matmul(PS[ZB][:, 0:nt * P], genc2, gA[:, cs], start=True, stop=True).then_inc(g_e2, 1)
                pe.wait_ge(g_h0, c + 1)
            with pe.Fori(0, L) as l:
                pe.wait_ge(g_cw, l * 16 + 16)
                pe.wait_ge(g_agg, l * 2 + 2)
                for c, (t0, nt) in enumerate(CH):
                    w = nt * P
                    H, A = gH[:, t0 * P:t0 * P + w], gA[:, t0 * P:t0 * P + w]
                    if c >= 1:
                        pe.wait_ge(g_hn, l * NC + c)
                    for k, b in enumerate((RB, ZB)):
                        nc.tensor.matmul(PS[b][:, 0:w], whh[:, k * F:(k + 1) * F], H, start=True, stop=False)
                        nc.tensor.matmul(PS[b][:, 0:w], gcw[:, k * F:(k + 1) * F], A, start=False, stop=True)
                    nc.tensor.matmul(PS[NB][:, 0:w], whh[:, 2 * F:G], H, start=True, stop=True)
                    nc.tensor.matmul(PS[IB][:, 0:w], gcw[:, 2 * F:G], A, start=True, stop=True).then_inc(g_gt, 1)
            pe.wait_ge(g_rh, 1)
            for c, (t0, nt) in enumerate(CH):
                cs = slice(t0 * P, (t0 + nt) * P)
                if c >= 1:
                    pe.wait_ge(g_d2b, c)
                nc.tensor.matmul(PS[RB][:, 0:nt * P], dec1[:, :], gH[:, cs], start=True, stop=True).then_inc(g_d1, 1)
                pe.wait_ge(g_d1s, c + 1)
                for j in range(nt):
                    last = nc.tensor.matmul(PS[CB][0:P, j * F:(j + 1) * F], gB[:, (t0 + j) * P:(t0 + j + 1) * P],
                                            dec2[:, :], start=True, stop=True)
                last.then_inc(g_d2, 1)
            to_features(1)
            pe.wait_ge(g_a1, 1)
            for c, (t0, nt) in enumerate(CH):
                cs = slice(t0 * P, (t0 + nt) * P)
                if c >= 1:
                    pe.wait_ge(g_w2s, c)
                for k in range(HID // F):
                    last = nc.tensor.matmul(PS[RB + k][:, 0:nt * P], gw1[:, k * F:(k + 1) * F], gA[:, cs],
                                            start=True, stop=True)
                last.then_inc(g_w1, 1)
                pe.wait_ge(g_w1s, 2 * (c + 1))
                for k in range(HID // F):
                    last = nc.tensor.matmul(PS[NB][:, 0:nt * P], gw2[:, k, :], (gH1, gH2)[k][:, cs],
                                            start=(k == 0), stop=(k == 1))
                last.then_inc(g_w2, 1)
            pe.wait_ge(g_a2, 1)
            for c, (t0, nt) in enumerate(CH):
                if c >= 1:
                    pe.wait_ge(g_o, c)
                for j in range(nt):
                    last = nc.tensor.transpose(PS[TB][0:P, j * F:(j + 1) * F], gA[:, (t0 + j) * P:(t0 + j + 1) * P],
                                               ident[:, :])
                last.then_inc(g_ot, 1)

        def general_scalar(act):
            def normalized(k):
                act.wait_ge(g_ln, k + 1)
                if k:
                    act.wait_ge(g_ut, NC)
                for t in range(T):
                    nc.scalar.activation(gU[:, t, :], gX[:, t, :], ACT.Relu, bias=lnb[0:P, t:t + 1],
                                         scale=lnsc[0:P, t:t + 1]).then_inc(g_un, 1)
                for c, (t0, nt) in enumerate(CH):
                    act.wait_ge(g_ut, k * NC + c + 1)
                    nc.scalar.activation(gB[:, t0 * P:(t0 + nt) * P], PS[TB][:, 0:nt * P], ACT.Copy).then_inc(g_utc, 1)

            normalized(0)
            for c, (t0, nt) in enumerate(CH):
                cs = slice(t0 * P, (t0 + nt) * P)
                act.wait_ge(g_e1, c + 1)
                nc.scalar.activation(gA[:, cs], PS[RB][:, 0:nt * P], ACT.Relu, bias=bias[:, B_E1:B_E1 + 1]
                                     ).then_inc(g_e1s, 1)
                act.wait_ge(g_e2, c + 1)
                nc.scalar.activation(gH[:, cs], PS[ZB][:, 0:nt * P], ACT.Identity, bias=bias[:, B_E2:B_E2 + 1]
                                     ).then_inc(g_h0, 1)
            with act.Fori(0, L) as l:
                for c, (t0, nt) in enumerate(CH):
                    w = nt * P
                    act.wait_ge(g_gt, l * NC + (c + 1))
                    nc.scalar.activation(rS[:, 0:w], PS[RB][:, 0:w], ACT.Sigmoid, bias=bias[:, B_R:B_R + 1])
                    nc.scalar.activation(zS[:, 0:w], PS[ZB][:, 0:w], ACT.Sigmoid, bias=bias[:, B_Z:B_Z + 1]
                                         ).then_inc(g_rz, 1)
                    act.wait_ge(g_t2, l * (2 * NC) + (2 * c + 2))
                    nc.scalar.activation(nS[:, 0:w], rS[:, 0:w], ACT.Tanh, bias=bias[:, B_IN:B_IN + 1]).then_inc(g_tn, 1)
                    act.wait_ge(g_hn, l * NC + (c + 1))
            for c, (t0, nt) in enumerate(CH):
                act.wait_ge(g_d1, c + 1)
                nc.scalar.activation(gB[:, t0 * P:(t0 + nt) * P], PS[RB][:, 0:nt * P], ACT.Relu,
                                     bias=bias[:, B_D1:B_D1 + 1]).then_inc(g_d1s, 1)
                act.wait_ge(g_d2b, c + 1)
                nc.scalar.activation(yS[0:P, 0:nt * F], yS[0:P, 0:nt * F], ACT.Sigmoid).then_inc(g_sg, 1)
                act.wait_ge(g_x1, c + 1)
            normalized(1)
            for c, (t0, nt) in enumerate(CH):
                act.wait_ge(g_w1, c + 1)
                for k in range(HID // F):
                    nc.scalar.activation((gH1, gH2)[k][:, t0 * P:(t0 + nt) * P], PS[RB + k][:, 0:nt * P], ACT.Relu,
                                         bias=bias[:, B_L1 + k:B_L1 + k + 1]).then_inc(g_w1s, 1)

        @block.sync
        def _(sp):
            sp.dma_start(samp_i, dst.rearrange("(p a b) -> p a b", p=P, a=NS)).then_inc(s_samp, 16)
            sp.dma_start(table[:, 0:SL], bass.AP(src_t, 0, [[RL, TR], [1, SL]])).then_inc(s_tab, 16)
            sp.dma_start(table[:, SL:2 * SL], bass.AP(dst_t, 0, [[RL, TR], [1, SL]])).then_inc(s_tab, 16)
            sp.dma_start(X32[0:P], x.rearrange("(t p) f -> p t f", p=P)).then_inc(s_x, 16)
            for d, v in ((enc1, enc_w1T), (enc2, enc_w2T), (convT, conv_wT.rearrange("l k m -> k l m")),
                         (wih, gru_wihT), (whh[:, :], gru_whhT),
                         (bias[:, 4:5], enc_b1), (bias[:, 5:6], enc_b2), (bias[:, 6:7], dec_b1),
                         (bias[:, 7:9], l1_b1), (bias[:, 9:12], gru_bih), (bias[:, 12:15], gru_bhh),
                         (dec1[:, :], dec_w1T), (dec2[:, :], dec_w2T), (dec2b[:, :], dec_b2.to_broadcast([128, F]))):
                sp.dma_start(d, v).then_inc(s_wts, 16)
            sp.wait_ge(s_cms, L)
            sp.dma_start(comb_dram.rearrange("l k m -> k l m"), combS).then_inc(s_combst, 16)
            sp.wait_ge(s_combst, 16)
            for l in range(L):
                if l >= 2:
                    sp.wait_ge(s_gI, (l - 1) * NC)
                sp.dma_start(comb[:, l % 2, :], comb_dram[l, :, :]).then_inc(s_comb[l % 2], 16)
            sp.wait_ge(s_S, (L - 1) * NC)
            sp.dma_start(X32[0:P], x.rearrange("(t p) f -> p t f", p=P)).then_inc(s_x2, 16)
            sp.wait_ge(s_S, L * NC)
            sp.dma_start(w1, l1_w1T).then_inc(s_wts1, 16)
            sp.dma_start(w2, l1_w2T).then_inc(s_wts1, 16)
            sp.dma_start(l1b2, l1_b2.to_broadcast([128, F])).then_inc(s_wts1, 16)
            for c, (t0, nt) in enumerate(CH):
                sp.wait_ge(s_2o, c + 1)
                sp.dma_start(out.rearrange("(t p) f -> p t f", p=P)[:, t0:t0 + nt, :],
                             OUT[:, t0:t0 + nt, :]).then_inc(s_out, 16)
            sp.wait_ge(s_out, 16 * NC)
            sp.wait_ge(s_flag, 1)
            with sp.If(sp.value_load(flag[0:1, 0:1], min_val=0, max_val=1000) > 0):
                sp.dma_start(gX, x.rearrange("(t p) f -> p t f", p=P)).then_inc(g_x, 16)
                for d, v in ((genc1, enc_w1T), (genc2, enc_w2T), (gw1, l1_w1T), (gw2, l1_w2T),
                             (gb2, l1_b2.rearrange("a f -> f a"))):
                    sp.dma_start(d, v).then_inc(g_w, 16)

                def edge_loads(first):
                    with sp.Fori(0, T) as k:
                        sp.wait_ge(g_ebfree, first + k + 1)
                        sp.dma_start(ebuf[:, 0, :], src.rearrange("(k e) -> k e", e=EC)[bass.ds(k, 1), :]
                                     ).then_inc(g_eb, 16)
                        sp.dma_start(ebuf[:, 1, :], dst.rearrange("(k e) -> k e", e=EC)[bass.ds(k, 1), :]
                                     ).then_inc(g_eb, 16)

                with sp.Fori(0, L) as l:
                    sp.wait_ge(g_h0, NC)
                    sp.wait_ge(g_hn, l * NC)
                    sp.dma_start(gcw.unsqueeze(1), comb_dram[bass.ds(l, 1), :, :].rearrange("a k m -> k a m")
                                 ).then_inc(g_cw, 16)
                    edge_loads(l * T)
                for n in range(3):
                    edge_loads((L + n) * T)
                for c, (t0, nt) in enumerate(CH):
                    sp.wait_ge(g_o, c + 1)
                    sp.dma_start(out.rearrange("(t p) f -> p t f", p=P)[:, t0:t0 + nt, :],
                                 gX[:, t0:t0 + nt, :]).then_inc(g_out, 16)
                sp.wait_ge(g_out, 16 * NC)

        @block.gpsimd
        def _(pool):
            pool.memset(mhalf[:, :], -0.5).then_inc(s_mhalf, 1)
            pool.memset(ones, 1.0).then_inc(s_ones, 1)
            pool.memset(ident[:, :], 0.0).then_inc(s_id, 1)
            pool.wait_ge(s_id, 1)
            pool.affine_select(out=ident[:, :], in_=ident[:, :], compare_op=ALU.not_equal, fill=1.0,
                               base=0, pattern=[[-1, 128]], channel_multiplier=1).then_inc(s_id, 1)
            pool.iota(wstart, [[W * PW, KW]], base=0, channel_multiplier=W,
                      allow_small_or_imprecise_dtypes=True).then_inc(s_ws, 1)
            pool.iota(wstart1, [[W * PW, KW]], base=-1, channel_multiplier=W,
                      allow_small_or_imprecise_dtypes=True).then_inc(s_ws, 1)
            pool.iota(iotaP[:, 0:P], [[1, P]], base=0, channel_multiplier=0,
                      allow_small_or_imprecise_dtypes=True).then_inc(s_iota, 1)
            pool.iota(iotaK[:, 0:W * T], [[1, W * T]], base=1, channel_multiplier=0,
                      allow_small_or_imprecise_dtypes=True).then_inc(s_iota, 1)
            pool.wait_ge(s_mhalf, 1)
            pool.wait_ge(s_mv, 1)
            pool.tensor_tensor(lnsc[0:P, :], mv[0:P, :, 1], mhalf[0:P, :], ALU.pow).then_inc(s_rs, 1)
            pool.wait_ge(s_idx, 1)
            pool.wait_ge(s_tab, 32)
            for k in range(KW):
                pool.indirect_dma_start(out=Gt[:, k, :], out_offset=None, in_=table[:, :],
                                        in_offset=bass.IndirectOffsetOnAxis(ap=idx[:, k:k + 1], axis=0)
                                        ).then_inc(s_gath[k], 16)

            for c, (t0, nt) in enumerate(CH):
                pool.wait_ge(s_ehi, c + 1)
                pool.tensor_tensor(H16[0:P, 0, t0:t0 + nt, 1, :],
                                   yS[0:P, 0:nt * F].rearrange("p (t f) -> p t f", t=nt),
                                   H16[0:P, 0, t0:t0 + nt, 0, :], ALU.subtract).then_inc(s_elo, 1)
            pool.wait_ge(s_mv, 2)
            pool.tensor_tensor(dinv[0:P, :], deg[0:P, :], mhalf[0:P, :], ALU.pow).then_inc(s_rs, 1)
            pool.tensor_tensor(lnsc[0:P, :], mv[0:P, :, 1], mhalf[0:P, :], ALU.pow).then_inc(s_rs, 1)
            pool.wait_ge(s_S, L * NC)
            pool.memset(onesL, 1.0).then_inc(s_onesL, 1)
            pool.wait_ge(s_flag, 1)
            with pool.If(pool.value_load(flag[0:1, 0:1], min_val=0, max_val=1000) > 0):
                for k in range(2):
                    pool.wait_ge(g_mv, k + 1)
                    pool.tensor_tensor(lnsc[0:P, :], mv[0:P, :, 1], mhalf[0:P, :], ALU.pow).then_inc(g_rs, 1)
                pool.wait_ge(g_deg, 1)
                pool.tensor_tensor(gD, gD, mhalf[:, 0:1].to_broadcast([128, N]), ALU.pow).then_inc(g_dinv, 1)

        @block.vector
        def _(dve):
            n = [0]

            def link(ins):
                n[0] += 1
                ins.then_inc(s_chain, 1)
                dve.wait_ge(s_chain, n[0])

            dve.wait_ge(s_x, 16)

            def norm_stats(t0, t1):
                for t in range(t0, t1):
                    last = nc.vector.bn_stats(stat[0:P, t - t0, :], X32[0:P, t, :])
                link(last)
                for t in range(t0, t1):
                    last = nc.vector.bn_aggr(mv[0:P, t, :], stat[0:P, t - t0, :])
                link(last)

            for t0, nt in CH:
                norm_stats(t0, t0 + nt)
            nc.vector.tensor_scalar(mv[0:P, :, 1], mv[0:P, :, 1], 1e-5, None, ALU.add).then_inc(s_mv, 1)
            dve.wait_ge(s_rs, 1)
            nc.vector.scalar_tensor_tensor(lnb[0:P, :], mv[0:P, :, 0], -1.0, lnsc[0:P, :], ALU.mult, ALU.mult
                                           ).then_inc(s_ln, 1)
            dve.wait_ge(s_samp, 16)
            link(nc.vector.tensor_copy(samp, samp_i[:, :, 0]))
            dve.wait_ge(s_id, 2)
            nc.vector.tensor_tensor(diag, ident[0:P, 0:P].unsqueeze(1).to_broadcast([P, NS, P]),
                                    samp.unsqueeze(2).to_broadcast([P, NS, P]), ALU.mult).then_inc(s_diag, 1)
            nc.vector.memset(cnt, 0.0)
            dve.wait_ge(s_ws, 2)
            dve.wait_ge(s_bc, 5)
            link(nc.vector.tensor_copy(junk.rearrange("p (a b) -> p a b", a=5)[:, 0, :], PS[0][0:P, 0:425]))
            for q in range(1, 5):
                last = nc.vector.tensor_copy(junk[:, 425 * q:425 * q + 425], PS[q][0:P, 0:425])
            link(last)
            dve.sem_inc(s_bcused, 1)
            for k in range(KW):
                last = nc.vector.tensor_scalar(diag[0:PW].rearrange("p a b -> p (a b)"), junk[0:PW, :],
                                               wstart[:, k:k + 1], None, ALU.is_lt, ALU.add,
                                               accum_out=cnt[:, k:k + 1])
                link(last)
            link(nc.vector.tensor_scalar(cnt, cnt, -1.0, 0.0, ALU.add, ALU.max))
            link(nc.vector.tensor_scalar(cnt, cnt, float(TR - 1), None, ALU.min))
            nc.vector.tensor_copy(idx, cnt).then_inc(s_idx, 1)
            dve.wait_ge(s_wts, 14 * 16)
            nc.vector.tensor_tensor(bias[:, 0:2], bias[:, 9:11], bias[:, 12:14], ALU.add)
            nc.vector.tensor_copy(bias[:, 2:3], bias[:, 14:15])
            link(nc.vector.tensor_copy(bias[:, 3:4], bias[:, 11:12]))
            nc.vector.tensor_copy(ident16[:, :], ident[:, :]).then_inc(s_id16, 1)
            for k in range(KW):
                dve.wait_ge(s_gath[k], 16)
            sr, ds = Gt[:, :, 0:SL], Gt[:, :, SL:2 * SL]
            link(nc.vector.tensor_scalar(tf, sr, -float((P - 1) // 2), 1.0 / P, ALU.add, ALU.mult))
            link(nc.vector.tensor_scalar(tf, tf, MAGIC, MAGIC, ALU.add, ALU.subtract))
            link(nc.vector.scalar_tensor_tensor(pf, tf, -float(P), sr, ALU.mult, ALU.add))
            for k in range(KW):
                last = nc.vector.tensor_scalar(kf[:, k, :], ds[:, k, :], wstart1[:, k:k + 1], None, ALU.subtract)
            link(last)
            link(nc.vector.scalar_tensor_tensor(tf, tf, float(W), kf, ALU.mult, ALU.add))
            link(nc.vector.scalar_tensor_tensor(tf, kf, 1.0, tf, ALU.is_ge, ALU.mult))
            nc.vector.scalar_tensor_tensor(kf, kf, float(W), tf, ALU.is_le, ALU.mult).then_inc(s_keys, 1)
            dve.wait_ge(s_ktr, 1)
            for c in range(2):
                for k in range(KW):
                    j = c * KW + k
                    for v, (dstv, base) in enumerate(((pT, 0), (kT, 3))):
                        last = nc.vector.tensor_copy(dstv[:, j, :],
                                                     PS[base + j // 3][0:P, (j % 3) * PW:(j % 3) * PW + PW])
            link(last)
            dve.wait_ge(s_iota, 2)
            with dve.Fori(0, PW // 4) as i:
                for g in range(NG):
                    dve.wait_ge(s_win, i * NG + (g + 1))
                    for h in range(4):
                        k, pr, c, w = g % 3, g // 3, h % 2, h // 2
                        col = i * 4 + (pr * 2 + w)
                        nc.vector.tensor_scalar(ohP[:, g * 4 + h, 0:P], iotaP[:, 0:P],
                                                pT[:, c * KW + k, bass.ds(col, 1)], None, ALU.is_equal)
                        last = nc.vector.tensor_scalar(ohK[:, g * 4 + h, 0:W * T], iotaK[:, 0:W * T],
                                                       kT[:, c * KW + k, bass.ds(col, 1)], None, ALU.is_equal)
                    last.then_inc(s_oh, 1)

            def decoded(c):
                t0, nt = CH[c]
                if c == 0:
                    dve.wait_ge(s_x2, 16)
                dve.wait_ge(s_d2, c + 1)
                y = yS[0:P, 0:nt * F].rearrange("p (t f) -> p t f", t=nt)
                nc.vector.tensor_tensor(y, PS[CB][0:P, 0:nt * F].rearrange("p (t f) -> p t f", t=nt),
                                        dec2b[0:P, :].unsqueeze(1).to_broadcast([P, nt, F]),
                                        ALU.add).then_inc(s_d2b, 1)
                dve.wait_ge(s_sg, c + 1)
                link(nc.vector.tensor_tensor(X32[0:P, t0:t0 + nt, :], X32[0:P, t0:t0 + nt, :], y, ALU.add))
                dve.sem_inc(s_x1, 1)
                norm_stats(t0, t0 + nt)

            def decoded_tail():
                decoded(NC - 1)
                dve.wait_ge(s_deg, T)
                link(nc.vector.tensor_reduce(chk[0:P, 0:1], deg[0:P, :], AX.X, ALU.add))
                nc.vector.tensor_scalar(deg[0:P, :], deg[0:P, :], 1.0, 1.0, ALU.add, ALU.max)
                nc.vector.tensor_scalar(mv[0:P, :, 1], mv[0:P, :, 1], 1e-5, None, ALU.add).then_inc(s_mv, 1)
                dve.wait_ge(s_rs, 3)
                nc.vector.tensor_scalar(dinvs[0:P, :], dinv[0:P, :], S0, None, ALU.mult)
                link(nc.vector.scalar_tensor_tensor(lnsc[0:P, :], dinv[0:P, :], S1, lnsc[0:P, :], ALU.mult, ALU.mult))
                nc.vector.scalar_tensor_tensor(lnb[0:P, :], mv[0:P, :, 0], -1.0, lnsc[0:P, :], ALU.mult, ALU.mult
                                               ).then_inc(s_lsc, 1)
                dve.wait_ge(s_S, L * NC)
                nc.vector.tensor_tensor(diagD, ident[0:P, 0:P].unsqueeze(1).to_broadcast([P, T, P]),
                                        dinv[0:P, :].unsqueeze(2).to_broadcast([P, T, P]),
                                        ALU.mult).then_inc(s_diagD, 1)
                for c, (t0, nt) in enumerate(CH):
                    dve.wait_ge(s_u, t0 + nt)
                    hi, lo = V16[0:P, t0:t0 + nt, 0, :], V16[0:P, t0:t0 + nt, 1, :]
                    link(nc.vector.tensor_copy(hi, U32[:, t0:t0 + nt, :]))
                    nc.vector.tensor_tensor(lo, U32[:, t0:t0 + nt, :], hi, ALU.subtract).then_inc(s_uhl, 1)
                dve.wait_ge(s_wts1, 48)
                dve.wait_ge(s_u, T)
                link(nc.vector.tensor_tensor(X32[0:P], X32[0:P], l1b2[0:P, :].unsqueeze(1).to_broadcast([P, T, F]),
                                             ALU.add))
                dve.wait_ge(s_dBs, NC)
                for c in range(NC + 2):
                    if c < NC:
                        n0, w = CH[c][0] * P, CH[c][1] * P
                        dve.wait_ge(s_1S, c + 1)
                        if c >= 1:
                            dve.wait_ge(s_1g, 2 * c)
                        nc.vector.scalar_tensor_tensor(aggS[:, 0:w], PS[AGG[c % 2]][:, 0:w], 1.0 / S1,
                                                       dinvB[:, n0:n0 + w], ALU.mult, ALU.mult).then_inc(s_1a, 1)
                    if c >= 2:
                        t0, nt = CH[c - 2]
                        dve.wait_ge(s_1hi, c - 1)
                        for j in range(nt):
                            last = nc.vector.scalar_tensor_tensor(
                                Z16[:, t0 + j, 1, :], PS[IB][0:P, j * F:j * F + F], dinvs[0:P, t0 + j:t0 + j + 1],
                                Z16[:, t0 + j, 0, :], ALU.mult, ALU.subtract)
                        last.then_inc(s_1lo, 1)
                link(nc.vector.tensor_reduce(chk[0:P, 2:3], Z16[:, :, 0, :], AX.XY, ALU.max, apply_absolute_value=True))
                nc.vector.tensor_scalar(chk[0:P, 2:3], chk[0:P, 2:3], LIMIT * S0, None, ALU.is_gt).then_inc(s_chk, 1)
                dve.wait_ge(s_chksum, 1)
                nc.vector.tensor_scalar(flag_f[:, 0:1], PS[RB][0:1, 0:1], float(E), None, ALU.not_equal)
                nc.vector.tensor_copy(flag_f[:, 1:2], PS[RB][0:1, 1:2])
                link(nc.vector.tensor_copy(flag_f[:, 2:3], PS[RB][0:1, 2:3]))
                link(nc.vector.tensor_reduce(flag_f[:, 3:4], flag_f[:, 0:3], AX.X, ALU.add))
                nc.vector.tensor_copy(flag[:, :], flag_f[:, 3:4]).then_inc(s_flag, 1)
                for c, (t0, nt) in enumerate(CH):
                    dve.wait_ge(s_2t, c + 1)
                    for j in range(nt):
                        last = nc.vector.scalar_tensor_tensor(
                            OUT[:, t0 + j, :], PS[TB][0:P, j * F:j * F + F], dinv[0:P, t0 + j:t0 + j + 1],
                            X32[0:P, t0 + j, :], ALU.mult, ALU.add)
                    last.then_inc(s_2o, 1)

            link(nc.vector.memset(chk[:, :], 0.0))
            dve.wait_ge(s_elo, NC)
            link(nc.vector.tensor_reduce(chk[:, 1:2], HT[:, :], AX.X, ALU.max, apply_absolute_value=True))
            link(nc.vector.tensor_scalar(chk[:, 1:2], chk[:, 1:2], LIMIT, None, ALU.is_gt))
            for l in range(L):
                for c in range(NC + 2):
                    q = l * NC + c
                    if c < NC:
                        for m in cgroups(q):
                            if m % 2 == 0:
                                evac_block_group(dve, m)
                    if 1 <= c <= NC:
                        n0, w = CH[c - 1][0] * P, CH[c - 1][1] * P
                        H = HT[:, n0:n0 + w]
                        dve.wait_ge(s_gN, q)
                        dve.wait_ge(s_r, q)
                        nc.vector.scalar_tensor_tensor(rS[:, 0:w], PS[NB][:, 0:w], bias[:, B_HN:B_HN + 1],
                                                       rS[:, 0:w], ALU.add, ALU.mult).then_inc(s_t1, 1)
                        dve.wait_ge(s_t1, q)
                        dve.wait_ge(s_gI, q)
                        nc.vector.tensor_tensor(rS[:, 0:w], PS[IB][:, 0:w], rS[:, 0:w], ALU.add).then_inc(s_t2, 1)
                    if c >= 2 and l < L - 1:
                        t0, nt = CH[c - 2]
                        dve.wait_ge(s_hi, q - 1)
                        nc.vector.scalar_tensor_tensor(
                            H16[0:P, (l + 1) % 2, t0:t0 + nt, 1, :],
                            PS[TB][0:P, 0:nt * F].rearrange("p (t f) -> p t f", t=nt), S0,
                            H16[0:P, (l + 1) % 2, t0:t0 + nt, 0, :], ALU.mult, ALU.subtract).then_inc(s_lo, 1)
                    if 1 <= c <= NC:
                        dve.wait_ge(s_n, q)
                        link(nc.vector.tensor_tensor(H, H, nS[:, 0:w], ALU.subtract))
                        link(nc.vector.tensor_tensor(H, H, zS[:, 0:w], ALU.mult))
                        last = nc.vector.tensor_tensor(H, H, nS[:, 0:w], ALU.add)
                        if l == L - 1:
                            link(last)
                            last = nc.vector.tensor_scalar(H, H, 0.0, None, ALU.max)
                        last.then_inc(s_h, 1)
                    if l == L - 1 and c >= 3:
                        decoded(c - 3)
            decoded_tail()
            dve.wait_ge(s_flag, 1)
            with dve.If(dve.value_load(flag[0:1, 0:1], min_val=0, max_val=1000) > 0):
                general_vector(dve)
        @block.tensor
        def _(pe):
            pe.sem_inc(s_win, NG)
            pe.wait_ge(s_ones, 1)
            pe.wait_ge(s_diag, 1)
            dg = diag.rearrange("p a b -> p (a b)")
            for q in range(5):
                nc.tensor.matmul(PS[q][0:P, 0:425], ones[0:P, 0:P], dg[:, 425 * q:425 * q + 425],
                                 start=True, stop=True).then_inc(s_bc, 1)
            pe.wait_ge(s_wts, 14 * 16)
            pe.wait_ge(s_bcused, 1)
            for s in range(NC + 3):
                if s < NC:
                    t0, nt = CH[s]
                    pe.wait_ge(s_xn, t0 + nt)
                    if s >= 1:
                        pe.wait_ge(s_eXs, s)
                    for j in range(nt):
                        last = nc.tensor.transpose(PS[5][:, j * P:(j + 1) * P], X32[0:P, t0 + j, :], ident[0:P, 0:P])
                    last.then_inc(s_eX, 1)
                if 1 <= s <= NC:
                    w = CH[s - 1][1] * P
                    pe.wait_ge(s_eXs, s)
                    if s >= 2:
                        pe.wait_ge(s_e1s, s - 1)
                    nc.tensor.matmul(PS[6][:, 0:w], enc1, aggS[:, 0:w], start=True, stop=True).then_inc(s_e1, 1)
                if 2 <= s <= NC + 1:
                    w = CH[s - 2][1] * P
                    pe.wait_ge(s_e1s, s - 1)
                    if s >= 3:
                        pe.wait_ge(s_eh, s - 2)
                    nc.tensor.matmul(PS[7][:, 0:w], enc2, rS[:, 0:w], start=True, stop=True).then_inc(s_e2, 1)
                if s >= 3:
                    t0, nt = CH[s - 3]
                    pe.wait_ge(s_eh, s - 2)
                    if s >= 4:
                        pe.wait_ge(s_eTs, s - 3)
                    for j in range(nt):
                        last = nc.tensor.transpose(PS[4][0:P, j * F:(j + 1) * F],
                                                   HT[:, (t0 + j) * P:(t0 + j + 1) * P], ident[:, :])
                    last.then_inc(s_eT, 1)
            for l in range(L):
                if l >= 1:
                    pe.wait_ge(s_cms, l)
                nc.tensor.matmul(PS[5][:, 0:G], convT[:, l, :], wih, start=True, stop=True).then_inc(s_cm, 1)
            pe.wait_ge(s_cms, L)
            pe.wait_ge(s_keys, 1)
            for c in range(2):
                for k in range(KW):
                    j = c * KW + k
                    for base, v in ((0, pf), (3, kf)):
                        last = nc.tensor.transpose(PS[base + j // 3][0:P, (j % 3) * PW:(j % 3) * PW + PW],
                                                   v[:, k, c * P:(c + 1) * P], ident[0:PW, 0:PW])
            last.then_inc(s_ktr, 1)
            with pe.Fori(0, PW // 4) as i:
                for g in range(NG):
                    pe.wait_ge(s_oh, i * NG + (g + 1))
                    pe.wait_ge(s_winfree, i * NG + (g + 1))
                    for h in range(4):
                        c, w = h % 2, h // 2
                        last = nc.tensor.matmul(PS[g][0:P, w * W * T:(w + 1) * W * T], ohP[:, g * 4 + h, 0:P],
                                                ohK[:, g * 4 + h, 0:W * T], start=(c == 0), stop=(c == 1))
                    last.then_inc(s_win, 1)

            def aggregate(bank, w, n0, adj, halves, c, groups=(), loops=False, ready=None):
                m = list(groups)
                for t in range(T):
                    if ready is not None and t % TC == 0:
                        pe.wait_ge(*ready(t // TC))
                    for h in range(2):
                        last = nc.tensor.matmul(PS[bank][:, 0:w], halves[0:P, t, h, :], adj[0:P, t, n0:n0 + w],
                                                start=(t == 0 and h == 0), stop=(t == T - 1 and h == 1 and not loops))
                    if m and t in SPOT:
                        block_group(m.pop(0))
                if loops:
                    t0, nt = CH[c]
                    for j in range(nt):
                        for h in range(2):
                            last = nc.tensor.matmul(PS[bank][:, j * P:(j + 1) * P], halves[0:P, t0 + j, h, :],
                                                    ident16[0:P, 0:P], start=False, stop=(j == nt - 1 and h == 1))
                return last

            def block_group(m):
                if m >= 1:
                    pe.wait_ge(s_cev[(m - 1) % 2], (m - 1) // 2 + 1)
                b0, nb = 4 * m, min(4, NBLK - 4 * m)
                for j in range(nb):
                    tr, tc = divmod(b0 + j, T)
                    last = nc.tensor.matmul(PS[CB][0:P, j * P:(j + 1) * P], AT3[0:P, tc, tr * P:(tr + 1) * P],
                                            ident16[0:P, 0:P], start=True, stop=True)
                last.then_inc(s_cfull, 1)

            def gates(l, q, c):
                n0, w = CH[c][0] * P, CH[c][1] * P
                H = HT[:, n0:n0 + w]
                cl = comb[:, l % 2, :]
                pe.wait_ge(s_r, q) if q else None
                nc.tensor.matmul(PS[RB][:, 0:w], whh[:, 0:F], H, start=True, stop=False)
                pe.wait_ge(s_z, q) if q else None
                nc.tensor.matmul(PS[ZB][:, 0:w], whh[:, F:2 * F], H, start=True, stop=False)
                pe.wait_ge(s_t1, q) if q else None
                nc.tensor.matmul(PS[NB][:, 0:w], whh[:, 2 * F:G], H, start=True, stop=True).then_inc(s_gN, 1)
                pe.wait_ge(s_agg, q + 1)
                if c == 0:
                    pe.wait_ge(s_comb[l % 2], 16 * (l // 2 + 1))
                nc.tensor.matmul(PS[RB][:, 0:w], cl[:, 0:F], aggS[:, 0:w], start=False, stop=True).then_inc(s_gR, 1)
                nc.tensor.matmul(PS[ZB][:, 0:w], cl[:, F:2 * F], aggS[:, 0:w], start=False, stop=True).then_inc(s_gZ, 1)
                pe.wait_ge(s_t2, q) if q else None
                nc.tensor.matmul(PS[IB][:, 0:w], cl[:, 2 * F:G], aggS[:, 0:w], start=True, stop=True).then_inc(s_gI, 1)

            def decode1(c):
                n0, w = CH[c][0] * P, CH[c][1] * P
                pe.wait_ge(s_h, (L - 1) * NC + c + 1)
                if c == 0:
                    pe.wait_ge(s_lo, (L - 1) * NC)
                else:
                    pe.wait_ge(s_d1s, c)
                nc.tensor.matmul(PS[TB][:, 0:w], dec1[:, :], HT[:, n0:n0 + w], start=True, stop=True).then_inc(s_d1, 1)

            def decode2(c):
                t0, nt = CH[c]
                pe.wait_ge(s_d1s, c + 1)
                if c == 0:
                    pe.wait_ge(s_cev[0], (NCG + 1) // 2)
                    pe.wait_ge(s_cev[1], NCG // 2)
                else:
                    pe.wait_ge(s_d2b, c)
                for j in range(nt):
                    last = nc.tensor.matmul(PS[CB][0:P, j * F:(j + 1) * F], HT[:, (t0 + j) * P:(t0 + j + 1) * P],
                                            dec2[:, :], start=True, stop=True)
                last.then_inc(s_d2, 1)

            pe.wait_ge(s_winfree, NG + PW // 4 * NG)
            pe.wait_ge(s_elo, NC)
            pe.wait_ge(s_id16, 1)
            for l in range(L):
                for c in range(NC + 2):
                    q = l * NC + c
                    if c < NC:
                        n0, w = CH[c][0] * P, CH[c][1] * P
                        if q >= 2:
                            pe.wait_ge(s_agg, q - 1)
                        ready = None
                        if c == 0 and l >= 1:
                            ready = lambda g: (s_lo, (l - 1) * NC + g + 1)
                        aggregate(AGG[q % 2], w, n0, AT3, H16[:, l % 2], c, cgroups(q), ready=ready).then_inc(s_S, 1)
                    if 1 <= c <= NC:
                        gates(l, q - 1, c - 1)
                    if c >= 2 and l < L - 1:
                        t0, nt = CH[c - 2]
                        pe.wait_ge(s_h, q - 1)
                        if q >= 3:
                            pe.wait_ge(s_lo, q - 2)
                        for j in range(nt):
                            last = nc.tensor.transpose(PS[TB][0:P, j * F:(j + 1) * F],
                                                       HT[:, (t0 + j) * P:(t0 + j + 1) * P], ident[:, :])
                        last.then_inc(s_tr, 1)
                    if l == L - 1:
                        if c >= 2:
                            decode1(c - 2)
                        if c >= 3:
                            decode2(c - 3)
            decode2(NC - 1)

            pe.wait_ge(s_onesL, 1)
            pe.wait_ge(s_diagD, 1)
            for c, (t0, nt) in enumerate(CH):
                if c >= 2:
                    pe.wait_ge(s_dBs, c - 1)
                nc.tensor.matmul(PS[RB + c % 2][:, 0:nt * P], onesL[0:P, :],
                                 diagD[:, t0:t0 + nt, :].rearrange("p a b -> p (a b)"),
                                 start=True, stop=True).then_inc(s_dB, 1)
            pe.wait_ge(s_wts1, 48)
            pe.wait_ge(s_dBs, NC)
            for c in range(NC + 2):
                if c < NC:
                    n0, w = CH[c][0] * P, CH[c][1] * P
                    if c >= 2:
                        pe.wait_ge(s_1a, c - 1)
                    aggregate(AGG[c % 2], w, n0, CT3, V16, c, loops=True,
                              ready=(lambda g: (s_uhl, g + 1)) if c == 0 else None).then_inc(s_1S, 1)
                if 1 <= c <= NC:
                    w = CH[c - 1][1] * P
                    pe.wait_ge(s_1a, c)
                    if c >= 2:
                        pe.wait_ge(s_1h, 2 * (c - 1))
                    for k in range(HID // F):
                        nc.tensor.matmul(PS[RB + k][:, 0:w], w1[:, k * F:(k + 1) * F], aggS[:, 0:w],
                                         start=True, stop=True).then_inc(s_1g, 1)
                if c >= 2:
                    nt = CH[c - 2][1]
                    pe.wait_ge(s_1h, 2 * (c - 1))
                    if c >= 3:
                        pe.wait_ge(s_1lo, c - 2)
                    for j in range(nt):
                        for k in range(HID // F):
                            last = nc.tensor.matmul(PS[IB][0:P, j * F:(j + 1) * F],
                                                    (rS, zS)[k][:, j * P:(j + 1) * P], w2[:, k, :],
                                                    start=(k == 0), stop=(k == 1))
                    last.then_inc(s_1p, 1)
            for c in range(NC + 1):
                if c == 2:
                    pe.wait_ge(s_chk, 1)
                    nc.tensor.matmul(PS[RB][0:1, 0:3], onesL[:, 0:1], chk[:, 0:3], start=True, stop=True
                                     ).then_inc(s_chksum, 1)
                if c < NC:
                    n0, w = CH[c][0] * P, CH[c][1] * P
                    if c >= 2:
                        pe.wait_ge(s_2a, c - 1)
                    aggregate(AGG[c % 2], w, n0, CT3, Z16, c, loops=True,
                              ready=(lambda g: (s_1lo, g + 1)) if c == 0 else None).then_inc(s_2S, 1)
                if c >= 1:
                    nt = CH[c - 1][1]
                    pe.wait_ge(s_2a, c)
                    if c >= 2:
                        pe.wait_ge(s_2o, c - 1)
                    for j in range(nt):
                        last = nc.tensor.transpose(PS[TB][0:P, j * F:(j + 1) * F], aggS[:, j * P:(j + 1) * P],
                                                   ident[:, :])
                    last.then_inc(s_2t, 1)
            pe.wait_ge(s_flag, 1)
            with pe.If(pe.value_load(flag[0:1, 0:1], min_val=0, max_val=1000) > 0):
                general_tensor(pe)

        @block.scalar
        def _(act):
            def decode_sig(c):
                nt = CH[c][1]
                act.wait_ge(s_d2b, c + 1)
                nc.scalar.activation(yS[0:P, 0:nt * F], yS[0:P, 0:nt * F], ACT.Sigmoid).then_inc(s_sg, 1)

            ndeg = [0]

            def degree(t):
                if ndeg[0] == 0:
                    act.wait_ge(s_combst, 16)
                else:
                    act.wait_ge(s_deg, ndeg[0])
                ndeg[0] += 1
                nc.scalar.activation(CT3[0:P, T - 1, :], AT3[0:P, t, 0:N], ACT.Copy, saturate=False,
                                     accum_out=deg[0:P, t:t + 1]).then_inc(s_deg, 1)

            act.wait_ge(s_ln, 1)
            for t in range(T):
                nc.scalar.activation(X32[0:P, t, :], X32[0:P, t, :], ACT.Relu, bias=lnb[0:P, t:t + 1],
                                     scale=lnsc[0:P, t:t + 1]).then_inc(s_xn, 1)
            act.wait_ge(s_wts, 14 * 16)
            for s in range(NC + 3):
                if s < NC:
                    w = CH[s][1] * P
                    act.wait_ge(s_eX, s + 1)
                    if s >= 1:
                        act.wait_ge(s_e1, s)
                    nc.scalar.activation(aggS[:, 0:w], PS[5][:, 0:w], ACT.Copy).then_inc(s_eXs, 1)
                if 1 <= s <= NC:
                    w = CH[s - 1][1] * P
                    act.wait_ge(s_e1, s)
                    if s >= 2:
                        act.wait_ge(s_e2, s - 1)
                    nc.scalar.activation(rS[:, 0:w], PS[6][:, 0:w], ACT.Relu, bias=bias[:, B_E1:B_E1 + 1]
                                         ).then_inc(s_e1s, 1)
                if 2 <= s <= NC + 1:
                    n0, w = CH[s - 2][0] * P, CH[s - 2][1] * P
                    act.wait_ge(s_e2, s - 1)
                    nc.scalar.activation(HT[:, n0:n0 + w], PS[7][:, 0:w], ACT.Identity, bias=bias[:, B_E2:B_E2 + 1]
                                         ).then_inc(s_eh, 1)
                if s >= 3:
                    t0, nt = CH[s - 3]
                    act.wait_ge(s_eT, s - 2)
                    if s >= 4:
                        act.wait_ge(s_elo, s - 3)
                    nc.scalar.activation(yS[0:P, 0:nt * F], PS[4][0:P, 0:nt * F], ACT.Copy, scale=S0).then_inc(s_eTs, 1)
                    act.wait_ge(s_eTs, s - 2)
                    nc.scalar.activation(H16[0:P, 0, t0:t0 + nt, 0, :],
                                         yS[0:P, 0:nt * F].rearrange("p (t f) -> p t f", t=nt),
                                         ACT.Copy).then_inc(s_ehi, 1)
            for l in range(L):
                act.wait_ge(s_cm, l + 1)
                nc.scalar.activation(combS[:, l, :], PS[5][:, 0:G], ACT.Copy).then_inc(s_cms, 1)
            act.sem_inc(s_winfree, NG)
            for n in range(PW // 4 * NG):
                i, g = n // NG, n % NG
                act.wait_ge(s_win, NG + n + 1)
                d0 = (g % 3) * PW * W + (4 * i + 2 * (g // 3)) * W
                nc.scalar.activation(
                    AT3[0:P, :, d0:d0 + 2 * W].rearrange("p t (w d) -> p w t d", w=2),
                    PS[g][0:P, 0:2 * W * T].rearrange("p (w t d) -> p w t d", w=2, t=T),
                    ACT.Copy, saturate=False).then_inc(s_winfree, 1)
            for l in range(L):
                for c in range(NC + 2):
                    q = l * NC + c
                    if c < NC:
                        for m in cgroups(q):
                            if m % 2 == 1:
                                evac_block_group(act, m)
                        w = CH[c][1] * P
                        for t in (q, q + 3 * NC):
                            if t < T and q < 3 * NC:
                                degree(t)
                        act.wait_ge(s_S, q + 1)
                        if q >= 1:
                            act.wait_ge(s_gI, q)
                        nc.scalar.activation(aggS[:, 0:w], PS[AGG[q % 2]][:, 0:w], ACT.Copy, scale=1.0 / S0
                                             ).then_inc(s_agg, 1)
                    if 1 <= c <= NC:
                        w = CH[c - 1][1] * P
                        act.wait_ge(s_gR, q)
                        if q >= 2:
                            act.wait_ge(s_n, q - 1)
                        nc.scalar.activation(rS[:, 0:w], PS[RB][:, 0:w], ACT.Sigmoid, bias=bias[:, B_R:B_R + 1]
                                             ).then_inc(s_r, 1)
                        act.wait_ge(s_gZ, q)
                        if q >= 2:
                            act.wait_ge(s_h, q - 1)
                        nc.scalar.activation(zS[:, 0:w], PS[ZB][:, 0:w], ACT.Sigmoid, bias=bias[:, B_Z:B_Z + 1]
                                             ).then_inc(s_z, 1)
                    if c >= 2 and l < L - 1:
                        t0, nt = CH[c - 2]
                        act.wait_ge(s_tr, q - 1)
                        nc.scalar.activation(H16[0:P, (l + 1) % 2, t0:t0 + nt, 0, :],
                                             PS[TB][0:P, 0:nt * F].rearrange("p (t f) -> p t f", t=nt),
                                             ACT.Copy, scale=S0).then_inc(s_hi, 1)
                    if 1 <= c <= NC:
                        act.wait_ge(s_t2, q)
                        nc.scalar.activation(nS[:, 0:w], rS[:, 0:w], ACT.Tanh, bias=bias[:, B_IN:B_IN + 1]
                                             ).then_inc(s_n, 1)
                    if l == L - 1 and c >= 2:
                        n0, w = CH[c - 2][0] * P, CH[c - 2][1] * P
                        act.wait_ge(s_d1, c - 1)
                        nc.scalar.activation(HT[:, n0:n0 + w], PS[TB][:, 0:w], ACT.Relu, bias=bias[:, B_D1:B_D1 + 1]
                                             ).then_inc(s_d1s, 1)
                    if l == L - 1 and c >= 3:
                        decode_sig(c - 3)
            decode_sig(NC - 1)
            act.wait_ge(s_lsc, 1)
            for t in range(T):
                nc.scalar.activation(U32[:, t, :], X32[0:P, t, :], ACT.Relu, bias=lnb[0:P, t:t + 1],
                                     scale=lnsc[0:P, t:t + 1]).then_inc(s_u, 1)
            for c, (t0, nt) in enumerate(CH):
                act.wait_ge(s_dB, c + 1)
                nc.scalar.activation(dinvB[:, t0 * P:(t0 + nt) * P], PS[RB + c % 2][:, 0:nt * P], ACT.Copy
                                     ).then_inc(s_dBs, 1)
            for c in range(1, NC + 2):
                if c <= NC:
                    w = CH[c - 1][1] * P
                    for k in range(HID // F):
                        act.wait_ge(s_1g, 2 * (c - 1) + k + 1)
                        if c >= 2:
                            act.wait_ge(s_1p, c - 1)
                        nc.scalar.activation((rS, zS)[k][:, 0:w], PS[RB + k][:, 0:w], ACT.Relu,
                                             bias=bias[:, B_L1 + k:B_L1 + k + 1]).then_inc(s_1h, 1)
                if c >= 1 and c <= NC:
                    t0, nt = CH[c - 1]
                    act.wait_ge(s_1p, c)
                    for j in range(nt):
                        last = nc.scalar.activation(Z16[:, t0 + j, 0, :], PS[IB][0:P, j * F:j * F + F], ACT.Copy,
                                                    scale=dinvs[0:P, t0 + j:t0 + j + 1])
                    last.then_inc(s_1hi, 1)
            for c in range(NC):
                w = CH[c][1] * P
                act.wait_ge(s_2S, c + 1)
                if c >= 1:
                    act.wait_ge(s_2t, c)
                nc.scalar.activation(aggS[:, 0:w], PS[AGG[c % 2]][:, 0:w], ACT.Copy, scale=1.0 / S0
                                     ).then_inc(s_2a, 1)
            act.wait_ge(s_flag, 1)
            with act.If(act.value_load(flag[0:1, 0:1], min_val=0, max_val=1000) > 0):
                general_scalar(act)


_IN = ['x', 'src', 'dst', 'enc_w1T', 'enc_b1', 'enc_w2T', 'enc_b2', 'conv_wT', 'gru_wihT', 'gru_whhT',
       'gru_bih', 'gru_bhh', 'dec_w1T', 'dec_b1', 'dec_w2T', 'dec_b2', 'l1_w1T', 'l1_b1', 'l1_w2T', 'l1_b2']


def layout(inputs):
    import numpy as np
    a = {k: np.asarray(v) for k, v in inputs.items()}
    g = lambda n: a['L0_gnn_' + n]
    f = lambda n: a['L1_gnn_' + n]
    c = np.ascontiguousarray
    H = g('gru_whh').shape[1]
    return {
        'x': c(a['x']), 'src': c(a['src']), 'dst': c(a['dst']),
        'enc_w1T': c(g('enc_w1').T), 'enc_b1': c(g('enc_b1').reshape(-1, 1)),
        'enc_w2T': c(g('enc_w2').T), 'enc_b2': c(g('enc_b2').reshape(-1, 1)),
        'conv_wT': c(g('conv_w').transpose(0, 2, 1)),
        'gru_wihT': c(g('gru_wih').T), 'gru_whhT': c(g('gru_whh').T),
        'gru_bih': c(g('gru_bih').reshape(3, H).T), 'gru_bhh': c(g('gru_bhh').reshape(3, H).T),
        'dec_w1T': c(g('dec_w1').T), 'dec_b1': c(g('dec_b1').reshape(-1, 1)),
        'dec_w2T': c(g('dec_w2').T), 'dec_b2': c(g('dec_b2').reshape(1, -1)),
        'l1_w1T': c(f('W1').T), 'l1_b1': c(f('b1').reshape(2, -1).T),
        'l1_w2T': c(f('W2').T.reshape(2, H, -1).transpose(1, 0, 2)), 'l1_b2': c(f('b2').reshape(1, -1)),
    }


def kernel(**inputs):
    import numpy as np
    import concourse.bacc as bacc
    from concourse.bass_utils import run_bass_kernel_spmd

    nc = bacc.Bacc("TRN2", target_bir_lowering=False, num_devices=1)
    arrays = layout(inputs)
    args = [nc.dram_tensor(f"in_{n}", arrays[n].shape, mybir.dt.from_np(arrays[n].dtype),
                           kind="ExternalInput").ap() for n in _IN]
    out = nc.dram_tensor("out", inputs['x'].shape, mybir.dt.float32, kind="ExternalOutput").ap()
    gnn_kernel(nc, *args, out)
    r = run_bass_kernel_spmd(nc, [{f"in_{n}": arrays[n] for n in _IN}], core_ids=[0])
    return np.asarray(r.results[0]["out"])
```

```python
import concourse.bass as bass
from concourse import mybir
from contextlib import ExitStack


def gnn_kernel(nc, x, src, dst, enc_w1T, enc_b1, enc_w2T, enc_b2, conv_wT, gru_wihT, gru_whhT,
               gru_bih, gru_bhh, dec_w1T, dec_b1, dec_w2T, dec_b2, l1_w1T, l1_b1, l1_w2T, l1_b2, out):
    F32, F16, BF16, I32 = mybir.dt.float32, mybir.dt.float16, mybir.dt.bfloat16, mybir.dt.int32
    FP8 = mybir.dt.float8e3
    ALU, ACT, AX = mybir.AluOpType, mybir.ActivationFunctionType, mybir.AxisListType

    N, F = x.shape
    E = src.shape[0]
    L = conv_wT.shape[0]
    G = 3 * F
    HID = l1_w1T.shape[1]
    P = 125
    T = N // P
    assert T * P == N
    W = 9
    KW = 3
    PW = 116
    assert KW * PW * W >= N
    DP = KW * PW * W
    RL = 25
    NR = E // RL
    assert NR * RL == E
    SL = 2 * P
    TR = NR - SL // RL + 1
    NS = NR // P
    assert NS * P == NR
    LIMIT = 1000.0
    MAGIC = 12582912.0
    TC = 4
    CH = [(t, min(TC, T - t)) for t in range(0, T, TC)]
    NC = len(CH)
    S0 = 64.0
    S1 = 1024.0

    src_t, dst_t = src.tensor, dst.tensor
    table = nc.dram_tensor("edge_table", (TR, 2 * SL), I32, kind="Internal").ap()
    comb_dram = nc.dram_tensor("comb_scratch", (L, F, G), F32, kind="Internal").ap()

    ctx = ExitStack()
    with ctx:
        def sb(name, shape, dt):
            return ctx.enter_context(nc.sbuf_tensor(name, shape, dt))

        def sem(name):
            return ctx.enter_context(nc.semaphore(name))

        def carve(region, at, shape, dt):
            size = {F32: 4, I32: 4, F16: 2, BF16: 2}[dt]
            n = size
            for s in shape[1:]:
                n *= s
            v = region[0:shape[0], at:at + n].bitcast(dt)
            if len(shape) == 3:
                v = v.rearrange("p (a b) -> p a b", a=shape[1])
            if len(shape) == 4:
                v = v.rearrange("p (a b c) -> p a b c", a=shape[1], b=shape[2])
            return v

        AT = sb("AT", [128, T * DP], FP8)
        CT = sb("CT", [128, T * N + 3], FP8)
        HT = sb("HT", [128, N], F32)
        H16 = sb("H16", [128, 2, T, 2, F], F16)
        AT3 = AT[:, :].rearrange("p (t d) -> p t d", t=T)
        CT3 = CT[:, 0:T * N].rearrange("p (t s) -> p t s", t=T)
        ident = sb("ident", [128, 128], F32)
        ident16 = sb("ident16", [128, 128], F16)
        comb = sb("comb", [128, 2, G], F32)
        whh = sb("whh", [128, G], F32)
        aggS = sb("aggS", [128, TC * P], F32)
        rS = sb("rS", [128, TC * P], F32)
        zS = sb("zS", [128, TC * P], F32)
        nS = sb("nS", [128, TC * P], F32)
        bias = sb("bias", [128, 16], F32)
        dec1 = sb("dec1", [128, F], F32)
        dec2 = sb("dec2", [128, F], F32)
        dec2b = sb("dec2b", [128, F], F32)
        yS = sb("yS", [128, TC * F], F32)
        deg = sb("deg", [128, T], F32)
        dinv = sb("dinv", [128, T], F32)
        dinvs = sb("dinvs", [128, T], F32)
        stat = sb("stat", [128, TC, 6], F32)
        mv = sb("mv", [128, T, 2], F32)
        lnsc = sb("lnsc", [128, T], F32)
        chk = sb("chk", [128, 4], F32)
        flag_f = sb("flag_f", [1, 4], F32)
        flag = sb("flag", [1, 1], I32)
        mhalf = sb("mhalf", [128, T], F32)
        lnb = sb("lnb", [128, T], F32)
        X32 = H16[:, 1, :, :, :].rearrange("p t h f -> p (t h f)").bitcast(F32).rearrange("p (t f) -> p t f", t=T)
        (B_R, B_Z, B_HN, B_IN, B_E1, B_E2, B_D1, B_L1) = range(8)

        PS = [ctx.enter_context(nc.psum_tensor(f"PS{i}", [128, 512], F32)) for i in range(8)]

        o = [0]

        def early(shape, dt):
            size = {F32: 4, I32: 4, F16: 2, BF16: 2}[dt]
            n = size
            for s in shape[1:]:
                n *= s
            v = carve(CT, o[0], shape, dt)
            o[0] += (n + 31) // 32 * 32
            return v

        ones = early([128, 128], F32)
        samp_i = early([P, NS, RL], I32)
        samp = early([P, NS], F32)
        diag = early([P, NS, P], F32)
        junk = early([P, NS * P], F32)
        wstart = early([PW, KW], F32)
        wstart1 = early([PW, KW], F32)
        cnt = early([PW, KW], F32)
        idx = early([PW, KW], I32)
        Gt = early([PW, KW, 2 * SL], I32)
        tf = early([PW, KW, SL], F32)
        pf = early([PW, KW, SL], F32)
        kf = early([PW, KW, SL], F32)
        pT = early([P, KW, PW * 2], BF16)
        kT = early([P, KW, PW * 2], BF16)
        WB = 4
        J = 2 * WB
        assert PW % WB == 0 and WB % 2 == 0
        iotaP = early([P, P, J], BF16)
        iotaK = early([P, W * T, J], BF16)
        NG = KW * WB // 2
        ohP = early([P, KW, P * J], BF16).rearrange("p k (n j) -> p k n j", j=J)
        ohK = early([P, KW, W * T * J], BF16).rearrange("p k (n j) -> p k n j", j=J)
        enc1 = early([128, F], F32)
        enc2 = early([128, F], F32)
        convT = early([128, L, F], F32)
        wih = early([128, G], F32)
        combS = early([128, L, G], F32)
        assert o[0] <= T * N, o[0]

        p2 = [0]

        def late(shape, dt):
            size = {F32: 4, I32: 4, F16: 2, BF16: 2}[dt]
            n = size
            for d in shape[1:]:
                n *= d
            v = carve(AT, p2[0], shape, dt)
            p2[0] += (n + 31) // 32 * 32
            return v

        w1 = late([128, HID], F32)
        w2 = late([128, HID // F, F], F32)
        l1b2 = late([128, F], F32)
        onesL = late([128, 128], F32)
        dinvB = late([128, N], F32)
        diagD = late([P, T, P], F32)
        U32 = late([P, T, F], F32)
        OUT = late([P, T, F], F32)
        V16 = H16[:, 0, :, :, :]
        Z16 = late([P, T, 2 * F], F16).rearrange("p t (h f) -> p t h f", h=2)
        assert p2[0] <= T * DP

        gp = [0, 0]

        def spare(r, shape, dt):
            n = 2 if dt == F16 else 4
            for d in shape[1:]:
                n *= d
            v = carve((AT, CT)[r], gp[r], shape, dt)
            gp[r] += (n + 31) // 32 * 32
            return v

        gH, gA, gB, gD, gH1, gH2 = [spare(0, [128, N], F32) for _ in range(6)]
        gX, gU = [spare(1, [P, T, F], F32) for _ in range(2)]
        EC = E // T
        ebuf = spare(1, [1, 2, EC], I32)
        genc1, genc2 = [spare(1, [128, F], F32) for _ in range(2)]
        gcw = spare(1, [128, G], F32)
        gw1 = spare(1, [128, HID], F32)
        gw2 = spare(1, [128, HID // F, F], F32)
        gb2 = spare(1, [128, 1], F32)
        assert gp[0] <= T * DP and gp[1] <= T * N

        AGG, RB, ZB, NB, IB, TB, CB = (0, 1), 2, 3, 4, 5, 6, 7
        NBLK = T * T
        NCG = (NBLK + 3) // 4
        CPS = 7
        SPOT = [10, 12, 14, 16, 18, 20, 23]
        CHOST = [q for q in range(L * NC) if (q == 0 or q % NC) and q % NC < NC - 1]
        cgroups = lambda q: ([m for m in range(CPS * CHOST.index(q), CPS * CHOST.index(q) + CPS) if m < NCG]
                             if q in CHOST else [])

        s_tab = sem("s_tab"); s_samp = sem("s_samp"); s_idxl = sem("s_idxl")
        s_id = sem("s_id"); s_ones = sem("s_ones"); s_ws = sem("s_ws"); s_iota = sem("s_iota")
        s_diag = sem("s_diag"); s_bc = sem("s_bc"); s_idx = sem("s_idx")
        s_gath = [sem(f"s_gath{k}") for k in range(KW)]
        s_keys = sem("s_keys"); s_ktr = sem("s_ktr"); s_kt = sem("s_kt")
        s_oh = sem("s_oh"); s_win = sem("s_win"); s_winfree = sem("s_winfree")
        s_wts = sem("s_wts"); s_mhalf = sem("s_mhalf"); s_mv = sem("s_mv"); s_rs = sem("s_rs"); s_deg = sem("s_deg"); s_x = sem("s_x"); s_x2 = sem("s_x2"); s_wts1 = sem("s_wts1")
        s_ln = sem("s_ln"); s_xn = sem("s_xn"); s_eX = sem("s_eX"); s_eXs = sem("s_eXs"); s_e1 = sem("s_e1")
        s_e1s = sem("s_e1s"); s_e2 = sem("s_e2"); s_eh = sem("s_eh"); s_eT = sem("s_eT"); s_eTs = sem("s_eTs")
        s_ehi = sem("s_ehi"); s_elo = sem("s_elo"); s_bcused = sem("s_bcused"); s_bias = sem("s_bias")
        s_id16 = sem("s_id16"); s_cm = sem("s_cm"); s_cms = sem("s_cms"); s_combst = sem("s_combst")
        s_comb = [sem("s_comb0"), sem("s_comb1")]
        s_S = sem("s_S"); s_agg = sem("s_agg"); s_gN = sem("s_gN"); s_gR = sem("s_gR"); s_gZ = sem("s_gZ")
        s_gI = sem("s_gI"); s_r = sem("s_r"); s_z = sem("s_z"); s_n = sem("s_n"); s_t1 = sem("s_t1"); s_t2 = sem("s_t2")
        s_h = sem("s_h"); s_tr = sem("s_tr"); s_hi = sem("s_hi"); s_lo = sem("s_lo"); s_cfull = sem("s_cfull")
        s_cev = [sem("s_cevd"), sem("s_ceva")]
        s_d1 = sem("s_d1"); s_d1s = sem("s_d1s"); s_d2 = sem("s_d2"); s_d2b = sem("s_d2b"); s_sg = sem("s_sg")
        s_x1 = sem("s_x1"); s_lsc = sem("s_lsc"); s_diagD = sem("s_diagD"); s_dB = sem("s_dB"); s_dBs = sem("s_dBs")
        s_u = sem("s_u"); s_uhl = sem("s_uhl"); s_1S = sem("s_1S"); s_1a = sem("s_1a"); s_1g = sem("s_1g")
        s_1h = sem("s_1h"); s_1p = sem("s_1p"); s_1hi = sem("s_1hi"); s_1lo = sem("s_1lo")
        s_2S = sem("s_2S"); s_2a = sem("s_2a"); s_2t = sem("s_2t"); s_2o = sem("s_2o"); s_onesL = sem("s_onesL"); s_uh = sem("s_uh")
        s_chk = sem("s_chk"); s_chksum = sem("s_chksum"); s_flag = sem("s_flag")
        g_x = sem("g_x"); g_w = sem("g_w"); g_mv = sem("g_mv"); g_rs = sem("g_rs"); g_ln = sem("g_ln")
        g_un = sem("g_un"); g_ut = sem("g_ut"); g_utc = sem("g_utc"); g_e1 = sem("g_e1"); g_e1s = sem("g_e1s")
        g_e2 = sem("g_e2"); g_h0 = sem("g_h0"); g_cw = sem("g_cw"); g_agg = sem("g_agg"); g_gt = sem("g_gt")
        g_rz = sem("g_rz"); g_t2 = sem("g_t2"); g_tn = sem("g_tn"); g_hn = sem("g_hn"); g_rh = sem("g_rh")
        g_d1 = sem("g_d1"); g_d1s = sem("g_d1s"); g_d2 = sem("g_d2"); g_d2b = sem("g_d2b"); g_sg = sem("g_sg")
        g_x1 = sem("g_x1"); g_deg = sem("g_deg"); g_dinv = sem("g_dinv"); g_a1 = sem("g_a1"); g_w1 = sem("g_w1")
        g_w1s = sem("g_w1s"); g_w2 = sem("g_w2"); g_w2s = sem("g_w2s"); g_a2 = sem("g_a2"); g_ot = sem("g_ot")
        g_o = sem("g_o"); g_out = sem("g_out"); g_eb = sem("g_eb"); g_ebfree = sem("g_ebfree"); g_edge = sem("g_edge"); g_tick = sem("g_tick")
        g_chain = sem("g_chain")
        s_chain = sem("s_chain"); s_out = sem("s_out"); s_built = sem("s_built")

        block = ctx.enter_context(nc.Block())

        def evac_block_group(eng, m):
            b0, nb = 4 * m, min(4, NBLK - 4 * m)
            eng.wait_ge(s_cfull, m + 1)
            if 4 * m + nb > T * (T - 1):
                eng.wait_ge(s_deg, T)
            if m < 2:
                eng.wait_ge(s_combst, 16)
            o_, i_ = CT[0:P, b0 * P:(b0 + nb) * P], PS[CB][0:P, 0:nb * P]
            if m % 2 == 0:
                nc.vector.tensor_copy(o_, i_, saturate=False).then_inc(s_cev[0], 1)
            else:
                nc.scalar.activation(o_, i_, ACT.Copy, saturate=False).then_inc(s_cev[1], 1)

        def general_vector(dve):
            n = [0]

            def link(ins):
                n[0] += 1
                ins.then_inc(g_chain, 1)
                dve.wait_ge(g_chain, n[0])

            def norm(k):
                for t in range(T):
                    link(nc.vector.bn_stats(stat[0:P, 0, :], gX[:, t, :]))
                    link(nc.vector.bn_aggr(mv[0:P, t, :], stat[0:P, 0, :]))
                nc.vector.tensor_scalar(mv[0:P, :, 1], mv[0:P, :, 1], 1e-5, None, ALU.add).then_inc(g_mv, 1)
                dve.wait_ge(g_rs, k + 1)
                nc.vector.scalar_tensor_tensor(lnb[0:P, :], mv[0:P, :, 0], -1.0, lnsc[0:P, :], ALU.mult, ALU.mult
                                               ).then_inc(g_ln, 1)

            def edges(first, to, frm, fi, ti):
                with dve.Fori(0, T) as k:
                    dve.wait_ge(g_eb, (first + k + 1) * 32)
                    dve.sem_inc(g_tick, 1)
                    with dve.Fori(0, EC) as i:
                        a = dve.value_load(ebuf[0:1, ti, bass.ds(i, 1)], min_val=0, max_val=N - 1)
                        if frm is None:
                            ins = nc.vector.tensor_scalar(to[:, bass.ds(a, 1)], to[:, bass.ds(a, 1)], 1.0, None, ALU.add)
                        else:
                            b = dve.value_load(ebuf[0:1, fi, bass.ds(i, 1)], min_val=0, max_val=N - 1)
                            ins = nc.vector.tensor_tensor(to[:, bass.ds(a, 1)], to[:, bass.ds(a, 1)],
                                                          frm[:, bass.ds(b, 1)], ALU.add)
                        ins.then_inc(g_edge, 1)
                        dve.wait_ge(g_edge, i + 1)
                    dve.sem_clear(g_edge)
                    dve.sem_inc(g_ebfree, 1)

            dve.sem_inc(g_ebfree, 1)
            dve.wait_ge(g_x, 16)
            norm(0)
            dve.wait_ge(g_h0, NC)
            with dve.Fori(0, L) as l:
                nc.vector.memset(gA, 0.0).then_inc(g_agg, 1)
                dve.wait_ge(g_agg, l * 2 + 1)
                dve.sem_inc(g_tick, 1)
                edges(l * T, gA, gH, 0, 1)
                dve.sem_inc(g_agg, 1)
                for c, (t0, nt) in enumerate(CH):
                    w = nt * P
                    H = gH[:, t0 * P:t0 * P + w]
                    dve.wait_ge(g_rz, l * NC + (c + 1))
                    nc.vector.scalar_tensor_tensor(rS[:, 0:w], PS[NB][:, 0:w], bias[:, B_HN:B_HN + 1], rS[:, 0:w],
                                                   ALU.add, ALU.mult).then_inc(g_t2, 1)
                    dve.wait_ge(g_t2, l * (2 * NC) + (2 * c + 1))
                    nc.vector.tensor_tensor(rS[:, 0:w], PS[IB][:, 0:w], rS[:, 0:w], ALU.add).then_inc(g_t2, 1)
                    dve.wait_ge(g_tn, l * (3 * NC) + (3 * c + 1))
                    nc.vector.tensor_tensor(H, H, nS[:, 0:w], ALU.subtract).then_inc(g_tn, 1)
                    dve.wait_ge(g_tn, l * (3 * NC) + (3 * c + 2))
                    nc.vector.tensor_tensor(H, H, zS[:, 0:w], ALU.mult).then_inc(g_tn, 1)
                    dve.wait_ge(g_tn, l * (3 * NC) + (3 * c + 3))
                    nc.vector.tensor_tensor(H, H, nS[:, 0:w], ALU.add).then_inc(g_hn, 1)
            dve.wait_ge(g_hn, L * NC)
            nc.vector.tensor_scalar(gH, gH, 0.0, None, ALU.max).then_inc(g_rh, 1)
            for c, (t0, nt) in enumerate(CH):
                y = yS[0:P, 0:nt * F].rearrange("p (t f) -> p t f", t=nt)
                dve.wait_ge(g_d2, c + 1)
                nc.vector.tensor_tensor(y, PS[CB][0:P, 0:nt * F].rearrange("p (t f) -> p t f", t=nt),
                                        dec2b[0:P, :].unsqueeze(1).to_broadcast([P, nt, F]), ALU.add).then_inc(g_d2b, 1)
                dve.wait_ge(g_sg, c + 1)
                nc.vector.tensor_tensor(gX[:, t0:t0 + nt, :], gX[:, t0:t0 + nt, :], y, ALU.add).then_inc(g_x1, 1)
                dve.wait_ge(g_x1, c + 1)
            norm(1)
            link(nc.vector.memset(gD, 1.0))
            edges(L * T, gD, None, 0, 0)
            dve.sem_inc(g_deg, 1)
            dve.wait_ge(g_utc, 2 * NC)
            dve.wait_ge(g_dinv, 1)
            link(nc.vector.tensor_tensor(gB, gB, gD, ALU.mult))
            link(nc.vector.tensor_copy(gA, gB))
            edges((L + 1) * T, gA, gB, 1, 0)
            nc.vector.tensor_tensor(gA, gA, gD, ALU.mult).then_inc(g_a1, 1)
            for c, (t0, nt) in enumerate(CH):
                cs = slice(t0 * P, (t0 + nt) * P)
                dve.wait_ge(g_w2, c + 1)
                nc.vector.tensor_tensor(gB[:, cs], PS[NB][:, 0:nt * P], gD[:, cs], ALU.mult).then_inc(g_w2s, 1)
            dve.wait_ge(g_w2s, NC)
            link(nc.vector.tensor_copy(gA, gB))
            edges((L + 2) * T, gA, gB, 1, 0)
            dve.wait_ge(g_w, 16 * 5)
            link(nc.vector.tensor_tensor(gA, gA, gD, ALU.mult))
            nc.vector.tensor_scalar(gA, gA, gb2[:, 0:1], None, ALU.add).then_inc(g_a2, 1)
            for c, (t0, nt) in enumerate(CH):
                dve.wait_ge(g_ot, c + 1)
                nc.vector.tensor_tensor(gX[:, t0:t0 + nt, :], gX[:, t0:t0 + nt, :],
                                        PS[TB][0:P, 0:nt * F].rearrange("p (t f) -> p t f", t=nt), ALU.add
                                        ).then_inc(g_o, 1)

        def general_tensor(pe):
            def to_features(k):
                for c, (t0, nt) in enumerate(CH):
                    pe.wait_ge(g_un, k * T + t0 + nt)
                    if k * NC + c >= 1:
                        pe.wait_ge(g_utc, k * NC + c)
                    for j in range(nt):
                        last = nc.tensor.transpose(PS[TB][:, j * P:(j + 1) * P], gU[:, t0 + j, :], ident[0:P, 0:P])
                    last.then_inc(g_ut, 1)

            to_features(0)
            pe.wait_ge(g_w, 16 * 5)
            for c, (t0, nt) in enumerate(CH):
                cs = slice(t0 * P, (t0 + nt) * P)
                pe.wait_ge(g_utc, c + 1)
                nc.tensor.matmul(PS[RB][:, 0:nt * P], genc1, gB[:, cs], start=True, stop=True).then_inc(g_e1, 1)
                pe.wait_ge(g_e1s, c + 1)
                nc.tensor.matmul(PS[ZB][:, 0:nt * P], genc2, gA[:, cs], start=True, stop=True).then_inc(g_e2, 1)
                pe.wait_ge(g_h0, c + 1)
            with pe.Fori(0, L) as l:
                pe.wait_ge(g_cw, l * 16 + 16)
                pe.wait_ge(g_agg, l * 2 + 2)
                for c, (t0, nt) in enumerate(CH):
                    w = nt * P
                    H, A = gH[:, t0 * P:t0 * P + w], gA[:, t0 * P:t0 * P + w]
                    if c >= 1:
                        pe.wait_ge(g_hn, l * NC + c)
                    for k, b in enumerate((RB, ZB)):
                        nc.tensor.matmul(PS[b][:, 0:w], whh[:, k * F:(k + 1) * F], H, start=True, stop=False)
                        nc.tensor.matmul(PS[b][:, 0:w], gcw[:, k * F:(k + 1) * F], A, start=False, stop=True)
                    nc.tensor.matmul(PS[NB][:, 0:w], whh[:, 2 * F:G], H, start=True, stop=True)
                    nc.tensor.matmul(PS[IB][:, 0:w], gcw[:, 2 * F:G], A, start=True, stop=True).then_inc(g_gt, 1)
            pe.wait_ge(g_rh, 1)
            for c, (t0, nt) in enumerate(CH):
                cs = slice(t0 * P, (t0 + nt) * P)
                if c >= 1:
                    pe.wait_ge(g_d2b, c)
                nc.tensor.matmul(PS[RB][:, 0:nt * P], dec1[:, :], gH[:, cs], start=True, stop=True).then_inc(g_d1, 1)
                pe.wait_ge(g_d1s, c + 1)
                for j in range(nt):
                    last = nc.tensor.matmul(PS[CB][0:P, j * F:(j + 1) * F], gB[:, (t0 + j) * P:(t0 + j + 1) * P],
                                            dec2[:, :], start=True, stop=True)
                last.then_inc(g_d2, 1)
            to_features(1)
            pe.wait_ge(g_a1, 1)
            for c, (t0, nt) in enumerate(CH):
                cs = slice(t0 * P, (t0 + nt) * P)
                if c >= 1:
                    pe.wait_ge(g_w2s, c)
                for k in range(HID // F):
                    last = nc.tensor.matmul(PS[RB + k][:, 0:nt * P], gw1[:, k * F:(k + 1) * F], gA[:, cs],
                                            start=True, stop=True)
                last.then_inc(g_w1, 1)
                pe.wait_ge(g_w1s, 2 * (c + 1))
                for k in range(HID // F):
                    last = nc.tensor.matmul(PS[NB][:, 0:nt * P], gw2[:, k, :], (gH1, gH2)[k][:, cs],
                                            start=(k == 0), stop=(k == 1))
                last.then_inc(g_w2, 1)
            pe.wait_ge(g_a2, 1)
            for c, (t0, nt) in enumerate(CH):
                if c >= 1:
                    pe.wait_ge(g_o, c)
                for j in range(nt):
                    last = nc.tensor.transpose(PS[TB][0:P, j * F:(j + 1) * F], gA[:, (t0 + j) * P:(t0 + j + 1) * P],
                                               ident[:, :])
                last.then_inc(g_ot, 1)

        def general_scalar(act):
            def normalized(k):
                act.wait_ge(g_ln, k + 1)
                if k:
                    act.wait_ge(g_ut, NC)
                for t in range(T):
                    nc.scalar.activation(gU[:, t, :], gX[:, t, :], ACT.Relu, bias=lnb[0:P, t:t + 1],
                                         scale=lnsc[0:P, t:t + 1]).then_inc(g_un, 1)
                for c, (t0, nt) in enumerate(CH):
                    act.wait_ge(g_ut, k * NC + c + 1)
                    nc.scalar.activation(gB[:, t0 * P:(t0 + nt) * P], PS[TB][:, 0:nt * P], ACT.Copy).then_inc(g_utc, 1)

            normalized(0)
            for c, (t0, nt) in enumerate(CH):
                cs = slice(t0 * P, (t0 + nt) * P)
                act.wait_ge(g_e1, c + 1)
                nc.scalar.activation(gA[:, cs], PS[RB][:, 0:nt * P], ACT.Relu, bias=bias[:, B_E1:B_E1 + 1]
                                     ).then_inc(g_e1s, 1)
                act.wait_ge(g_e2, c + 1)
                nc.scalar.activation(gH[:, cs], PS[ZB][:, 0:nt * P], ACT.Identity, bias=bias[:, B_E2:B_E2 + 1]
                                     ).then_inc(g_h0, 1)
            with act.Fori(0, L) as l:
                for c, (t0, nt) in enumerate(CH):
                    w = nt * P
                    act.wait_ge(g_gt, l * NC + (c + 1))
                    nc.scalar.activation(rS[:, 0:w], PS[RB][:, 0:w], ACT.Sigmoid, bias=bias[:, B_R:B_R + 1])
                    nc.scalar.activation(zS[:, 0:w], PS[ZB][:, 0:w], ACT.Sigmoid, bias=bias[:, B_Z:B_Z + 1]
                                         ).then_inc(g_rz, 1)
                    act.wait_ge(g_t2, l * (2 * NC) + (2 * c + 2))
                    nc.scalar.activation(nS[:, 0:w], rS[:, 0:w], ACT.Tanh, bias=bias[:, B_IN:B_IN + 1]).then_inc(g_tn, 1)
                    act.wait_ge(g_hn, l * NC + (c + 1))
            for c, (t0, nt) in enumerate(CH):
                act.wait_ge(g_d1, c + 1)
                nc.scalar.activation(gB[:, t0 * P:(t0 + nt) * P], PS[RB][:, 0:nt * P], ACT.Relu,
                                     bias=bias[:, B_D1:B_D1 + 1]).then_inc(g_d1s, 1)
                act.wait_ge(g_d2b, c + 1)
                nc.scalar.activation(yS[0:P, 0:nt * F], yS[0:P, 0:nt * F], ACT.Sigmoid).then_inc(g_sg, 1)
                act.wait_ge(g_x1, c + 1)
            normalized(1)
            for c, (t0, nt) in enumerate(CH):
                act.wait_ge(g_w1, c + 1)
                for k in range(HID // F):
                    nc.scalar.activation((gH1, gH2)[k][:, t0 * P:(t0 + nt) * P], PS[RB + k][:, 0:nt * P], ACT.Relu,
                                         bias=bias[:, B_L1 + k:B_L1 + k + 1]).then_inc(g_w1s, 1)

        @block.sync
        def _(sp):
            sp.dma_start(samp_i, dst.rearrange("(p a b) -> p a b", p=P, a=NS)).then_inc(s_samp, 16)
            sp.dma_start(table[:, 0:SL], bass.AP(src_t, 0, [[RL, TR], [1, SL]])).then_inc(s_tab, 16)
            sp.dma_start(table[:, SL:2 * SL], bass.AP(dst_t, 0, [[RL, TR], [1, SL]])).then_inc(s_tab, 16)
            sp.dma_start(X32[0:P], x.rearrange("(t p) f -> p t f", p=P)).then_inc(s_x, 16)
            for d, v in ((enc1, enc_w1T), (enc2, enc_w2T), (convT, conv_wT.rearrange("l k m -> k l m")),
                         (wih, gru_wihT), (whh[:, :], gru_whhT),
                         (bias[:, 4:5], enc_b1), (bias[:, 5:6], enc_b2), (bias[:, 6:7], dec_b1),
                         (bias[:, 7:9], l1_b1), (bias[:, 9:12], gru_bih), (bias[:, 12:15], gru_bhh),
                         (dec1[:, :], dec_w1T), (dec2[:, :], dec_w2T), (dec2b[:, :], dec_b2.to_broadcast([128, F]))):
                sp.dma_start(d, v).then_inc(s_wts, 16)
            sp.wait_ge(s_cms, L)
            sp.dma_start(comb_dram.rearrange("l k m -> k l m"), combS).then_inc(s_combst, 16)
            sp.wait_ge(s_combst, 16)
            for l in range(L):
                if l >= 2:
                    sp.wait_ge(s_gI, (l - 1) * NC)
                sp.dma_start(comb[:, l % 2, :], comb_dram[l, :, :]).then_inc(s_comb[l % 2], 16)
            sp.wait_ge(s_S, (L - 1) * NC)
            sp.dma_start(X32[0:P], x.rearrange("(t p) f -> p t f", p=P)).then_inc(s_x2, 16)
            sp.wait_ge(s_S, L * NC)
            sp.dma_start(w1, l1_w1T).then_inc(s_wts1, 16)
            sp.dma_start(w2, l1_w2T).then_inc(s_wts1, 16)
            sp.dma_start(l1b2, l1_b2.to_broadcast([128, F])).then_inc(s_wts1, 16)
            for c, (t0, nt) in enumerate(CH):
                sp.wait_ge(s_2o, c + 1)
                sp.dma_start(out.rearrange("(t p) f -> p t f", p=P)[:, t0:t0 + nt, :],
                             OUT[:, t0:t0 + nt, :]).then_inc(s_out, 16)
            sp.wait_ge(s_out, 16 * NC)
            sp.wait_ge(s_flag, 1)
            with sp.If(sp.value_load(flag[0:1, 0:1], min_val=0, max_val=1000) > 0):
                sp.dma_start(gX, x.rearrange("(t p) f -> p t f", p=P)).then_inc(g_x, 16)
                for d, v in ((genc1, enc_w1T), (genc2, enc_w2T), (gw1, l1_w1T), (gw2, l1_w2T),
                             (gb2, l1_b2.rearrange("a f -> f a"))):
                    sp.dma_start(d, v).then_inc(g_w, 16)

                def edge_loads(first):
                    with sp.Fori(0, T) as k:
                        sp.wait_ge(g_ebfree, first + k + 1)
                        sp.dma_start(ebuf[:, 0, :], src.rearrange("(k e) -> k e", e=EC)[bass.ds(k, 1), :]
                                     ).then_inc(g_eb, 16)
                        sp.dma_start(ebuf[:, 1, :], dst.rearrange("(k e) -> k e", e=EC)[bass.ds(k, 1), :]
                                     ).then_inc(g_eb, 16)

                with sp.Fori(0, L) as l:
                    sp.wait_ge(g_h0, NC)
                    sp.wait_ge(g_hn, l * NC)
                    sp.dma_start(gcw.unsqueeze(1), comb_dram[bass.ds(l, 1), :, :].rearrange("a k m -> k a m")
                                 ).then_inc(g_cw, 16)
                    edge_loads(l * T)
                for n in range(3):
                    edge_loads((L + n) * T)
                for c, (t0, nt) in enumerate(CH):
                    sp.wait_ge(g_o, c + 1)
                    sp.dma_start(out.rearrange("(t p) f -> p t f", p=P)[:, t0:t0 + nt, :],
                                 gX[:, t0:t0 + nt, :]).then_inc(g_out, 16)
                sp.wait_ge(g_out, 16 * NC)

        @block.gpsimd
        def _(pool):
            pool.memset(mhalf[:, :], -0.5).then_inc(s_mhalf, 1)
            pool.memset(ones, 1.0).then_inc(s_ones, 1)
            pool.memset(ident[:, :], 0.0).then_inc(s_id, 1)
            pool.wait_ge(s_id, 1)
            pool.affine_select(out=ident[:, :], in_=ident[:, :], compare_op=ALU.not_equal, fill=1.0,
                               base=0, pattern=[[-1, 128]], channel_multiplier=1).then_inc(s_id, 1)
            pool.iota(wstart, [[W * PW, KW]], base=0, channel_multiplier=W,
                      allow_small_or_imprecise_dtypes=True).then_inc(s_ws, 1)
            pool.iota(wstart1, [[W * PW, KW]], base=-1, channel_multiplier=W,
                      allow_small_or_imprecise_dtypes=True).then_inc(s_ws, 1)
            pool.iota(iotaP, [[1, P], [0, J]], base=0, channel_multiplier=0,
                      allow_small_or_imprecise_dtypes=True).then_inc(s_iota, 1)
            pool.iota(iotaK, [[1, W * T], [0, J]], base=1, channel_multiplier=0,
                      allow_small_or_imprecise_dtypes=True).then_inc(s_iota, 1)
            pool.wait_ge(s_mhalf, 1)
            pool.wait_ge(s_mv, 1)
            pool.tensor_tensor(lnsc[0:P, :], mv[0:P, :, 1], mhalf[0:P, :], ALU.pow).then_inc(s_rs, 1)
            pool.wait_ge(s_idx, 1)
            pool.wait_ge(s_tab, 32)
            for k in range(KW):
                pool.indirect_dma_start(out=Gt[:, k, :], out_offset=None, in_=table[:, :],
                                        in_offset=bass.IndirectOffsetOnAxis(ap=idx[:, k:k + 1], axis=0)
                                        ).then_inc(s_gath[k], 16)

            for c, (t0, nt) in enumerate(CH):
                pool.wait_ge(s_ehi, c + 1)
                pool.tensor_tensor(H16[0:P, 0, t0:t0 + nt, 1, :],
                                   yS[0:P, 0:nt * F].rearrange("p (t f) -> p t f", t=nt),
                                   H16[0:P, 0, t0:t0 + nt, 0, :], ALU.subtract).then_inc(s_elo, 1)
            pool.wait_ge(s_mv, 2)
            pool.tensor_tensor(dinv[0:P, :], deg[0:P, :], mhalf[0:P, :], ALU.pow).then_inc(s_rs, 1)
            def low_half(c):
                t0, nt = CH[c]
                pool.wait_ge(s_uh, c + 1)
                pool.tensor_tensor(V16[0:P, t0:t0 + nt, 1, :], U32[:, t0:t0 + nt, :], V16[0:P, t0:t0 + nt, 0, :],
                                   ALU.subtract).then_inc(s_uhl, 1)

            for c, (t0, nt) in enumerate(CH):
                pool.wait_ge(s_mv, 3 + c)
                pool.tensor_tensor(lnsc[0:P, t0:t0 + nt], mv[0:P, t0:t0 + nt, 1], mhalf[0:P, 0:nt], ALU.pow
                                   ).then_inc(s_rs, 1)
                if c == NC - 5:
                    pool.wait_ge(s_S, L * NC)
                    pool.memset(onesL, 1.0).then_inc(s_onesL, 1)
                    low_half(0)
                if c >= NC - 5:
                    low_half(c - NC + 6)
            low_half(NC - 1)
            pool.wait_ge(s_flag, 1)
            with pool.If(pool.value_load(flag[0:1, 0:1], min_val=0, max_val=1000) > 0):
                for k in range(2):
                    pool.wait_ge(g_mv, k + 1)
                    pool.tensor_tensor(lnsc[0:P, :], mv[0:P, :, 1], mhalf[0:P, :], ALU.pow).then_inc(g_rs, 1)
                pool.wait_ge(g_deg, 1)
                pool.tensor_tensor(gD, gD, mhalf[:, 0:1].to_broadcast([128, N]), ALU.pow).then_inc(g_dinv, 1)

        @block.vector
        def _(dve):
            n = [0]

            def link(ins):
                n[0] += 1
                ins.then_inc(s_chain, 1)
                dve.wait_ge(s_chain, n[0])

            dve.wait_ge(s_x, 16)

            def norm_stats(t0, t1):
                for t in range(t0, t1):
                    last = nc.vector.bn_stats(stat[0:P, t - t0, :], X32[0:P, t, :])
                link(last)
                for t in range(t0, t1):
                    last = nc.vector.bn_aggr(mv[0:P, t, :], stat[0:P, t - t0, :])
                link(last)

            for t0, nt in CH:
                norm_stats(t0, t0 + nt)
            nc.vector.tensor_scalar(mv[0:P, :, 1], mv[0:P, :, 1], 1e-5, None, ALU.add).then_inc(s_mv, 1)
            dve.wait_ge(s_rs, 1)
            nc.vector.scalar_tensor_tensor(lnb[0:P, :], mv[0:P, :, 0], -1.0, lnsc[0:P, :], ALU.mult, ALU.mult
                                           ).then_inc(s_ln, 1)
            dve.wait_ge(s_samp, 16)
            link(nc.vector.tensor_copy(samp, samp_i[:, :, 0]))
            dve.wait_ge(s_id, 2)
            nc.vector.tensor_tensor(diag, ident[0:P, 0:P].unsqueeze(1).to_broadcast([P, NS, P]),
                                    samp.unsqueeze(2).to_broadcast([P, NS, P]), ALU.mult).then_inc(s_diag, 1)
            nc.vector.memset(cnt, 0.0)
            dve.wait_ge(s_ws, 2)
            dve.wait_ge(s_bc, 5)
            link(nc.vector.tensor_copy(junk.rearrange("p (a b) -> p a b", a=5)[:, 0, :], PS[0][0:P, 0:425]))
            for q in range(1, 5):
                last = nc.vector.tensor_copy(junk[:, 425 * q:425 * q + 425], PS[q][0:P, 0:425])
            link(last)
            dve.sem_inc(s_bcused, 1)
            for k in range(KW):
                last = nc.vector.tensor_scalar(diag[0:PW].rearrange("p a b -> p (a b)"), junk[0:PW, :],
                                               wstart[:, k:k + 1], None, ALU.is_lt, ALU.add,
                                               accum_out=cnt[:, k:k + 1])
                link(last)
            link(nc.vector.tensor_scalar(cnt, cnt, -1.0, 0.0, ALU.add, ALU.max))
            link(nc.vector.tensor_scalar(cnt, cnt, float(TR - 1), None, ALU.min))
            nc.vector.tensor_copy(idx, cnt).then_inc(s_idx, 1)
            dve.wait_ge(s_wts, 14 * 16)
            nc.vector.tensor_tensor(bias[:, 0:2], bias[:, 9:11], bias[:, 12:14], ALU.add)
            nc.vector.tensor_copy(bias[:, 2:3], bias[:, 14:15])
            link(nc.vector.tensor_copy(bias[:, 3:4], bias[:, 11:12]))
            nc.vector.tensor_copy(ident16[:, :], ident[:, :]).then_inc(s_id16, 1)
            for k in range(KW):
                dve.wait_ge(s_gath[k], 16)
            sr, ds = Gt[:, :, 0:SL], Gt[:, :, SL:2 * SL]
            link(nc.vector.tensor_scalar(tf, sr, -float((P - 1) // 2), 1.0 / P, ALU.add, ALU.mult))
            link(nc.vector.tensor_scalar(tf, tf, MAGIC, MAGIC, ALU.add, ALU.subtract))
            link(nc.vector.scalar_tensor_tensor(pf, tf, -float(P), sr, ALU.mult, ALU.add))
            for k in range(KW):
                last = nc.vector.tensor_scalar(kf[:, k, :], ds[:, k, :], wstart1[:, k:k + 1], None, ALU.subtract)
            link(last)
            link(nc.vector.scalar_tensor_tensor(tf, tf, float(W), kf, ALU.mult, ALU.add))
            link(nc.vector.scalar_tensor_tensor(tf, kf, 1.0, tf, ALU.is_ge, ALU.mult))
            nc.vector.scalar_tensor_tensor(kf, kf, float(W), tf, ALU.is_le, ALU.mult).then_inc(s_keys, 1)
            dve.wait_ge(s_ktr, 1)
            for c in range(2):
                for k in range(KW):
                    j = c * KW + k
                    for dstv, base in ((pT, 0), (kT, 3)):
                        last = nc.vector.tensor_copy(dstv[:, k, :].rearrange("p (w c) -> p w c", c=2)[:, :, c],
                                                     PS[base + j // 3][0:P, (j % 3) * PW:(j % 3) * PW + PW])
            link(last)
            dve.wait_ge(s_iota, 2)
            with dve.Fori(0, PW // WB) as i:
                for k in range(KW):
                    dve.wait_ge(s_win, i * NG + (k + 1) * (NG // KW))
                    for oh, io, v, n_ in ((ohP, iotaP, pT, P), (ohK, iotaK, kT, W * T)):
                        last = nc.vector.tensor_tensor(
                            oh[:, k, :, :], io,
                            v[:, k, bass.ds(i * J, J)].unsqueeze(1).to_broadcast([P, n_, J]), ALU.is_equal)
                    last.then_inc(s_oh, 1)

            def decoded(c):
                t0, nt = CH[c]
                if c == 0:
                    dve.wait_ge(s_x2, 16)
                dve.wait_ge(s_d2, c + 1)
                y = yS[0:P, 0:nt * F].rearrange("p (t f) -> p t f", t=nt)
                nc.vector.tensor_tensor(y, PS[CB][0:P, 0:nt * F].rearrange("p (t f) -> p t f", t=nt),
                                        dec2b[0:P, :].unsqueeze(1).to_broadcast([P, nt, F]),
                                        ALU.add).then_inc(s_d2b, 1)
                dve.wait_ge(s_sg, c + 1)
                link(nc.vector.tensor_tensor(X32[0:P, t0:t0 + nt, :], X32[0:P, t0:t0 + nt, :], y, ALU.add))
                norm_stats(t0, t0 + nt)
                nc.vector.tensor_scalar(mv[0:P, t0:t0 + nt, 1], mv[0:P, t0:t0 + nt, 1], 1e-5, None, ALU.add
                                        ).then_inc(s_mv, 1)
                dve.wait_ge(s_rs, 2 + c + 1)
                sc = lnsc[0:P, t0:t0 + nt]
                link(nc.vector.scalar_tensor_tensor(sc, dinv[0:P, t0:t0 + nt], S1, sc, ALU.mult, ALU.mult))
                nc.vector.scalar_tensor_tensor(lnb[0:P, t0:t0 + nt], mv[0:P, t0:t0 + nt, 0], -1.0, sc,
                                               ALU.mult, ALU.mult).then_inc(s_lsc, 1)

            def degrees():
                dve.wait_ge(s_deg, T)
                link(nc.vector.tensor_reduce(chk[0:P, 0:1], deg[0:P, :], AX.X, ALU.add))
                nc.vector.tensor_scalar(deg[0:P, :], deg[0:P, :], 1.0, 1.0, ALU.add, ALU.max).then_inc(s_mv, 1)
                dve.wait_ge(s_rs, 2)
                link(nc.vector.tensor_scalar(dinvs[0:P, :], dinv[0:P, :], S0, None, ALU.mult))

            def high_half(c):
                t0, nt = CH[c]
                dve.wait_ge(s_u, t0 + nt)
                nc.vector.tensor_copy(V16[0:P, t0:t0 + nt, 0, :], U32[:, t0:t0 + nt, :]).then_inc(s_uh, 1)

            def decoded_tail():
                decoded(NC - 1)
                for c in range(5, NC):
                    high_half(c)
                nc.vector.tensor_tensor(diagD, ident[0:P, 0:P].unsqueeze(1).to_broadcast([P, T, P]),
                                        dinv[0:P, :].unsqueeze(2).to_broadcast([P, T, P]),
                                        ALU.mult).then_inc(s_diagD, 1)
                dve.wait_ge(s_wts1, 48)
                dve.wait_ge(s_u, T)
                link(nc.vector.tensor_tensor(X32[0:P], X32[0:P], l1b2[0:P, :].unsqueeze(1).to_broadcast([P, T, F]),
                                             ALU.add))
                for c in range(NC + 2):
                    if c < NC:
                        n0, w = CH[c][0] * P, CH[c][1] * P
                        dve.wait_ge(s_1S, c + 1)
                        dve.wait_ge(s_dBs, c + 1)
                        if c >= 1:
                            dve.wait_ge(s_1g, 2 * c)
                        nc.vector.scalar_tensor_tensor(aggS[:, 0:w], PS[AGG[(c + 1) % 2]][:, 0:w], 1.0 / S1,
                                                       dinvB[:, n0:n0 + w], ALU.mult, ALU.mult).then_inc(s_1a, 1)
                    if c >= 2:
                        t0, nt = CH[c - 2]
                        dve.wait_ge(s_1hi, c - 1)
                        for j in range(nt):
                            last = nc.vector.scalar_tensor_tensor(
                                Z16[:, t0 + j, 1, :], PS[IB][0:P, j * F:j * F + F], dinvs[0:P, t0 + j:t0 + j + 1],
                                Z16[:, t0 + j, 0, :], ALU.mult, ALU.subtract)
                        last.then_inc(s_1lo, 1)
                link(nc.vector.tensor_reduce(chk[0:P, 2:3], Z16[:, :, 0, :], AX.XY, ALU.max, apply_absolute_value=True))
                nc.vector.tensor_scalar(chk[0:P, 2:3], chk[0:P, 2:3], LIMIT * S0, None, ALU.is_gt).then_inc(s_chk, 1)
                dve.wait_ge(s_chksum, 1)
                nc.vector.tensor_scalar(flag_f[:, 0:1], PS[RB][0:1, 0:1], float(E), None, ALU.not_equal)
                nc.vector.tensor_copy(flag_f[:, 1:2], PS[RB][0:1, 1:2])
                link(nc.vector.tensor_copy(flag_f[:, 2:3], PS[RB][0:1, 2:3]))
                link(nc.vector.tensor_reduce(flag_f[:, 3:4], flag_f[:, 0:3], AX.X, ALU.add))
                nc.vector.tensor_copy(flag[:, :], flag_f[:, 3:4]).then_inc(s_flag, 1)
                for c, (t0, nt) in enumerate(CH):
                    dve.wait_ge(s_2t, c + 1)
                    for j in range(nt):
                        last = nc.vector.scalar_tensor_tensor(
                            OUT[:, t0 + j, :], PS[TB][0:P, j * F:j * F + F], dinv[0:P, t0 + j:t0 + j + 1],
                            X32[0:P, t0 + j, :], ALU.mult, ALU.add)
                    last.then_inc(s_2o, 1)

            link(nc.vector.memset(chk[:, :], 0.0))
            dve.wait_ge(s_elo, NC)
            link(nc.vector.tensor_reduce(chk[:, 1:2], HT[:, :], AX.X, ALU.max, apply_absolute_value=True))
            link(nc.vector.tensor_scalar(chk[:, 1:2], chk[:, 1:2], LIMIT, None, ALU.is_gt))
            for l in range(L):
                for c in range(NC + 2):
                    q = l * NC + c
                    if c < NC:
                        for m in cgroups(q):
                            if m % 2 == 0:
                                evac_block_group(dve, m)
                    if 1 <= c <= NC:
                        n0, w = CH[c - 1][0] * P, CH[c - 1][1] * P
                        H = HT[:, n0:n0 + w]
                        dve.wait_ge(s_gN, q)
                        dve.wait_ge(s_r, q)
                        nc.vector.scalar_tensor_tensor(rS[:, 0:w], PS[NB][:, 0:w], bias[:, B_HN:B_HN + 1],
                                                       rS[:, 0:w], ALU.add, ALU.mult).then_inc(s_t1, 1)
                        if l == L - 1 and c == NC - 1:
                            high_half(0)
                        dve.wait_ge(s_t1, q)
                        dve.wait_ge(s_gI, q)
                        nc.vector.tensor_tensor(rS[:, 0:w], PS[IB][:, 0:w], rS[:, 0:w], ALU.add).then_inc(s_t2, 1)
                    if c >= 2 and l < L - 1:
                        t0, nt = CH[c - 2]
                        dve.wait_ge(s_hi, q - 1)
                        nc.vector.scalar_tensor_tensor(
                            H16[0:P, (l + 1) % 2, t0:t0 + nt, 1, :],
                            PS[TB][0:P, 0:nt * F].rearrange("p (t f) -> p t f", t=nt), S0,
                            H16[0:P, (l + 1) % 2, t0:t0 + nt, 0, :], ALU.mult, ALU.subtract).then_inc(s_lo, 1)
                    if 1 <= c <= NC:
                        dve.wait_ge(s_n, q)
                        link(nc.vector.tensor_tensor(H, H, nS[:, 0:w], ALU.subtract))
                        link(nc.vector.tensor_tensor(H, H, zS[:, 0:w], ALU.mult))
                        last = nc.vector.tensor_tensor(H, H, nS[:, 0:w], ALU.add)
                        if l == L - 1:
                            link(last)
                            last = nc.vector.tensor_scalar(H, H, 0.0, None, ALU.max)
                        last.then_inc(s_h, 1)
                    if l == L - 1 and c == 0:
                        degrees()
                    if l == L - 1 and c >= 3:
                        if NC - 1 <= c <= NC:
                            high_half(c - NC + 2)
                        decoded(c - 3)
                        if c >= NC:
                            high_half(c - NC + 3)
            decoded_tail()
            dve.wait_ge(s_flag, 1)
            with dve.If(dve.value_load(flag[0:1, 0:1], min_val=0, max_val=1000) > 0):
                general_vector(dve)
        @block.tensor
        def _(pe):
            pe.sem_inc(s_win, NG)
            pe.wait_ge(s_ones, 1)
            pe.wait_ge(s_diag, 1)
            dg = diag.rearrange("p a b -> p (a b)")
            for q in range(5):
                nc.tensor.matmul(PS[q][0:P, 0:425], ones[0:P, 0:P], dg[:, 425 * q:425 * q + 425],
                                 start=True, stop=True).then_inc(s_bc, 1)
            pe.wait_ge(s_wts, 14 * 16)
            pe.wait_ge(s_bcused, 1)
            for s in range(NC + 3):
                if s < NC:
                    t0, nt = CH[s]
                    pe.wait_ge(s_xn, t0 + nt)
                    if s >= 1:
                        pe.wait_ge(s_eXs, s)
                    for j in range(nt):
                        last = nc.tensor.transpose(PS[5][:, j * P:(j + 1) * P], X32[0:P, t0 + j, :], ident[0:P, 0:P])
                    last.then_inc(s_eX, 1)
                if 1 <= s <= NC:
                    w = CH[s - 1][1] * P
                    pe.wait_ge(s_eXs, s)
                    if s >= 2:
                        pe.wait_ge(s_e1s, s - 1)
                    nc.tensor.matmul(PS[6][:, 0:w], enc1, aggS[:, 0:w], start=True, stop=True).then_inc(s_e1, 1)
                if 2 <= s <= NC + 1:
                    w = CH[s - 2][1] * P
                    pe.wait_ge(s_e1s, s - 1)
                    if s >= 3:
                        pe.wait_ge(s_eh, s - 2)
                    nc.tensor.matmul(PS[7][:, 0:w], enc2, rS[:, 0:w], start=True, stop=True).then_inc(s_e2, 1)
                if s >= 3:
                    t0, nt = CH[s - 3]
                    pe.wait_ge(s_eh, s - 2)
                    if s >= 4:
                        pe.wait_ge(s_eTs, s - 3)
                    for j in range(nt):
                        last = nc.tensor.transpose(PS[4][0:P, j * F:(j + 1) * F],
                                                   HT[:, (t0 + j) * P:(t0 + j + 1) * P], ident[:, :])
                    last.then_inc(s_eT, 1)
            for l in range(L):
                if l >= 1:
                    pe.wait_ge(s_cms, l)
                nc.tensor.matmul(PS[5][:, 0:G], convT[:, l, :], wih, start=True, stop=True).then_inc(s_cm, 1)
            pe.wait_ge(s_cms, L)
            pe.wait_ge(s_keys, 1)
            for c in range(2):
                for k in range(KW):
                    j = c * KW + k
                    for base, v in ((0, pf), (3, kf)):
                        last = nc.tensor.transpose(PS[base + j // 3][0:P, (j % 3) * PW:(j % 3) * PW + PW],
                                                   v[:, k, c * P:(c + 1) * P], ident[0:PW, 0:PW])
            last.then_inc(s_ktr, 1)
            with pe.Fori(0, PW // WB) as i:
                for k in range(KW):
                    pe.wait_ge(s_oh, i * KW + (k + 1))
                    for pr in range(WB // 2):
                        g = k * (WB // 2) + pr
                        pe.wait_ge(s_winfree, i * NG + (g + 1))
                        for w in range(2):
                            for c in range(2):
                                j = (pr * 2 + w) * 2 + c
                                last = nc.tensor.matmul(PS[g][0:P, w * W * T:(w + 1) * W * T], ohP[:, k, :, j],
                                                        ohK[:, k, :, j], start=(c == 0), stop=(c == 1))
                        last.then_inc(s_win, 1)
            def aggregate(bank, w, n0, adj, halves, c, groups=(), loops=False, ready=None, between=None):
                m = list(groups)
                for t in range(T):
                    if between is not None and t % TC == 0:
                        between(t // TC)
                    if ready is not None and t % TC == 0:
                        pe.wait_ge(*ready(t // TC))
                    for h in range(2):
                        last = nc.tensor.matmul(PS[bank][:, 0:w], halves[0:P, t, h, :], adj[0:P, t, n0:n0 + w],
                                                start=(t == 0 and h == 0), stop=(t == T - 1 and h == 1 and not loops))
                    if m and t in SPOT:
                        block_group(m.pop(0))
                if loops:
                    t0, nt = CH[c]
                    for j in range(nt):
                        for h in range(2):
                            last = nc.tensor.matmul(PS[bank][:, j * P:(j + 1) * P], halves[0:P, t0 + j, h, :],
                                                    ident16[0:P, 0:P], start=False, stop=(j == nt - 1 and h == 1))
                return last

            def block_group(m):
                if m >= 1:
                    pe.wait_ge(s_cev[(m - 1) % 2], (m - 1) // 2 + 1)
                b0, nb = 4 * m, min(4, NBLK - 4 * m)
                for j in range(nb):
                    tr, tc = divmod(b0 + j, T)
                    last = nc.tensor.matmul(PS[CB][0:P, j * P:(j + 1) * P], AT3[0:P, tc, tr * P:(tr + 1) * P],
                                            ident16[0:P, 0:P], start=True, stop=True)
                last.then_inc(s_cfull, 1)

            def gates(l, q, c):
                n0, w = CH[c][0] * P, CH[c][1] * P
                H = HT[:, n0:n0 + w]
                cl = comb[:, l % 2, :]
                pe.wait_ge(s_r, q) if q else None
                nc.tensor.matmul(PS[RB][:, 0:w], whh[:, 0:F], H, start=True, stop=False)
                pe.wait_ge(s_z, q) if q else None
                nc.tensor.matmul(PS[ZB][:, 0:w], whh[:, F:2 * F], H, start=True, stop=False)
                pe.wait_ge(s_t1, q) if q else None
                nc.tensor.matmul(PS[NB][:, 0:w], whh[:, 2 * F:G], H, start=True, stop=True).then_inc(s_gN, 1)
                pe.wait_ge(s_agg, q + 1)
                if c == 0:
                    pe.wait_ge(s_comb[l % 2], 16 * (l // 2 + 1))
                nc.tensor.matmul(PS[RB][:, 0:w], cl[:, 0:F], aggS[:, 0:w], start=False, stop=True).then_inc(s_gR, 1)
                nc.tensor.matmul(PS[ZB][:, 0:w], cl[:, F:2 * F], aggS[:, 0:w], start=False, stop=True).then_inc(s_gZ, 1)
                pe.wait_ge(s_t2, q) if q else None
                nc.tensor.matmul(PS[IB][:, 0:w], cl[:, 2 * F:G], aggS[:, 0:w], start=True, stop=True).then_inc(s_gI, 1)

            def decode1(c):
                n0, w = CH[c][0] * P, CH[c][1] * P
                pe.wait_ge(s_h, (L - 1) * NC + c + 1)
                if c == 0:
                    pe.wait_ge(s_lo, (L - 1) * NC)
                else:
                    pe.wait_ge(s_d1s, c)
                nc.tensor.matmul(PS[TB][:, 0:w], dec1[:, :], HT[:, n0:n0 + w], start=True, stop=True).then_inc(s_d1, 1)

            def decode2(c):
                t0, nt = CH[c]
                pe.wait_ge(s_d1s, c + 1)
                if c == 0:
                    pe.wait_ge(s_cev[0], (NCG + 1) // 2)
                    pe.wait_ge(s_cev[1], NCG // 2)
                else:
                    pe.wait_ge(s_d2b, c)
                for j in range(nt):
                    last = nc.tensor.matmul(PS[CB][0:P, j * F:(j + 1) * F], HT[:, (t0 + j) * P:(t0 + j + 1) * P],
                                            dec2[:, :], start=True, stop=True)
                last.then_inc(s_d2, 1)

            pe.wait_ge(s_winfree, NG + PW // WB * NG)
            pe.wait_ge(s_elo, NC)
            pe.wait_ge(s_id16, 1)
            def state_back(l, c):
                t0, nt = CH[c]
                q = l * NC + c
                pe.wait_ge(s_h, q + 1)
                if q >= 1:
                    pe.wait_ge(s_lo, q)
                for j in range(nt):
                    last = nc.tensor.transpose(PS[TB][0:P, j * F:(j + 1) * F],
                                               HT[:, (t0 + j) * P:(t0 + j + 1) * P], ident[:, :])
                last.then_inc(s_tr, 1)

            def last_chunks(l):
                def step(g):
                    if g == 2:
                        gates(l, (l + 1) * NC - 1, NC - 1)
                    if g == NC - 3:
                        state_back(l, NC - 2)
                    if g == NC - 2:
                        state_back(l, NC - 1)
                return step

            for l in range(L):
                for c in range(NC):
                    q = l * NC + c
                    if c < NC:
                        n0, w = CH[c][0] * P, CH[c][1] * P
                        if q >= 2:
                            pe.wait_ge(s_agg, q - 1)
                        ready = between = None
                        if c == 0 and l >= 1:
                            ready = lambda g: (s_lo, (l - 1) * NC + g + 1)
                            between = last_chunks(l - 1)
                        aggregate(AGG[q % 2], w, n0, AT3, H16[:, l % 2], c, cgroups(q), ready=ready,
                                  between=between).then_inc(s_S, 1)
                    if 1 <= c <= NC:
                        gates(l, q - 1, c - 1)
                    if 2 <= c and l < L - 1:
                        state_back(l, c - 2)
                    if l == L - 1:
                        if 2 <= c:
                            decode1(c - 2)
                        if 3 <= c:
                            decode2(c - 3)

            def last_decodes(g):
                if g == 1:
                    gates(L - 1, L * NC - 1, NC - 1)
                if g == 2:
                    decode1(NC - 2)
                    decode2(NC - 3)
                if g == 3:
                    decode1(NC - 1)
                    decode2(NC - 2)
                if g == 4:
                    decode2(NC - 1)

            def column_scales():
                pe.wait_ge(s_onesL, 1)
                pe.wait_ge(s_diagD, 1)
                for c, (t0, nt) in enumerate(CH):
                    if c >= 2:
                        pe.wait_ge(s_dBs, c - 1)
                    nc.tensor.matmul(PS[RB + c % 2][:, 0:nt * P], onesL[0:P, :],
                                     diagD[:, t0:t0 + nt, :].rearrange("p a b -> p (a b)"),
                                     start=True, stop=True).then_inc(s_dB, 1)

            def expand(c):
                w = CH[c][1] * P
                pe.wait_ge(s_1a, c + 1)
                if c == 0:
                    pe.wait_ge(s_wts1, 48)
                    pe.wait_ge(s_dBs, NC)
                else:
                    pe.wait_ge(s_1h, 2 * c)
                for k in range(HID // F):
                    nc.tensor.matmul(PS[RB + k][:, 0:w], w1[:, k * F:(k + 1) * F], aggS[:, 0:w],
                                     start=True, stop=True).then_inc(s_1g, 1)

            def project(c):
                nt = CH[c][1]
                pe.wait_ge(s_1h, 2 * (c + 1))
                if c >= 1:
                    pe.wait_ge(s_1lo, c)
                for j in range(nt):
                    for k in range(HID // F):
                        last = nc.tensor.matmul(PS[IB][0:P, j * F:(j + 1) * F],
                                                (rS, zS)[k][:, j * P:(j + 1) * P], w2[:, k, :],
                                                start=(k == 0), stop=(k == 1))
                last.then_inc(s_1p, 1)

            def last_projections(g):
                if g == 1:
                    expand(NC - 1)
                if g == 2:
                    project(NC - 2)
                if g == 4:
                    project(NC - 1)

            pe.wait_ge(s_agg, L * NC - 1)
            for c in range(NC):
                n0, w = CH[c][0] * P, CH[c][1] * P
                if c >= 2:
                    pe.wait_ge(s_1a, c - 1)
                if c == 1:
                    pe.wait_ge(s_agg, L * NC)
                aggregate(AGG[(c + 1) % 2], w, n0, CT3, V16, c, loops=True,
                          ready=(lambda g: (s_uhl, g + 1)) if c == 0 else None,
                          between=last_decodes if c == 0 else None).then_inc(s_1S, 1)
                if c == 0:
                    column_scales()
                if c >= 1:
                    expand(c - 1)
                if c >= 2:
                    project(c - 2)
            for c in range(NC + 1):
                if c == 2:
                    pe.wait_ge(s_chk, 1)
                    nc.tensor.matmul(PS[RB][0:1, 0:3], onesL[:, 0:1], chk[:, 0:3], start=True, stop=True
                                     ).then_inc(s_chksum, 1)
                if c < NC:
                    n0, w = CH[c][0] * P, CH[c][1] * P
                    if c < 2:
                        pe.wait_ge(s_1a, NC - 1 + c)
                    else:
                        pe.wait_ge(s_2a, c - 1)
                    aggregate(AGG[c % 2], w, n0, CT3, Z16, c, loops=True,
                              ready=(lambda g: (s_1lo, g + 1)) if c == 0 else None,
                              between=last_projections if c == 0 else None).then_inc(s_2S, 1)
                if c >= 1:
                    nt = CH[c - 1][1]
                    pe.wait_ge(s_2a, c)
                    if c >= 2:
                        pe.wait_ge(s_2o, c - 1)
                    for j in range(nt):
                        last = nc.tensor.transpose(PS[TB][0:P, j * F:(j + 1) * F], aggS[:, j * P:(j + 1) * P],
                                                   ident[:, :])
                    last.then_inc(s_2t, 1)

            pe.wait_ge(s_flag, 1)
            with pe.If(pe.value_load(flag[0:1, 0:1], min_val=0, max_val=1000) > 0):
                general_tensor(pe)

        @block.scalar
        def _(act):
            def decode_sig(c):
                nt = CH[c][1]
                act.wait_ge(s_d2b, c + 1)
                nc.scalar.activation(yS[0:P, 0:nt * F], yS[0:P, 0:nt * F], ACT.Sigmoid).then_inc(s_sg, 1)

            ndeg = [0]

            def degree(t):
                if ndeg[0] == 0:
                    act.wait_ge(s_combst, 16)
                else:
                    act.wait_ge(s_deg, ndeg[0])
                ndeg[0] += 1
                nc.scalar.activation(CT3[0:P, T - 1, :], AT3[0:P, t, 0:N], ACT.Copy, saturate=False,
                                     accum_out=deg[0:P, t:t + 1]).then_inc(s_deg, 1)

            def second_input(c):
                t0, nt = CH[c]
                if c == 0:
                    act.wait_ge(s_S, L * NC)
                act.wait_ge(s_lsc, c + 1)
                for t in range(t0, t0 + nt):
                    nc.scalar.activation(U32[:, t, :], X32[0:P, t, :], ACT.Relu, bias=lnb[0:P, t:t + 1],
                                         scale=lnsc[0:P, t:t + 1]).then_inc(s_u, 1)

            act.wait_ge(s_ln, 1)
            for t in range(T):
                nc.scalar.activation(X32[0:P, t, :], X32[0:P, t, :], ACT.Relu, bias=lnb[0:P, t:t + 1],
                                     scale=lnsc[0:P, t:t + 1]).then_inc(s_xn, 1)
            act.wait_ge(s_wts, 14 * 16)
            for s in range(NC + 3):
                if s < NC:
                    w = CH[s][1] * P
                    act.wait_ge(s_eX, s + 1)
                    if s >= 1:
                        act.wait_ge(s_e1, s)
                    nc.scalar.activation(aggS[:, 0:w], PS[5][:, 0:w], ACT.Copy).then_inc(s_eXs, 1)
                if 1 <= s <= NC:
                    w = CH[s - 1][1] * P
                    act.wait_ge(s_e1, s)
                    if s >= 2:
                        act.wait_ge(s_e2, s - 1)
                    nc.scalar.activation(rS[:, 0:w], PS[6][:, 0:w], ACT.Relu, bias=bias[:, B_E1:B_E1 + 1]
                                         ).then_inc(s_e1s, 1)
                if 2 <= s <= NC + 1:
                    n0, w = CH[s - 2][0] * P, CH[s - 2][1] * P
                    act.wait_ge(s_e2, s - 1)
                    nc.scalar.activation(HT[:, n0:n0 + w], PS[7][:, 0:w], ACT.Identity, bias=bias[:, B_E2:B_E2 + 1]
                                         ).then_inc(s_eh, 1)
                if s >= 3:
                    t0, nt = CH[s - 3]
                    act.wait_ge(s_eT, s - 2)
                    if s >= 4:
                        act.wait_ge(s_elo, s - 3)
                    nc.scalar.activation(yS[0:P, 0:nt * F], PS[4][0:P, 0:nt * F], ACT.Copy, scale=S0).then_inc(s_eTs, 1)
                    act.wait_ge(s_eTs, s - 2)
                    nc.scalar.activation(H16[0:P, 0, t0:t0 + nt, 0, :],
                                         yS[0:P, 0:nt * F].rearrange("p (t f) -> p t f", t=nt),
                                         ACT.Copy).then_inc(s_ehi, 1)
            for l in range(L):
                act.wait_ge(s_cm, l + 1)
                nc.scalar.activation(combS[:, l, :], PS[5][:, 0:G], ACT.Copy).then_inc(s_cms, 1)
            act.sem_inc(s_winfree, NG)
            for n in range(PW // WB * NG):
                i, g = n // NG, n % NG
                k, pr = g // (WB // 2), g % (WB // 2)
                act.wait_ge(s_win, NG + n + 1)
                d0 = (k * PW + WB * i + 2 * pr) * W
                nc.scalar.activation(
                    AT3[0:P, :, d0:d0 + 2 * W].rearrange("p t (w d) -> p w t d", w=2),
                    PS[g][0:P, 0:2 * W * T].rearrange("p (w t d) -> p w t d", w=2, t=T),
                    ACT.Copy, saturate=False).then_inc(s_winfree, 1)
            for l in range(L):
                for c in range(NC + 2):
                    q = l * NC + c
                    if c < NC:
                        for m in cgroups(q):
                            if m % 2 == 1:
                                evac_block_group(act, m)
                        w = CH[c][1] * P
                        for t in (q, q + 3 * NC):
                            if t < T and q < 3 * NC:
                                degree(t)
                        act.wait_ge(s_S, q + 1)
                        if q >= 1:
                            act.wait_ge(s_gI, q)
                        nc.scalar.activation(aggS[:, 0:w], PS[AGG[q % 2]][:, 0:w], ACT.Copy, scale=1.0 / S0
                                             ).then_inc(s_agg, 1)
                    if 1 <= c <= NC:
                        w = CH[c - 1][1] * P
                        act.wait_ge(s_gR, q)
                        if q >= 2:
                            act.wait_ge(s_n, q - 1)
                        nc.scalar.activation(rS[:, 0:w], PS[RB][:, 0:w], ACT.Sigmoid, bias=bias[:, B_R:B_R + 1]
                                             ).then_inc(s_r, 1)
                        act.wait_ge(s_gZ, q)
                        if q >= 2:
                            act.wait_ge(s_h, q - 1)
                        nc.scalar.activation(zS[:, 0:w], PS[ZB][:, 0:w], ACT.Sigmoid, bias=bias[:, B_Z:B_Z + 1]
                                             ).then_inc(s_z, 1)
                    if l == L - 1 and NC - 1 <= c <= NC:
                        second_input(2 * (c - NC + 1))
                    if c >= 2 and l < L - 1:
                        t0, nt = CH[c - 2]
                        act.wait_ge(s_tr, q - 1)
                        nc.scalar.activation(H16[0:P, (l + 1) % 2, t0:t0 + nt, 0, :],
                                             PS[TB][0:P, 0:nt * F].rearrange("p (t f) -> p t f", t=nt),
                                             ACT.Copy, scale=S0).then_inc(s_hi, 1)
                    if 1 <= c <= NC:
                        act.wait_ge(s_t2, q)
                        nc.scalar.activation(nS[:, 0:w], rS[:, 0:w], ACT.Tanh, bias=bias[:, B_IN:B_IN + 1]
                                             ).then_inc(s_n, 1)
                    if l == L - 1 and c == NC - 1:
                        second_input(1)
                    if l == L - 1 and c >= 2:
                        n0, w = CH[c - 2][0] * P, CH[c - 2][1] * P
                        act.wait_ge(s_d1, c - 1)
                        nc.scalar.activation(HT[:, n0:n0 + w], PS[TB][:, 0:w], ACT.Relu, bias=bias[:, B_D1:B_D1 + 1]
                                             ).then_inc(s_d1s, 1)
                    if l == L - 1 and c >= 3:
                        decode_sig(c - 3)
                    if l == L - 1 and c >= NC:
                        second_input(3 + c - NC)
            decode_sig(NC - 1)
            for c in range(5, NC):
                second_input(c)
            for c, (t0, nt) in enumerate(CH):
                act.wait_ge(s_dB, c + 1)
                nc.scalar.activation(dinvB[:, t0 * P:(t0 + nt) * P], PS[RB + c % 2][:, 0:nt * P], ACT.Copy
                                     ).then_inc(s_dBs, 1)
            for c in range(1, NC + 2):
                if c <= NC:
                    w = CH[c - 1][1] * P
                    for k in range(HID // F):
                        act.wait_ge(s_1g, 2 * (c - 1) + k + 1)
                        if c >= 2:
                            act.wait_ge(s_1p, c - 1)
                        nc.scalar.activation((rS, zS)[k][:, 0:w], PS[RB + k][:, 0:w], ACT.Relu,
                                             bias=bias[:, B_L1 + k:B_L1 + k + 1]).then_inc(s_1h, 1)
                if c >= 1 and c <= NC:
                    t0, nt = CH[c - 1]
                    act.wait_ge(s_1p, c)
                    for j in range(nt):
                        last = nc.scalar.activation(Z16[:, t0 + j, 0, :], PS[IB][0:P, j * F:j * F + F], ACT.Copy,
                                                    scale=dinvs[0:P, t0 + j:t0 + j + 1])
                    last.then_inc(s_1hi, 1)
            for c in range(NC):
                w = CH[c][1] * P
                act.wait_ge(s_2S, c + 1)
                if c >= 1:
                    act.wait_ge(s_2t, c)
                nc.scalar.activation(aggS[:, 0:w], PS[AGG[c % 2]][:, 0:w], ACT.Copy, scale=1.0 / S0
                                     ).then_inc(s_2a, 1)
            act.wait_ge(s_flag, 1)
            with act.If(act.value_load(flag[0:1, 0:1], min_val=0, max_val=1000) > 0):
                general_scalar(act)


_IN = ['x', 'src', 'dst', 'enc_w1T', 'enc_b1', 'enc_w2T', 'enc_b2', 'conv_wT', 'gru_wihT', 'gru_whhT',
       'gru_bih', 'gru_bhh', 'dec_w1T', 'dec_b1', 'dec_w2T', 'dec_b2', 'l1_w1T', 'l1_b1', 'l1_w2T', 'l1_b2']


def layout(inputs):
    import numpy as np
    a = {k: np.asarray(v) for k, v in inputs.items()}
    g = lambda n: a['L0_gnn_' + n]
    f = lambda n: a['L1_gnn_' + n]
    c = np.ascontiguousarray
    H = g('gru_whh').shape[1]
    return {
        'x': c(a['x']), 'src': c(a['src']), 'dst': c(a['dst']),
        'enc_w1T': c(g('enc_w1').T), 'enc_b1': c(g('enc_b1').reshape(-1, 1)),
        'enc_w2T': c(g('enc_w2').T), 'enc_b2': c(g('enc_b2').reshape(-1, 1)),
        'conv_wT': c(g('conv_w').transpose(0, 2, 1)),
        'gru_wihT': c(g('gru_wih').T), 'gru_whhT': c(g('gru_whh').T),
        'gru_bih': c(g('gru_bih').reshape(3, H).T), 'gru_bhh': c(g('gru_bhh').reshape(3, H).T),
        'dec_w1T': c(g('dec_w1').T), 'dec_b1': c(g('dec_b1').reshape(-1, 1)),
        'dec_w2T': c(g('dec_w2').T), 'dec_b2': c(g('dec_b2').reshape(1, -1)),
        'l1_w1T': c(f('W1').T), 'l1_b1': c(f('b1').reshape(2, -1).T),
        'l1_w2T': c(f('W2').T.reshape(2, H, -1).transpose(1, 0, 2)), 'l1_b2': c(f('b2').reshape(1, -1)),
    }


def kernel(**inputs):
    import numpy as np
    import concourse.bacc as bacc
    from concourse.bass_utils import run_bass_kernel_spmd

    nc = bacc.Bacc("TRN2", target_bir_lowering=False, num_devices=1)
    arrays = layout(inputs)
    args = [nc.dram_tensor(f"in_{n}", arrays[n].shape, mybir.dt.from_np(arrays[n].dtype),
                           kind="ExternalInput").ap() for n in _IN]
    out = nc.dram_tensor("out", inputs['x'].shape, mybir.dt.float32, kind="ExternalOutput").ap()
    gnn_kernel(nc, *args, out)
    r = run_bass_kernel_spmd(nc, [{f"in_{n}": arrays[n] for n in _IN}], core_ids=[0])
    return np.asarray(r.results[0]["out"])
```

```python
import concourse.bass as bass
from concourse import mybir
from contextlib import ExitStack


def gnn_kernel(nc, x, src, dst, enc_w1T, enc_b1, enc_w2T, enc_b2, conv_wT, gru_wihT, gru_whhT,
               gru_bih, gru_bhh, dec_w1T, dec_b1, dec_w2T, dec_b2, l1_w1T, l1_b1, l1_w2T, l1_b2, out):
    F32, F16, BF16, I32 = mybir.dt.float32, mybir.dt.float16, mybir.dt.bfloat16, mybir.dt.int32
    FP8 = mybir.dt.float8e3
    ALU, ACT, AX = mybir.AluOpType, mybir.ActivationFunctionType, mybir.AxisListType

    N, F = x.shape
    E = src.shape[0]
    L = conv_wT.shape[0]
    G = 3 * F
    HID = l1_w1T.shape[1]
    P = 125
    T = N // P
    assert T * P == N
    W = 4
    KW = 7
    PW = 112
    assert KW * PW * W >= N
    DP = (N + W - 1) // W * W
    NW = DP // W
    RL = 17
    NR = E // RL
    assert NR * RL == E
    SL = 128
    TR = (E - SL) // RL + 2
    NS = NR // P
    assert NS * P == NR
    J = 14
    GW = [5, 5, 4]
    NBT = KW * PW // J
    BL = 4
    BANKS = 3
    assert sum(GW) == J and PW % J == 0 and NBT % BL == 0 and BL * len(GW) % BANKS == 0
    TOP = 4096.0
    assert TOP > KW * PW * W
    LIMIT = 1000.0
    MAGIC = 12582912.0
    TC = 4
    CH = [(t, min(TC, T - t)) for t in range(0, T, TC)]
    NC = len(CH)
    NORMS = [(0, 4), (4, NC)]
    S0 = 64.0
    S1 = 1024.0

    src_t, dst_t = src.tensor, dst.tensor
    table = nc.dram_tensor("edge_table", (TR, 2 * SL), I32, kind="Internal").ap()
    comb_dram = nc.dram_tensor("comb_scratch", (L, F, G), F32, kind="Internal").ap()

    ctx = ExitStack()
    with ctx:
        def sb(name, shape, dt):
            return ctx.enter_context(nc.sbuf_tensor(name, shape, dt))

        def sem(name):
            return ctx.enter_context(nc.semaphore(name))

        def carve(region, at, shape, dt):
            size = {F32: 4, I32: 4, F16: 2, BF16: 2}[dt]
            n = size
            for s in shape[1:]:
                n *= s
            v = region[0:shape[0], at:at + n].bitcast(dt)
            if len(shape) == 3:
                v = v.rearrange("p (a b) -> p a b", a=shape[1])
            if len(shape) == 4:
                v = v.rearrange("p (a b c) -> p a b c", a=shape[1], b=shape[2])
            return v

        AT = sb("AT", [128, T * DP], FP8)
        CT = sb("CT", [128, T * N + 3], FP8)
        HT = sb("HT", [128, N], F32)
        H16 = sb("H16", [128, 2, T, 2, F], F16)
        AT3 = AT[:, :].rearrange("p (t d) -> p t d", t=T)
        CT3 = CT[:, 0:T * N].rearrange("p (t s) -> p t s", t=T)
        ident = sb("ident", [128, 128], F32)
        ident16 = sb("ident16", [128, 128], F16)
        comb = sb("comb", [128, 2, G], F32)
        whh = sb("whh", [128, G], F32)
        aggS = sb("aggS", [128, TC * P], F32)
        rS = sb("rS", [128, TC * P], F32)
        zS = sb("zS", [128, TC * P], F32)
        nS = sb("nS", [128, TC * P], F32)
        bias = sb("bias", [128, 16], F32)
        dec1 = sb("dec1", [128, F], F32)
        dec2 = sb("dec2", [128, F], F32)
        dec2b = sb("dec2b", [128, F], F32)
        yS = sb("yS", [128, TC * F], F32)
        deg = sb("deg", [128, T], F32)
        dinv = sb("dinv", [128, T], F32)
        dinvs = sb("dinvs", [128, T], F32)
        stat = sb("stat", [128, TC, 6], F32)
        mv = sb("mv", [128, T, 2], F32)
        lnsc = sb("lnsc", [128, T], F32)
        chk = sb("chk", [128, 4], F32)
        flag_f = sb("flag_f", [1, 4], F32)
        flag = sb("flag", [1, 1], I32)
        mhalf = sb("mhalf", [128, T], F32)
        lnb = sb("lnb", [128, T], F32)
        X32 = H16[:, 1, :, :, :].rearrange("p t h f -> p (t h f)").bitcast(F32).rearrange("p (t f) -> p t f", t=T)
        (B_R, B_Z, B_HN, B_IN, B_E1, B_E2, B_D1, B_L1) = range(8)

        PS = [ctx.enter_context(nc.psum_tensor(f"PS{i}", [128, 512], F32)) for i in range(8)]

        o = [0]

        def early(shape, dt):
            size = {F32: 4, I32: 4, F16: 2, BF16: 2}[dt]
            n = size
            for s in shape[1:]:
                n *= s
            v = carve(CT, o[0], shape, dt)
            o[0] += (n + 31) // 32 * 32
            return v

        samp_i = early([P, NS, RL], I32)
        samp = early([P, NS], F32)
        row_len = early([P, 1], F32)
        wtop = early([P, KW * PW], F32)
        full = early([P, KW * PW], F32)
        part = early([P, KW * PW], F32)
        wtop_p = early([PW, KW], F32)
        inrow = early([PW, KW, NS], F32)
        wstart1 = early([PW, KW], F32)
        cnt = early([PW, KW], F32)
        idx = early([PW, KW], I32)
        Gt = early([PW, KW, 2 * SL], I32)
        tf = early([PW, KW, SL], F32)
        pf = early([PW, KW, SL], F32)
        kf = early([PW, KW, SL], F32)
        pT = early([SL, KW * PW], BF16)
        kT = early([SL, KW * PW], BF16)
        iotaP = early([SL, P, J], BF16)
        iotaK = early([SL, W * T, J], BF16)
        ohP = early([SL, BL, P * J], BF16).rearrange("p k (n j) -> p k n j", j=J)
        ohK = early([SL, BL, W * T * J], BF16).rearrange("p k (n j) -> p k n j", j=J)
        enc1 = early([128, F], F32)
        enc2 = early([128, F], F32)
        convT = early([128, L, F], F32)
        wih = early([128, G], F32)
        combS = early([128, L, G], F32)
        assert o[0] <= T * N, o[0]

        p2 = [0]

        def late(shape, dt):
            size = {F32: 4, I32: 4, F16: 2, BF16: 2}[dt]
            n = size
            for d in shape[1:]:
                n *= d
            v = carve(AT, p2[0], shape, dt)
            p2[0] += (n + 31) // 32 * 32
            return v

        w1 = late([128, HID], F32)
        w2 = late([128, HID // F, F], F32)
        l1b2 = late([128, F], F32)
        onesL = late([128, 128], F32)
        dinvB = late([128, N], F32)
        U32 = late([P, T, F], F32)
        OUT = late([P, T, F], F32)
        V16 = H16[:, 0, :, :, :]
        Z16 = late([P, T, 2 * F], F16).rearrange("p t (h f) -> p t h f", h=2)
        assert p2[0] <= T * DP

        gp = [0, 0]

        def spare(r, shape, dt):
            n = 2 if dt == F16 else 4
            for d in shape[1:]:
                n *= d
            v = carve((AT, CT)[r], gp[r], shape, dt)
            gp[r] += (n + 31) // 32 * 32
            return v

        gH, gA, gB, gD, gH1, gH2 = [spare(0, [128, N], F32) for _ in range(6)]
        gX, gU = [spare(1, [P, T, F], F32) for _ in range(2)]
        EC = E // T
        ebuf = spare(1, [1, 2, EC], I32)
        genc1, genc2 = [spare(1, [128, F], F32) for _ in range(2)]
        gcw = spare(1, [128, G], F32)
        gw1 = spare(1, [128, HID], F32)
        gw2 = spare(1, [128, HID // F, F], F32)
        gb2 = spare(1, [128, 1], F32)
        assert gp[0] <= T * DP and gp[1] <= T * N

        AGG, RB, ZB, NB, IB, TB, CB = (0, 1), 2, 3, 4, 5, 6, 7
        NBLK = T * T
        NCG = (NBLK + 3) // 4
        AHEAD = 4
        ENC = 4 * (NC + 1)
        COMB = [ENC + 2 * l for l in range(L)]
        PART = {4 * g + 10: (0, g) for g in range(NC - 1)}
        PART.update({ENC + n: cg for n, cg in enumerate(
            [(1, 0), (1, 1), (0, NC - 1)] + [(1, g) for g in range(2, NC)]
            + [(c, g) for c in range(2, AHEAD) for g in range(NC)])})
        assert max(PART) < NBT and len(PART) == AHEAD * NC
        EA, EC1, EC2, EB = 1, 6, 7, 0
        WBANK = (RB, ZB, NB)
        agg_bank = lambda q: PS[(IB, TB, CB)[q] if q < AHEAD - 1 else AGG[q % 2]]
        CPS = 8
        SPOT = [11, 14, 16, 19, 21, 24]
        CHOST = [q for q in range(AHEAD, L * NC) if 0 < q % NC < NC - 1]
        cgroups = lambda q: ([m for m in range(CPS * CHOST.index(q), CPS * CHOST.index(q) + CPS) if m < NCG]
                             if q in CHOST else [])

        table_loaded = sem("table_loaded"); samples_loaded = sem("samples_loaded")
        row_len_set = sem("row_len_set"); window_starts = sem("window_starts")
        compares_ready = sem("compares_ready"); samples_counted = sem("samples_counted")
        rows_found = sem("rows_found")
        rows_gathered = [sem(f"rows_gathered{k}") for k in range(KW)]
        keys_ready = sem("keys_ready"); keys_transposed = sem("keys_transposed")
        keys_copied = sem("keys_copied"); onehot_iotas = sem("onehot_iotas")
        onehots_ready = sem("onehots_ready"); windows_counted = sem("windows_counted")
        window_bank_free = sem("window_bank_free")
        ident_set = sem("ident_set"); ident16_set = sem("ident16_set"); gate_biases = sem("gate_biases")
        mhalf_set = sem("mhalf_set"); weights_loaded = sem("weights_loaded")
        weights2_loaded = sem("weights2_loaded"); x_loaded = sem("x_loaded"); x_reloaded = sem("x_reloaded")
        late_ones_set = sem("late_ones_set")
        variances_ready = sem("variances_ready"); roots_ready = sem("roots_ready")
        tile_normalized = sem("tile_normalized"); scales2_ready = sem("scales2_ready")
        x_transposed = sem("x_transposed"); x_copied = sem("x_copied"); enc1_product = sem("enc1_product")
        enc1_relu = sem("enc1_relu"); enc2_product = sem("enc2_product"); state_encoded = sem("state_encoded")
        encoded_transposed = sem("encoded_transposed"); encoded_copied = sem("encoded_copied")
        encoded_hi = sem("encoded_hi"); encoded_lo = sem("encoded_lo")
        comb_product = sem("comb_product"); comb_copied = sem("comb_copied"); comb_stored = sem("comb_stored")
        comb_loaded = [sem("comb_loaded0"), sem("comb_loaded1")]
        sum_ready = sem("sum_ready"); sum_copied = sem("sum_copied"); hidden_product = sem("hidden_product")
        reset_product = sem("reset_product"); update_product = sem("update_product")
        input_product = sem("input_product"); reset_gate = sem("reset_gate"); update_gate = sem("update_gate")
        new_gate = sem("new_gate"); reset_hidden = sem("reset_hidden"); new_input = sem("new_input")
        state_ready = sem("state_ready"); state_transposed = sem("state_transposed"); state_hi = sem("state_hi")
        state_lo = sem("state_lo")
        blocks_ready = sem("blocks_ready"); degree_summed = sem("degree_summed")
        blocks_copied = [sem("blocks_copied_vector"), sem("blocks_copied_scalar")]
        dec1_product = sem("dec1_product"); dec1_relu = sem("dec1_relu"); dec2_product = sem("dec2_product")
        dec2_biased = sem("dec2_biased"); sigmoid_ready = sem("sigmoid_ready")
        input2_ready = sem("input2_ready"); input2_hi = sem("input2_hi"); input2_lo = sem("input2_lo")
        scales_product = sem("scales_product"); scales_copied = sem("scales_copied")
        sum1_ready = sem("sum1_ready"); sum1_scaled = sem("sum1_scaled"); expand_product = sem("expand_product")
        expand_relu = sem("expand_relu"); project_product = sem("project_product")
        projected_hi = sem("projected_hi"); projected_lo = sem("projected_lo"); sum2_ready = sem("sum2_ready")
        sum2_copied = sem("sum2_copied"); sum2_transposed = sem("sum2_transposed")
        output_ready = sem("output_ready")
        check_ready = sem("check_ready"); check_summed = sem("check_summed"); flag_ready = sem("flag_ready")
        output_stored = sem("output_stored")
        vector_chain = sem("vector_chain"); general_chain = sem("general_chain")
        general_tick = sem("general_tick")
        gx_loaded = sem("gx_loaded"); gweights_loaded = sem("gweights_loaded")
        gvariances_ready = sem("gvariances_ready"); groots_ready = sem("groots_ready")
        gnorm_ready = sem("gnorm_ready"); gtile_normalized = sem("gtile_normalized")
        gnormal_transposed = sem("gnormal_transposed"); gnormal_copied = sem("gnormal_copied")
        genc1_product = sem("genc1_product"); genc1_relu = sem("genc1_relu")
        genc2_product = sem("genc2_product"); gstate_encoded = sem("gstate_encoded")
        glayer_weights = sem("glayer_weights"); gedges_loaded = sem("gedges_loaded")
        gedges_used = sem("gedges_used"); gedge_added = sem("gedge_added"); gsum_ready = sem("gsum_ready")
        ggate_products = sem("ggate_products"); greset_update = sem("greset_update")
        gnew_input = sem("gnew_input"); gnew_gate = sem("gnew_gate"); gstate_ready = sem("gstate_ready")
        gstate_relu = sem("gstate_relu"); gdec1_product = sem("gdec1_product"); gdec1_relu = sem("gdec1_relu")
        gdec2_product = sem("gdec2_product"); gdec2_biased = sem("gdec2_biased")
        gsigmoid_ready = sem("gsigmoid_ready"); ginput2_ready = sem("ginput2_ready"); gdegrees = sem("gdegrees")
        gdegree_roots = sem("gdegree_roots"); gsum1_ready = sem("gsum1_ready")
        gexpand_product = sem("gexpand_product"); gexpand_relu = sem("gexpand_relu")
        gproject_product = sem("gproject_product"); gproject_copied = sem("gproject_copied")
        gsum2_ready = sem("gsum2_ready"); gsum2_transposed = sem("gsum2_transposed")
        goutput_ready = sem("goutput_ready"); goutput_stored = sem("goutput_stored")

        block = ctx.enter_context(nc.Block())

        def evac_block_group(eng, m):
            b0, nb = 4 * m, min(4, NBLK - 4 * m)
            eng.wait_ge(blocks_ready, m + 1)
            if 4 * m + nb > T * (T - 1):
                eng.wait_ge(degree_summed, T)
            if m < 2:
                eng.wait_ge(comb_stored, 16)
            o_, i_ = CT[0:P, b0 * P:(b0 + nb) * P], PS[CB][0:P, 0:nb * P]
            if m % 2 == 0:
                nc.vector.tensor_copy(o_, i_, saturate=False).then_inc(blocks_copied[0], 1)
            else:
                nc.scalar.activation(o_, i_, ACT.Copy, saturate=False).then_inc(blocks_copied[1], 1)

        def general_vector(dve):
            n = [0]

            def link(ins):
                n[0] += 1
                ins.then_inc(general_chain, 1)
                dve.wait_ge(general_chain, n[0])

            def norm(k):
                for t in range(T):
                    link(nc.vector.bn_stats(stat[0:P, 0, :], gX[:, t, :]))
                    link(nc.vector.bn_aggr(mv[0:P, t, :], stat[0:P, 0, :]))
                nc.vector.tensor_scalar(mv[0:P, :, 1], mv[0:P, :, 1], 1e-5, None, ALU.add).then_inc(gvariances_ready, 1)
                dve.wait_ge(groots_ready, k + 1)
                nc.vector.scalar_tensor_tensor(lnb[0:P, :], mv[0:P, :, 0], -1.0, lnsc[0:P, :], ALU.mult, ALU.mult
                                               ).then_inc(gnorm_ready, 1)

            def edges(first, to, frm, fi, ti):
                with dve.Fori(0, T) as k:
                    dve.wait_ge(gedges_loaded, (first + k + 1) * 32)
                    dve.sem_inc(general_tick, 1)
                    with dve.Fori(0, EC) as i:
                        a = dve.value_load(ebuf[0:1, ti, bass.ds(i, 1)], min_val=0, max_val=N - 1)
                        if frm is None:
                            ins = nc.vector.tensor_scalar(to[:, bass.ds(a, 1)], to[:, bass.ds(a, 1)], 1.0, None, ALU.add)
                        else:
                            b = dve.value_load(ebuf[0:1, fi, bass.ds(i, 1)], min_val=0, max_val=N - 1)
                            ins = nc.vector.tensor_tensor(to[:, bass.ds(a, 1)], to[:, bass.ds(a, 1)],
                                                          frm[:, bass.ds(b, 1)], ALU.add)
                        ins.then_inc(gedge_added, 1)
                        dve.wait_ge(gedge_added, i + 1)
                    dve.sem_clear(gedge_added)
                    dve.sem_inc(gedges_used, 1)

            dve.sem_inc(gedges_used, 1)
            dve.wait_ge(gx_loaded, 16)
            norm(0)
            dve.wait_ge(gstate_encoded, NC)
            with dve.Fori(0, L) as l:
                nc.vector.memset(gA, 0.0).then_inc(gsum_ready, 1)
                dve.wait_ge(gsum_ready, l * 2 + 1)
                dve.sem_inc(general_tick, 1)
                edges(l * T, gA, gH, 0, 1)
                dve.sem_inc(gsum_ready, 1)
                for c, (t0, nt) in enumerate(CH):
                    w = nt * P
                    H = gH[:, t0 * P:t0 * P + w]
                    dve.wait_ge(greset_update, l * NC + (c + 1))
                    nc.vector.scalar_tensor_tensor(rS[:, 0:w], PS[NB][:, 0:w], bias[:, B_HN:B_HN + 1], rS[:, 0:w],
                                                   ALU.add, ALU.mult).then_inc(gnew_input, 1)
                    dve.wait_ge(gnew_input, l * (2 * NC) + (2 * c + 1))
                    nc.vector.tensor_tensor(rS[:, 0:w], PS[IB][:, 0:w], rS[:, 0:w], ALU.add).then_inc(gnew_input, 1)
                    dve.wait_ge(gnew_gate, l * (3 * NC) + (3 * c + 1))
                    nc.vector.tensor_tensor(H, H, nS[:, 0:w], ALU.subtract).then_inc(gnew_gate, 1)
                    dve.wait_ge(gnew_gate, l * (3 * NC) + (3 * c + 2))
                    nc.vector.tensor_tensor(H, H, zS[:, 0:w], ALU.mult).then_inc(gnew_gate, 1)
                    dve.wait_ge(gnew_gate, l * (3 * NC) + (3 * c + 3))
                    nc.vector.tensor_tensor(H, H, nS[:, 0:w], ALU.add).then_inc(gstate_ready, 1)
            dve.wait_ge(gstate_ready, L * NC)
            nc.vector.tensor_scalar(gH, gH, 0.0, None, ALU.max).then_inc(gstate_relu, 1)
            for c, (t0, nt) in enumerate(CH):
                y = yS[0:P, 0:nt * F].rearrange("p (t f) -> p t f", t=nt)
                dve.wait_ge(gdec2_product, c + 1)
                nc.vector.tensor_tensor(y, PS[CB][0:P, 0:nt * F].rearrange("p (t f) -> p t f", t=nt),
                                        dec2b[0:P, :].unsqueeze(1).to_broadcast([P, nt, F]), ALU.add).then_inc(gdec2_biased, 1)
                dve.wait_ge(gsigmoid_ready, c + 1)
                nc.vector.tensor_tensor(gX[:, t0:t0 + nt, :], gX[:, t0:t0 + nt, :], y, ALU.add).then_inc(ginput2_ready, 1)
                dve.wait_ge(ginput2_ready, c + 1)
            norm(1)
            link(nc.vector.memset(gD, 1.0))
            edges(L * T, gD, None, 0, 0)
            dve.sem_inc(gdegrees, 1)
            dve.wait_ge(gnormal_copied, 2 * NC)
            dve.wait_ge(gdegree_roots, 1)
            link(nc.vector.tensor_tensor(gB, gB, gD, ALU.mult))
            link(nc.vector.tensor_copy(gA, gB))
            edges((L + 1) * T, gA, gB, 1, 0)
            nc.vector.tensor_tensor(gA, gA, gD, ALU.mult).then_inc(gsum1_ready, 1)
            for c, (t0, nt) in enumerate(CH):
                cs = slice(t0 * P, (t0 + nt) * P)
                dve.wait_ge(gproject_product, c + 1)
                nc.vector.tensor_tensor(gB[:, cs], PS[NB][:, 0:nt * P], gD[:, cs], ALU.mult).then_inc(gproject_copied, 1)
            dve.wait_ge(gproject_copied, NC)
            link(nc.vector.tensor_copy(gA, gB))
            edges((L + 2) * T, gA, gB, 1, 0)
            dve.wait_ge(gweights_loaded, 16 * 5)
            link(nc.vector.tensor_tensor(gA, gA, gD, ALU.mult))
            nc.vector.tensor_scalar(gA, gA, gb2[:, 0:1], None, ALU.add).then_inc(gsum2_ready, 1)
            for c, (t0, nt) in enumerate(CH):
                dve.wait_ge(gsum2_transposed, c + 1)
                nc.vector.tensor_tensor(gX[:, t0:t0 + nt, :], gX[:, t0:t0 + nt, :],
                                        PS[TB][0:P, 0:nt * F].rearrange("p (t f) -> p t f", t=nt), ALU.add
                                        ).then_inc(goutput_ready, 1)

        def general_tensor(pe):
            def to_features(k):
                for c, (t0, nt) in enumerate(CH):
                    pe.wait_ge(gtile_normalized, k * T + t0 + nt)
                    if k * NC + c >= 1:
                        pe.wait_ge(gnormal_copied, k * NC + c)
                    for j in range(nt):
                        last = nc.tensor.transpose(PS[TB][:, j * P:(j + 1) * P], gU[:, t0 + j, :], ident[0:P, 0:P])
                    last.then_inc(gnormal_transposed, 1)

            to_features(0)
            pe.wait_ge(gweights_loaded, 16 * 5)
            for c, (t0, nt) in enumerate(CH):
                cs = slice(t0 * P, (t0 + nt) * P)
                pe.wait_ge(gnormal_copied, c + 1)
                nc.tensor.matmul(PS[RB][:, 0:nt * P], genc1, gB[:, cs], start=True, stop=True).then_inc(genc1_product, 1)
                pe.wait_ge(genc1_relu, c + 1)
                nc.tensor.matmul(PS[ZB][:, 0:nt * P], genc2, gA[:, cs], start=True, stop=True).then_inc(genc2_product, 1)
                pe.wait_ge(gstate_encoded, c + 1)
            with pe.Fori(0, L) as l:
                pe.wait_ge(glayer_weights, l * 16 + 16)
                pe.wait_ge(gsum_ready, l * 2 + 2)
                for c, (t0, nt) in enumerate(CH):
                    w = nt * P
                    H, A = gH[:, t0 * P:t0 * P + w], gA[:, t0 * P:t0 * P + w]
                    if c >= 1:
                        pe.wait_ge(gstate_ready, l * NC + c)
                    for k, b in enumerate((RB, ZB)):
                        nc.tensor.matmul(PS[b][:, 0:w], whh[:, k * F:(k + 1) * F], H, start=True, stop=False)
                        nc.tensor.matmul(PS[b][:, 0:w], gcw[:, k * F:(k + 1) * F], A, start=False, stop=True)
                    nc.tensor.matmul(PS[NB][:, 0:w], whh[:, 2 * F:G], H, start=True, stop=True)
                    nc.tensor.matmul(PS[IB][:, 0:w], gcw[:, 2 * F:G], A, start=True, stop=True).then_inc(ggate_products, 1)
            pe.wait_ge(gstate_relu, 1)
            for c, (t0, nt) in enumerate(CH):
                cs = slice(t0 * P, (t0 + nt) * P)
                if c >= 1:
                    pe.wait_ge(gdec2_biased, c)
                nc.tensor.matmul(PS[RB][:, 0:nt * P], dec1[:, :], gH[:, cs], start=True, stop=True).then_inc(gdec1_product, 1)
                pe.wait_ge(gdec1_relu, c + 1)
                for j in range(nt):
                    last = nc.tensor.matmul(PS[CB][0:P, j * F:(j + 1) * F], gB[:, (t0 + j) * P:(t0 + j + 1) * P],
                                            dec2[:, :], start=True, stop=True)
                last.then_inc(gdec2_product, 1)
            to_features(1)
            pe.wait_ge(gsum1_ready, 1)
            for c, (t0, nt) in enumerate(CH):
                cs = slice(t0 * P, (t0 + nt) * P)
                if c >= 1:
                    pe.wait_ge(gproject_copied, c)
                for k in range(HID // F):
                    last = nc.tensor.matmul(PS[RB + k][:, 0:nt * P], gw1[:, k * F:(k + 1) * F], gA[:, cs],
                                            start=True, stop=True)
                last.then_inc(gexpand_product, 1)
                pe.wait_ge(gexpand_relu, 2 * (c + 1))
                for k in range(HID // F):
                    last = nc.tensor.matmul(PS[NB][:, 0:nt * P], gw2[:, k, :], (gH1, gH2)[k][:, cs],
                                            start=(k == 0), stop=(k == 1))
                last.then_inc(gproject_product, 1)
            pe.wait_ge(gsum2_ready, 1)
            for c, (t0, nt) in enumerate(CH):
                if c >= 1:
                    pe.wait_ge(goutput_ready, c)
                for j in range(nt):
                    last = nc.tensor.transpose(PS[TB][0:P, j * F:(j + 1) * F], gA[:, (t0 + j) * P:(t0 + j + 1) * P],
                                               ident[:, :])
                last.then_inc(gsum2_transposed, 1)

        def general_scalar(act):
            def normalized(k):
                act.wait_ge(gnorm_ready, k + 1)
                if k:
                    act.wait_ge(gnormal_transposed, NC)
                for t in range(T):
                    nc.scalar.activation(gU[:, t, :], gX[:, t, :], ACT.Relu, bias=lnb[0:P, t:t + 1],
                                         scale=lnsc[0:P, t:t + 1]).then_inc(gtile_normalized, 1)
                for c, (t0, nt) in enumerate(CH):
                    act.wait_ge(gnormal_transposed, k * NC + c + 1)
                    nc.scalar.activation(gB[:, t0 * P:(t0 + nt) * P], PS[TB][:, 0:nt * P], ACT.Copy).then_inc(gnormal_copied, 1)

            normalized(0)
            for c, (t0, nt) in enumerate(CH):
                cs = slice(t0 * P, (t0 + nt) * P)
                act.wait_ge(genc1_product, c + 1)
                nc.scalar.activation(gA[:, cs], PS[RB][:, 0:nt * P], ACT.Relu, bias=bias[:, B_E1:B_E1 + 1]
                                     ).then_inc(genc1_relu, 1)
                act.wait_ge(genc2_product, c + 1)
                nc.scalar.activation(gH[:, cs], PS[ZB][:, 0:nt * P], ACT.Identity, bias=bias[:, B_E2:B_E2 + 1]
                                     ).then_inc(gstate_encoded, 1)
            with act.Fori(0, L) as l:
                for c, (t0, nt) in enumerate(CH):
                    w = nt * P
                    act.wait_ge(ggate_products, l * NC + (c + 1))
                    nc.scalar.activation(rS[:, 0:w], PS[RB][:, 0:w], ACT.Sigmoid, bias=bias[:, B_R:B_R + 1])
                    nc.scalar.activation(zS[:, 0:w], PS[ZB][:, 0:w], ACT.Sigmoid, bias=bias[:, B_Z:B_Z + 1]
                                         ).then_inc(greset_update, 1)
                    act.wait_ge(gnew_input, l * (2 * NC) + (2 * c + 2))
                    nc.scalar.activation(nS[:, 0:w], rS[:, 0:w], ACT.Tanh, bias=bias[:, B_IN:B_IN + 1]).then_inc(gnew_gate, 1)
                    act.wait_ge(gstate_ready, l * NC + (c + 1))
            for c, (t0, nt) in enumerate(CH):
                act.wait_ge(gdec1_product, c + 1)
                nc.scalar.activation(gB[:, t0 * P:(t0 + nt) * P], PS[RB][:, 0:nt * P], ACT.Relu,
                                     bias=bias[:, B_D1:B_D1 + 1]).then_inc(gdec1_relu, 1)
                act.wait_ge(gdec2_biased, c + 1)
                nc.scalar.activation(yS[0:P, 0:nt * F], yS[0:P, 0:nt * F], ACT.Sigmoid).then_inc(gsigmoid_ready, 1)
                act.wait_ge(ginput2_ready, c + 1)
            normalized(1)
            for c, (t0, nt) in enumerate(CH):
                act.wait_ge(gexpand_product, c + 1)
                for k in range(HID // F):
                    nc.scalar.activation((gH1, gH2)[k][:, t0 * P:(t0 + nt) * P], PS[RB + k][:, 0:nt * P], ACT.Relu,
                                         bias=bias[:, B_L1 + k:B_L1 + k + 1]).then_inc(gexpand_relu, 1)

        @block.sync
        def _(sp):
            sp.dma_start(samp_i, dst.rearrange("(p a b) -> p a b", p=P, a=NS)).then_inc(samples_loaded, 16)
            for h, t in enumerate((src_t, dst_t)):
                sp.dma_start(table[0:TR - 1, h * SL:(h + 1) * SL], bass.AP(t, 0, [[RL, TR - 1], [1, SL]])
                             ).then_inc(table_loaded, 16)
                sp.dma_start(table[TR - 1:TR, h * SL:(h + 1) * SL], bass.AP(t, E - SL, [[SL, 1], [1, SL]])
                             ).then_inc(table_loaded, 16)
            sp.dma_start(X32[0:P], x.rearrange("(t p) f -> p t f", p=P)).then_inc(x_loaded, 16)
            for d, v in ((enc1, enc_w1T), (enc2, enc_w2T), (convT, conv_wT.rearrange("l k m -> k l m")),
                         (wih, gru_wihT), (whh[:, :], gru_whhT),
                         (bias[:, 4:5], enc_b1), (bias[:, 5:6], enc_b2), (bias[:, 6:7], dec_b1),
                         (bias[:, 7:9], l1_b1), (bias[:, 9:12], gru_bih), (bias[:, 12:15], gru_bhh),
                         (dec1[:, :], dec_w1T), (dec2[:, :], dec_w2T), (dec2b[:, :], dec_b2.to_broadcast([128, F]))):
                sp.dma_start(d, v).then_inc(weights_loaded, 16)
            sp.wait_ge(comb_copied, L)
            sp.dma_start(comb_dram.rearrange("l k m -> k l m"), combS).then_inc(comb_stored, 16)
            sp.wait_ge(comb_stored, 16)
            for l in range(L):
                if l >= 2:
                    sp.wait_ge(input_product, (l - 1) * NC)
                sp.dma_start(comb[:, l % 2, :], comb_dram[l, :, :]).then_inc(comb_loaded[l % 2], 16)
            sp.wait_ge(sum_ready, (L - 1) * NC)
            sp.dma_start(X32[0:P], x.rearrange("(t p) f -> p t f", p=P)).then_inc(x_reloaded, 16)
            sp.wait_ge(sum_ready, L * NC)
            sp.dma_start(w1, l1_w1T).then_inc(weights2_loaded, 16)
            sp.dma_start(w2, l1_w2T).then_inc(weights2_loaded, 16)
            sp.dma_start(l1b2, l1_b2.to_broadcast([128, F])).then_inc(weights2_loaded, 16)
            for c, (t0, nt) in enumerate(CH):
                sp.wait_ge(output_ready, c + 1)
                sp.dma_start(out.rearrange("(t p) f -> p t f", p=P)[:, t0:t0 + nt, :],
                             OUT[:, t0:t0 + nt, :]).then_inc(output_stored, 16)
            sp.wait_ge(output_stored, 16 * NC)
            sp.wait_ge(flag_ready, 1)
            with sp.If(sp.value_load(flag[0:1, 0:1], min_val=0, max_val=1000) > 0):
                sp.dma_start(gX, x.rearrange("(t p) f -> p t f", p=P)).then_inc(gx_loaded, 16)
                for d, v in ((genc1, enc_w1T), (genc2, enc_w2T), (gw1, l1_w1T), (gw2, l1_w2T),
                             (gb2, l1_b2.rearrange("a f -> f a"))):
                    sp.dma_start(d, v).then_inc(gweights_loaded, 16)

                def edge_loads(first):
                    with sp.Fori(0, T) as k:
                        sp.wait_ge(gedges_used, first + k + 1)
                        sp.dma_start(ebuf[:, 0, :], src.rearrange("(k e) -> k e", e=EC)[bass.ds(k, 1), :]
                                     ).then_inc(gedges_loaded, 16)
                        sp.dma_start(ebuf[:, 1, :], dst.rearrange("(k e) -> k e", e=EC)[bass.ds(k, 1), :]
                                     ).then_inc(gedges_loaded, 16)

                with sp.Fori(0, L) as l:
                    sp.wait_ge(gstate_encoded, NC)
                    sp.wait_ge(gstate_ready, l * NC)
                    sp.dma_start(gcw.unsqueeze(1), comb_dram[bass.ds(l, 1), :, :].rearrange("a k m -> k a m")
                                 ).then_inc(glayer_weights, 16)
                    edge_loads(l * T)
                for n in range(3):
                    edge_loads((L + n) * T)
                for c, (t0, nt) in enumerate(CH):
                    sp.wait_ge(goutput_ready, c + 1)
                    sp.dma_start(out.rearrange("(t p) f -> p t f", p=P)[:, t0:t0 + nt, :],
                                 gX[:, t0:t0 + nt, :]).then_inc(goutput_stored, 16)
                sp.wait_ge(goutput_stored, 16 * NC)

        @block.gpsimd
        def _(pool):
            pool.memset(mhalf[:, :], -0.5).then_inc(mhalf_set, 1)
            pool.iota(wtop, [[-W, KW * PW]], base=int(TOP), channel_multiplier=0,
                      allow_small_or_imprecise_dtypes=True).then_inc(window_starts, 1)
            pool.memset(row_len, float(NS)).then_inc(row_len_set, 1)
            pool.iota(wtop_p, [[-W * PW, KW]], base=int(TOP), channel_multiplier=-W,
                      allow_small_or_imprecise_dtypes=True).then_inc(window_starts, 1)
            pool.memset(ident[:, :], 0.0).then_inc(ident_set, 1)
            pool.wait_ge(ident_set, 1)
            pool.affine_select(out=ident[:, :], in_=ident[:, :], compare_op=ALU.not_equal, fill=1.0,
                               base=0, pattern=[[-1, 128]], channel_multiplier=1).then_inc(ident_set, 1)
            pool.iota(wstart1, [[W * PW, KW]], base=-1, channel_multiplier=W,
                      allow_small_or_imprecise_dtypes=True).then_inc(window_starts, 1)
            pool.iota(iotaP, [[1, P], [0, J]], base=0, channel_multiplier=0,
                      allow_small_or_imprecise_dtypes=True).then_inc(onehot_iotas, 1)
            pool.iota(iotaK, [[1, W * T], [0, J]], base=1, channel_multiplier=0,
                      allow_small_or_imprecise_dtypes=True).then_inc(onehot_iotas, 1)
            pool.wait_ge(rows_found, 1)
            pool.wait_ge(table_loaded, 64)
            for k in range(KW):
                pool.indirect_dma_start(out=Gt[:, k, :], out_offset=None, in_=table[:, :],
                                        in_offset=bass.IndirectOffsetOnAxis(ap=idx[:, k:k + 1], axis=0)
                                        ).then_inc(rows_gathered[k], 16)
            pool.wait_ge(mhalf_set, 1)
            for n, (c0, c1) in enumerate(NORMS):
                t0, t1 = CH[c0][0], CH[c1 - 1][0] + CH[c1 - 1][1]
                pool.wait_ge(variances_ready, n + 1)
                pool.tensor_tensor(lnsc[0:P, t0:t1], mv[0:P, t0:t1, 1], mhalf[0:P, t0:t1], ALU.pow).then_inc(roots_ready, 1)
                pool.wait_ge(roots_ready, n + 1)
                for t in range(t0, t1):
                    pool.tensor_scalar(X32[0:P, t, :], X32[0:P, t, :], mv[0:P, t, 0:1], lnsc[0:P, t:t + 1],
                                       ALU.subtract, ALU.mult).then_inc(tile_normalized, 1)
            for c, (t0, nt) in enumerate(CH):
                pool.wait_ge(encoded_copied, c + 1)
                pool.tensor_copy(H16[0:P, 0, t0:t0 + nt, 0, :],
                                 yS[0:P, 0:nt * F].rearrange("p (t f) -> p t f", t=nt)).then_inc(encoded_hi, 1)
                pool.wait_ge(encoded_hi, c + 1)
                pool.tensor_tensor(H16[0:P, 0, t0:t0 + nt, 1, :],
                                   yS[0:P, 0:nt * F].rearrange("p (t f) -> p t f", t=nt),
                                   H16[0:P, 0, t0:t0 + nt, 0, :], ALU.subtract).then_inc(encoded_lo, 1)
            pool.wait_ge(variances_ready, len(NORMS) + 1)
            pool.tensor_tensor(dinv[0:P, :], deg[0:P, :], mhalf[0:P, :], ALU.pow).then_inc(roots_ready, 1)
            def low_half(c):
                t0, nt = CH[c]
                pool.wait_ge(input2_hi, c + 1)
                pool.tensor_tensor(V16[0:P, t0:t0 + nt, 1, :], U32[:, t0:t0 + nt, :], V16[0:P, t0:t0 + nt, 0, :],
                                   ALU.subtract).then_inc(input2_lo, 1)

            for c, (t0, nt) in enumerate(CH):
                pool.wait_ge(variances_ready, len(NORMS) + 2 + c)
                pool.tensor_tensor(lnsc[0:P, t0:t0 + nt], mv[0:P, t0:t0 + nt, 1], mhalf[0:P, 0:nt], ALU.pow
                                   ).then_inc(roots_ready, 1)
                if c == NC - 5:
                    pool.wait_ge(sum_ready, L * NC)
                    pool.memset(onesL, 1.0).then_inc(late_ones_set, 1)
                    low_half(0)
                if c >= NC - 5:
                    low_half(c - NC + 6)
            low_half(NC - 1)
            pool.wait_ge(flag_ready, 1)
            with pool.If(pool.value_load(flag[0:1, 0:1], min_val=0, max_val=1000) > 0):
                for k in range(2):
                    pool.wait_ge(gvariances_ready, k + 1)
                    pool.tensor_tensor(lnsc[0:P, :], mv[0:P, :, 1], mhalf[0:P, :], ALU.pow).then_inc(groots_ready, 1)
                pool.wait_ge(gdegrees, 1)
                pool.tensor_tensor(gD, gD, mhalf[:, 0:1].to_broadcast([128, N]), ALU.pow).then_inc(gdegree_roots, 1)

        @block.vector
        def _(dve):
            n = [0]

            def link(ins):
                n[0] += 1
                ins.then_inc(vector_chain, 1)
                dve.wait_ge(vector_chain, n[0])

            dve.wait_ge(samples_loaded, 16)
            link(nc.vector.tensor_scalar(samp, samp_i[:, :, 0], -1.0, TOP, ALU.mult, ALU.add))
            dve.wait_ge(window_starts, 1)
            link(nc.vector.tensor_scalar(full, wtop, samp[:, NS - 1:NS], None, ALU.is_lt))
            nc.vector.scalar_tensor_tensor(part, wtop, samp[:, 0:1], full, ALU.is_lt, ALU.subtract).then_inc(compares_ready, 1)
            dve.wait_ge(window_starts, 3)
            dve.wait_ge(samples_counted, 1)
            link(nc.vector.tensor_tensor(inrow, PS[0][0:PW, 0:KW * NS].rearrange("p (k n) -> p k n", k=KW),
                                         wtop_p.unsqueeze(2).to_broadcast([PW, KW, NS]), ALU.is_gt))
            link(nc.vector.tensor_reduce(cnt, inrow, AX.X, ALU.add))
            link(nc.vector.scalar_tensor_tensor(cnt, PS[1][0:PW, 0:KW], -1.0, cnt, ALU.add, ALU.add))
            nc.vector.tensor_scalar(idx, cnt, 0.0, float(TR - 1), ALU.max, ALU.min).then_inc(rows_found, 1)

            def norm_stats(t0, t1):
                for t in range(t0, t1):
                    last = nc.vector.bn_stats(stat[0:P, t - t0, :], X32[0:P, t, :])
                link(last)
                for t in range(t0, t1):
                    last = nc.vector.bn_aggr(mv[0:P, t, :], stat[0:P, t - t0, :])
                link(last)

            def first_norm(c0, c1):
                for t0, nt in CH[c0:c1]:
                    norm_stats(t0, t0 + nt)
                t0, t1 = CH[c0][0], CH[c1 - 1][0] + CH[c1 - 1][1]
                nc.vector.tensor_scalar(mv[0:P, t0:t1, 1], mv[0:P, t0:t1, 1], 1e-5, None, ALU.add).then_inc(variances_ready, 1)

            dve.wait_ge(x_loaded, 16)
            first_norm(*NORMS[0])
            for k in range(KW):
                dve.wait_ge(rows_gathered[k], 16)
            sr, ds = Gt[:, :, 0:SL], Gt[:, :, SL:2 * SL]
            link(nc.vector.tensor_scalar(tf, sr, -float((P - 1) // 2), 1.0 / P, ALU.add, ALU.mult))
            link(nc.vector.tensor_scalar(tf, tf, MAGIC, MAGIC, ALU.add, ALU.subtract))
            link(nc.vector.scalar_tensor_tensor(pf, tf, -float(P), sr, ALU.mult, ALU.add))
            for k in range(KW):
                last = nc.vector.tensor_scalar(kf[:, k, :], ds[:, k, :], wstart1[:, k:k + 1], None, ALU.subtract)
            link(last)
            link(nc.vector.scalar_tensor_tensor(tf, tf, float(W), kf, ALU.mult, ALU.add))
            link(nc.vector.scalar_tensor_tensor(tf, kf, 1.0, tf, ALU.is_ge, ALU.mult))
            nc.vector.scalar_tensor_tensor(kf, kf, float(W), tf, ALU.is_le, ALU.mult).then_inc(keys_ready, 1)
            dve.wait_ge(ident_set, 2)
            nc.vector.tensor_copy(ident16[:, :], ident[:, :]).then_inc(ident16_set, 1)
            for cs in NORMS[1:]:
                first_norm(*cs)
            dve.wait_ge(keys_transposed, 1)
            for v, b in ((pT, 0), (kT, 2)):
                nc.vector.tensor_copy(v[:, 0:4 * PW], PS[b][0:SL, 0:4 * PW])
                last = nc.vector.tensor_copy(v[:, 4 * PW:KW * PW], PS[b + 1][0:SL, 0:(KW - 4) * PW])
            link(last)
            dve.sem_inc(keys_copied, 1)
            dve.wait_ge(onehot_iotas, 2)
            with dve.Fori(0, NBT // BL) as i:
                for k in range(BL):
                    dve.wait_ge(windows_counted, i * (BL * len(GW)) + (k + 1) * len(GW))
                    for oh, io, v, n_ in ((ohP, iotaP, pT, P), (ohK, iotaK, kT, W * T)):
                        last = nc.vector.tensor_tensor(
                            oh[:, k, :, :], io,
                            v[:, bass.ds(i * (BL * J) + k * J, J)].unsqueeze(1).to_broadcast([SL, n_, J]), ALU.is_equal)
                    last.then_inc(onehots_ready, 1)

            def decoder_bias(c):
                t0, nt = CH[c]
                dve.wait_ge(dec2_product, c + 1)
                y = yS[0:P, 0:nt * F].rearrange("p (t f) -> p t f", t=nt)
                nc.vector.tensor_tensor(y, PS[CB][0:P, 0:nt * F].rearrange("p (t f) -> p t f", t=nt),
                                        dec2b[0:P, :].unsqueeze(1).to_broadcast([P, nt, F]),
                                        ALU.add).then_inc(dec2_biased, 1)

            def decoded(c):
                t0, nt = CH[c]
                if c == 0:
                    dve.wait_ge(x_reloaded, 16)
                y = yS[0:P, 0:nt * F].rearrange("p (t f) -> p t f", t=nt)
                dve.wait_ge(sigmoid_ready, c + 1)
                link(nc.vector.tensor_tensor(X32[0:P, t0:t0 + nt, :], X32[0:P, t0:t0 + nt, :], y, ALU.add))
                norm_stats(t0, t0 + nt)
                nc.vector.tensor_scalar(mv[0:P, t0:t0 + nt, 1], mv[0:P, t0:t0 + nt, 1], 1e-5, None, ALU.add
                                        ).then_inc(variances_ready, 1)

            def norm_scales(c):
                t0, nt = CH[c]
                dve.wait_ge(roots_ready, len(NORMS) + 1 + c + 1)
                sc = lnsc[0:P, t0:t0 + nt]
                link(nc.vector.scalar_tensor_tensor(sc, dinv[0:P, t0:t0 + nt], S1, sc, ALU.mult, ALU.mult))
                nc.vector.scalar_tensor_tensor(lnb[0:P, t0:t0 + nt], mv[0:P, t0:t0 + nt, 0], -1.0, sc,
                                               ALU.mult, ALU.mult).then_inc(scales2_ready, 1)

            def degrees():
                dve.wait_ge(degree_summed, T)
                link(nc.vector.tensor_reduce(chk[0:P, 0:1], deg[0:P, :], AX.X, ALU.add))
                nc.vector.tensor_scalar(deg[0:P, :], deg[0:P, :], 1.0, 1.0, ALU.add, ALU.max).then_inc(variances_ready, 1)
                dve.wait_ge(roots_ready, len(NORMS) + 1)
                link(nc.vector.tensor_scalar(dinvs[0:P, :], dinv[0:P, :], S0, None, ALU.mult))

            def high_half(c):
                t0, nt = CH[c]
                dve.wait_ge(input2_ready, t0 + nt)
                nc.vector.tensor_copy(V16[0:P, t0:t0 + nt, 0, :], U32[:, t0:t0 + nt, :]).then_inc(input2_hi, 1)

            def decoded_tail():
                decoder_bias(NC - 1)
                norm_scales(NC - 2)
                decoded(NC - 1)
                norm_scales(NC - 1)
                for c in range(NC - 2, NC):
                    high_half(c)
                dve.wait_ge(weights2_loaded, 48)
                dve.wait_ge(input2_ready, T)
                link(nc.vector.tensor_tensor(X32[0:P], X32[0:P], l1b2[0:P, :].unsqueeze(1).to_broadcast([P, T, F]),
                                             ALU.add))
                for c in range(NC + 2):
                    if c < NC:
                        n0, w = CH[c][0] * P, CH[c][1] * P
                        dve.wait_ge(sum1_ready, c + 1)
                        dve.wait_ge(scales_copied, c + 1)
                        if c >= 1:
                            dve.wait_ge(expand_product, 2 * c)
                        nc.vector.scalar_tensor_tensor(aggS[:, 0:w], PS[AGG[(c + 1) % 2]][:, 0:w], 1.0 / S1,
                                                       dinvB[:, n0:n0 + w], ALU.mult, ALU.mult).then_inc(sum1_scaled, 1)
                    if c >= 2:
                        t0, nt = CH[c - 2]
                        dve.wait_ge(projected_hi, c - 1)
                        for j in range(nt):
                            last = nc.vector.scalar_tensor_tensor(
                                Z16[:, t0 + j, 1, :], PS[IB][0:P, j * F:j * F + F], dinvs[0:P, t0 + j:t0 + j + 1],
                                Z16[:, t0 + j, 0, :], ALU.mult, ALU.subtract)
                        last.then_inc(projected_lo, 1)
                link(nc.vector.tensor_reduce(chk[0:P, 2:3], Z16[:, :, 0, :], AX.XY, ALU.max, apply_absolute_value=True))
                nc.vector.tensor_scalar(chk[0:P, 2:3], chk[0:P, 2:3], LIMIT * S0, None, ALU.is_gt).then_inc(check_ready, 1)
                dve.wait_ge(check_summed, 1)
                nc.vector.tensor_scalar(flag_f[:, 0:1], PS[RB][0:1, 0:1], float(E), None, ALU.not_equal)
                nc.vector.tensor_copy(flag_f[:, 1:2], PS[RB][0:1, 1:2])
                link(nc.vector.tensor_copy(flag_f[:, 2:3], PS[RB][0:1, 2:3]))
                link(nc.vector.tensor_reduce(flag_f[:, 3:4], flag_f[:, 0:3], AX.X, ALU.add))
                nc.vector.tensor_copy(flag[:, :], flag_f[:, 3:4]).then_inc(flag_ready, 1)
                for c, (t0, nt) in enumerate(CH):
                    dve.wait_ge(sum2_transposed, c + 1)
                    for j in range(nt):
                        last = nc.vector.scalar_tensor_tensor(
                            OUT[:, t0 + j, :], PS[TB][0:P, j * F:j * F + F], dinv[0:P, t0 + j:t0 + j + 1],
                            X32[0:P, t0 + j, :], ALU.mult, ALU.add)
                    last.then_inc(output_ready, 1)

            dve.wait_ge(weights_loaded, 14 * 16)
            nc.vector.tensor_tensor(bias[:, 0:2], bias[:, 9:11], bias[:, 12:14], ALU.add)
            nc.vector.tensor_copy(bias[:, 2:3], bias[:, 14:15])
            nc.vector.tensor_copy(bias[:, 3:4], bias[:, 11:12]).then_inc(gate_biases, 1)

            link(nc.vector.memset(chk[:, :], 0.0))
            dve.wait_ge(encoded_lo, NC)
            link(nc.vector.tensor_reduce(chk[:, 1:2], HT[:, :], AX.X, ALU.max, apply_absolute_value=True))
            link(nc.vector.tensor_scalar(chk[:, 1:2], chk[:, 1:2], LIMIT, None, ALU.is_gt))
            for l in range(L):
                for c in range(NC + 2):
                    q = l * NC + c
                    if c < NC:
                        for m in cgroups(q):
                            if m % 2 == 0:
                                evac_block_group(dve, m)
                    if 1 <= c <= NC:
                        n0, w = CH[c - 1][0] * P, CH[c - 1][1] * P
                        H = HT[:, n0:n0 + w]
                        dve.wait_ge(hidden_product, q)
                        dve.wait_ge(reset_gate, q)
                        nc.vector.scalar_tensor_tensor(rS[:, 0:w], PS[NB][:, 0:w], bias[:, B_HN:B_HN + 1],
                                                       rS[:, 0:w], ALU.add, ALU.mult).then_inc(reset_hidden, 1)
                        if l == L - 1 and c == NC - 1:
                            high_half(0)
                        dve.wait_ge(reset_hidden, q)
                        dve.wait_ge(input_product, q)
                        nc.vector.tensor_tensor(rS[:, 0:w], PS[IB][:, 0:w], rS[:, 0:w], ALU.add).then_inc(new_input, 1)
                    if c >= 2 and l < L - 1:
                        t0, nt = CH[c - 2]
                        dve.wait_ge(state_hi, q - 1)
                        nc.vector.scalar_tensor_tensor(
                            H16[0:P, (l + 1) % 2, t0:t0 + nt, 1, :],
                            PS[TB][0:P, 0:nt * F].rearrange("p (t f) -> p t f", t=nt), S0,
                            H16[0:P, (l + 1) % 2, t0:t0 + nt, 0, :], ALU.mult, ALU.subtract).then_inc(state_lo, 1)
                    if 1 <= c <= NC:
                        dve.wait_ge(new_gate, q)
                        link(nc.vector.tensor_tensor(H, H, nS[:, 0:w], ALU.subtract))
                        link(nc.vector.tensor_tensor(H, H, zS[:, 0:w], ALU.mult))
                        last = nc.vector.tensor_tensor(H, H, nS[:, 0:w], ALU.add)
                        if l == L - 1:
                            link(last)
                            last = nc.vector.tensor_scalar(H, H, 0.0, None, ALU.max)
                        last.then_inc(state_ready, 1)
                    if l == L - 1 and c == 0:
                        degrees()
                    if l == L - 1 and c >= 3:
                        if NC - 1 <= c <= NC:
                            high_half(c - NC + 2)
                        decoder_bias(c - 3)
                        if c >= 4:
                            norm_scales(c - 4)
                        decoded(c - 3)
                        if c >= NC:
                            high_half(c - NC + 3)
            decoded_tail()
            dve.wait_ge(flag_ready, 1)
            with dve.If(dve.value_load(flag[0:1, 0:1], min_val=0, max_val=1000) > 0):
                general_vector(dve)
        @block.tensor
        def _(pe):
            pe.sem_inc(windows_counted, BL * len(GW))
            pe.wait_ge(row_len_set, 1)
            pe.wait_ge(compares_ready, 1)
            for k in range(KW):
                ks = slice(k * PW, (k + 1) * PW)
                nc.tensor.matmul(PS[0][0:PW, k * NS:(k + 1) * NS], part[:, ks], samp, start=True, stop=True)
                last = nc.tensor.matmul(PS[1][0:PW, k:k + 1], full[:, ks], row_len, start=True, stop=True)
            last.then_inc(samples_counted, 1)
            pe.wait_ge(keys_ready, 1)
            pe.wait_ge(ident_set, 2)
            for b, v in ((0, pf), (2, kf)):
                for k in range(KW):
                    last = nc.tensor.transpose(PS[b + k // 4][0:SL, (k % 4) * PW:(k % 4) * PW + PW],
                                               v[:, k, :], ident[0:PW, 0:PW])
            last.then_inc(keys_transposed, 1)

            def windows(b):
                pe.wait_ge(onehots_ready, b + 1)
                j = 0
                for g, gw in enumerate(GW):
                    n = b * len(GW) + g
                    pe.wait_ge(window_bank_free, n + 1)
                    for w in range(gw):
                        last = nc.tensor.matmul(PS[WBANK[n % BANKS]][0:P, w * W * T:(w + 1) * W * T],
                                                ohP[:, b % BL, :, j], ohK[:, b % BL, :, j], start=True, stop=True)
                        j += 1
                    last.then_inc(windows_counted, 1)

            def combine(l):
                pe.wait_ge(encoded_copied, NC)
                if l >= 1:
                    pe.wait_ge(comb_copied, l)
                nc.tensor.matmul(PS[EB][:, 0:G], convT[:, l, :], wih, start=True, stop=True).then_inc(comb_product, 1)

            def encoder(s, part):
                if part == 0 and s < NC:
                    t0, nt = CH[s]
                    pe.wait_ge(tile_normalized, t0 + nt)
                    if s >= 1:
                        pe.wait_ge(x_copied, s)
                    for j in range(nt):
                        last = nc.tensor.transpose(PS[EA][:, j * P:(j + 1) * P], X32[0:P, t0 + j, :], ident[0:P, 0:P])
                    last.then_inc(x_transposed, 1)
                if part == 1 and s >= 1:
                    w = CH[s - 1][1] * P
                    pe.wait_ge(enc1_relu, s)
                    if s >= 2:
                        pe.wait_ge(state_encoded, s - 1)
                    nc.tensor.matmul(PS[EC2][:, 0:w], enc2, rS[:, 0:w], start=True, stop=True).then_inc(enc2_product, 1)
                if part == 2 and s < NC:
                    w = CH[s][1] * P
                    pe.wait_ge(x_copied, s + 1)
                    if s == 0:
                        pe.wait_ge(weights_loaded, 14 * 16)
                    else:
                        pe.wait_ge(enc1_relu, s)
                    nc.tensor.matmul(PS[EC1][:, 0:w], enc1, aggS[:, 0:w], start=True, stop=True).then_inc(enc1_product, 1)
                if part == 3 and s >= 1:
                    t0, nt = CH[s - 1]
                    pe.wait_ge(state_encoded, s)
                    if s >= 2:
                        pe.wait_ge(encoded_copied, s - 1)
                    for j in range(nt):
                        last = nc.tensor.transpose(PS[EB][0:P, j * F:(j + 1) * F],
                                                   HT[:, (t0 + j) * P:(t0 + j + 1) * P], ident[:, :])
                    last.then_inc(encoded_transposed, 1)

            def aggregate(bank, w, n0, adj, halves, c, groups=(), loops=False, ready=None, between=None):
                m = list(groups)
                for t in range(T):
                    if between is not None and t % TC == 0:
                        between(t // TC)
                    if ready is not None and t % TC == 0:
                        pe.wait_ge(*ready(t // TC))
                    for h in range(2):
                        last = nc.tensor.matmul(bank[:, 0:w], halves[0:P, t, h, :], adj[0:P, t, n0:n0 + w],
                                                start=(t == 0 and h == 0), stop=(t == T - 1 and h == 1 and not loops))
                    if m and t in SPOT:
                        block_group(m.pop(0))
                if loops:
                    t0, nt = CH[c]
                    for j in range(nt):
                        for h in range(2):
                            last = nc.tensor.matmul(bank[:, j * P:(j + 1) * P], halves[0:P, t0 + j, h, :],
                                                    ident16[0:P, 0:P], start=False, stop=(j == nt - 1 and h == 1))
                return last

            def block_group(m):
                if m == 0:
                    pe.wait_ge(sum_copied, AHEAD - 1)
                else:
                    pe.wait_ge(blocks_copied[(m - 1) % 2], (m - 1) // 2 + 1)
                b0, nb = 4 * m, min(4, NBLK - 4 * m)
                for j in range(nb):
                    tr, tc = divmod(b0 + j, T)
                    last = nc.tensor.matmul(PS[CB][0:P, j * P:(j + 1) * P], AT3[0:P, tc, tr * P:(tr + 1) * P],
                                            ident16[0:P, 0:P], start=True, stop=True)
                last.then_inc(blocks_ready, 1)

            def gates(l, q, c, groups=()):
                n0, w = CH[c][0] * P, CH[c][1] * P
                H = HT[:, n0:n0 + w]
                cl = comb[:, l % 2, :]
                pe.wait_ge(reset_gate, q) if q else pe.wait_ge(window_bank_free, NBT * len(GW) + 1)
                nc.tensor.matmul(PS[RB][:, 0:w], whh[:, 0:F], H, start=True, stop=False)
                for m in groups[0:1]:
                    block_group(m)
                pe.wait_ge(update_gate, q) if q else pe.wait_ge(window_bank_free, NBT * len(GW) + 2)
                nc.tensor.matmul(PS[ZB][:, 0:w], whh[:, F:2 * F], H, start=True, stop=False)
                pe.wait_ge(reset_hidden, q) if q else pe.wait_ge(window_bank_free, NBT * len(GW) + 3)
                nc.tensor.matmul(PS[NB][:, 0:w], whh[:, 2 * F:G], H, start=True, stop=True).then_inc(hidden_product, 1)
                for m in groups[1:2]:
                    block_group(m)
                pe.wait_ge(sum_copied, q + 1)
                if c == 0:
                    pe.wait_ge(comb_loaded[l % 2], 16 * (l // 2 + 1))
                nc.tensor.matmul(PS[RB][:, 0:w], cl[:, 0:F], aggS[:, 0:w], start=False, stop=True).then_inc(reset_product, 1)
                nc.tensor.matmul(PS[ZB][:, 0:w], cl[:, F:2 * F], aggS[:, 0:w], start=False, stop=True).then_inc(update_product, 1)
                for m in groups[2:]:
                    block_group(m)
                pe.wait_ge(new_input, q) if q else None
                nc.tensor.matmul(PS[IB][:, 0:w], cl[:, 2 * F:G], aggS[:, 0:w], start=True, stop=True).then_inc(input_product, 1)

            def decode1(c):
                n0, w = CH[c][0] * P, CH[c][1] * P
                pe.wait_ge(state_ready, (L - 1) * NC + c + 1)
                if c == 0:
                    pe.wait_ge(state_lo, (L - 1) * NC)
                else:
                    pe.wait_ge(dec1_relu, c)
                nc.tensor.matmul(PS[TB][:, 0:w], dec1[:, :], HT[:, n0:n0 + w], start=True, stop=True).then_inc(dec1_product, 1)

            def decode2(c):
                t0, nt = CH[c]
                pe.wait_ge(dec1_relu, c + 1)
                if c == 0:
                    pe.wait_ge(blocks_copied[0], (NCG + 1) // 2)
                    pe.wait_ge(blocks_copied[1], NCG // 2)
                else:
                    pe.wait_ge(dec2_biased, c)
                for j in range(nt):
                    last = nc.tensor.matmul(PS[CB][0:P, j * F:(j + 1) * F], HT[:, (t0 + j) * P:(t0 + j + 1) * P],
                                            dec2[:, :], start=True, stop=True)
                last.then_inc(dec2_product, 1)

            def state_back(l, c):
                t0, nt = CH[c]
                q = l * NC + c
                pe.wait_ge(state_ready, q + 1)
                if q >= 1:
                    pe.wait_ge(state_lo, q)
                for j in range(nt):
                    last = nc.tensor.transpose(PS[TB][0:P, j * F:(j + 1) * F],
                                               HT[:, (t0 + j) * P:(t0 + j + 1) * P], ident[:, :])
                last.then_inc(state_transposed, 1)

            def last_chunks(l):
                def step(g):
                    if g == 2:
                        gates(l, (l + 1) * NC - 1, NC - 1)
                    if g == NC - 3:
                        state_back(l, NC - 2)
                    if g == NC - 2:
                        state_back(l, NC - 1)
                return step

            def aggregate_part(q, g):
                pe.wait_ge(encoded_lo, g + 1)
                t0, nt = CH[g]
                n0, w = CH[q][0] * P, CH[q][1] * P
                for t in range(t0, t0 + nt):
                    for h in range(2):
                        last = nc.tensor.matmul(agg_bank(q)[:, 0:w], H16[0:P, 0, t, h, :], AT3[0:P, t, n0:n0 + w],
                                                start=(t == 0 and h == 0), stop=(t == T - 1 and h == 1))
                if g == NC - 1:
                    last.then_inc(sum_ready, 1)

            for b in range(NBT):
                windows(b)
                if b < ENC:
                    encoder(*divmod(b, 4))
                if b in COMB:
                    combine(COMB.index(b))
                if b in PART:
                    aggregate_part(*PART[b])
            pe.wait_ge(ident16_set, 1)

            for l in range(L):
                for c in range(NC):
                    q = l * NC + c
                    if AHEAD <= q:
                        n0, w = CH[c][0] * P, CH[c][1] * P
                        if q >= 2:
                            pe.wait_ge(sum_copied, q - 1)
                        ready = between = None
                        if c == 0 and l >= 1:
                            ready = lambda g: (state_lo, (l - 1) * NC + g + 1)
                            between = last_chunks(l - 1)
                        aggregate(agg_bank(q), w, n0, AT3, H16[:, l % 2], c, cgroups(q)[0:len(SPOT)], ready=ready,
                                  between=between).then_inc(sum_ready, 1)
                    if 1 <= c <= NC:
                        gates(l, q - 1, c - 1, cgroups(q)[len(SPOT):])
                    if 2 <= c and l < L - 1:
                        state_back(l, c - 2)
                    if l == L - 1:
                        if 2 <= c:
                            decode1(c - 2)
                        if 3 <= c:
                            decode2(c - 3)

            def last_decodes(g):
                if g == 1:
                    gates(L - 1, L * NC - 1, NC - 1)
                if g == 2:
                    decode1(NC - 2)
                    decode2(NC - 3)
                if g == 3:
                    decode1(NC - 1)
                    decode2(NC - 2)
                if g == 4:
                    decode2(NC - 1)
                if g >= 2:
                    for c in range(2 * g - 4, min(2 * g - 2, NC)):
                        column_scales(c)

            def column_scales(c):
                t0, nt = CH[c]
                if c == 0:
                    pe.wait_ge(roots_ready, len(NORMS) + 1)
                    pe.wait_ge(update_gate, L * NC)
                if c >= 2:
                    pe.wait_ge(scales_copied, c - 1)
                for j in range(nt):
                    last = nc.tensor.matmul(PS[RB + c % 2][:, j * P:(j + 1) * P],
                                            dinv[0:P, t0 + j:t0 + j + 1].to_broadcast([P, 128]),
                                            ident[0:P, 0:P], start=True, stop=True)
                last.then_inc(scales_product, 1)

            def expand(c):
                w = CH[c][1] * P
                pe.wait_ge(sum1_scaled, c + 1)
                if c == 0:
                    pe.wait_ge(weights2_loaded, 48)
                    pe.wait_ge(scales_copied, NC)
                else:
                    pe.wait_ge(expand_relu, 2 * c)
                for k in range(HID // F):
                    nc.tensor.matmul(PS[RB + k][:, 0:w], w1[:, k * F:(k + 1) * F], aggS[:, 0:w],
                                     start=True, stop=True).then_inc(expand_product, 1)

            def project(c):
                nt = CH[c][1]
                pe.wait_ge(expand_relu, 2 * (c + 1))
                if c >= 1:
                    pe.wait_ge(projected_lo, c)
                for j in range(nt):
                    for k in range(HID // F):
                        last = nc.tensor.matmul(PS[IB][0:P, j * F:(j + 1) * F],
                                                (rS, zS)[k][:, j * P:(j + 1) * P], w2[:, k, :],
                                                start=(k == 0), stop=(k == 1))
                last.then_inc(project_product, 1)

            def last_projections(g):
                if g == 1:
                    expand(NC - 1)
                if g == 2:
                    project(NC - 2)
                if g == 4:
                    project(NC - 1)

            pe.wait_ge(sum_copied, L * NC - 1)
            for c in range(NC):
                n0, w = CH[c][0] * P, CH[c][1] * P
                if c >= 2:
                    pe.wait_ge(sum1_scaled, c - 1)
                if c == 1:
                    pe.wait_ge(sum_copied, L * NC)
                aggregate(PS[AGG[(c + 1) % 2]], w, n0, CT3, V16, c, loops=True,
                          ready=(lambda g: (input2_lo, g + 1)) if c == 0 else None,
                          between=last_decodes if c == 0 else None).then_inc(sum1_ready, 1)
                if c >= 1:
                    expand(c - 1)
                if c >= 2:
                    project(c - 2)
            for c in range(NC + 1):
                if c == 2:
                    pe.wait_ge(late_ones_set, 1)
                    pe.wait_ge(check_ready, 1)
                    nc.tensor.matmul(PS[RB][0:1, 0:3], onesL[:, 0:1], chk[:, 0:3], start=True, stop=True
                                     ).then_inc(check_summed, 1)
                if c < NC:
                    n0, w = CH[c][0] * P, CH[c][1] * P
                    if c < 2:
                        pe.wait_ge(sum1_scaled, NC - 1 + c)
                    else:
                        pe.wait_ge(sum2_copied, c - 1)
                    aggregate(PS[AGG[c % 2]], w, n0, CT3, Z16, c, loops=True,
                              ready=(lambda g: (projected_lo, g + 1)) if c == 0 else None,
                              between=last_projections if c == 0 else None).then_inc(sum2_ready, 1)
                if c >= 1:
                    nt = CH[c - 1][1]
                    pe.wait_ge(sum2_copied, c)
                    if c >= 2:
                        pe.wait_ge(output_ready, c - 1)
                    for j in range(nt):
                        last = nc.tensor.transpose(PS[TB][0:P, j * F:(j + 1) * F], aggS[:, j * P:(j + 1) * P],
                                                   ident[:, :])
                    last.then_inc(sum2_transposed, 1)

            pe.wait_ge(flag_ready, 1)
            with pe.If(pe.value_load(flag[0:1, 0:1], min_val=0, max_val=1000) > 0):
                general_tensor(pe)

        @block.scalar
        def _(act):
            def decode_sig(c):
                nt = CH[c][1]
                act.wait_ge(dec2_biased, c + 1)
                nc.scalar.activation(yS[0:P, 0:nt * F], yS[0:P, 0:nt * F], ACT.Sigmoid).then_inc(sigmoid_ready, 1)

            ndeg = [0]

            def degree(t):
                if ndeg[0] == 0:
                    act.wait_ge(comb_stored, 16)
                    act.wait_ge(window_bank_free, BANKS + NBT * len(GW))
                else:
                    act.wait_ge(degree_summed, ndeg[0])
                ndeg[0] += 1
                nc.scalar.activation(CT3[0:P, T - 1, :], AT3[0:P, t, 0:N], ACT.Copy, saturate=False,
                                     accum_out=deg[0:P, t:t + 1]).then_inc(degree_summed, 1)

            def column_scales(c):
                t0, nt = CH[c]
                act.wait_ge(scales_product, c + 1)
                if c == 0:
                    act.wait_ge(sum_ready, L * NC)
                nc.scalar.activation(dinvB[:, t0 * P:(t0 + nt) * P], PS[RB + c % 2][:, 0:nt * P], ACT.Copy
                                     ).then_inc(scales_copied, 1)

            def second_input(c):
                t0, nt = CH[c]
                if c == 0:
                    act.wait_ge(sum_ready, L * NC)
                act.wait_ge(scales2_ready, c + 1)
                for t in range(t0, t0 + nt):
                    nc.scalar.activation(U32[:, t, :], X32[0:P, t, :], ACT.Relu, bias=lnb[0:P, t:t + 1],
                                         scale=lnsc[0:P, t:t + 1]).then_inc(input2_ready, 1)

            def windows(b):
                for g in range(len(GW)):
                    n = b * len(GW) + g
                    w0 = b * J + sum(GW[:g])
                    gw = min(GW[g], NW - w0)
                    act.wait_ge(windows_counted, BL * len(GW) + n + 1)
                    nc.scalar.activation(
                        AT3[0:P, :, w0 * W:(w0 + gw) * W].rearrange("p t (w d) -> p w t d", w=gw),
                        PS[WBANK[n % BANKS]][0:P, 0:gw * W * T].rearrange("p (w t d) -> p w t d", w=gw, t=T),
                        ACT.Copy, saturate=False).then_inc(window_bank_free, 1)

            def encoder(s, part):
                if part == 0 and s < NC:
                    w = CH[s][1] * P
                    act.wait_ge(x_transposed, s + 1)
                    if s >= 1:
                        act.wait_ge(enc1_product, s)
                    nc.scalar.activation(aggS[:, 0:w], PS[EA][:, 0:w], ACT.Relu).then_inc(x_copied, 1)
                if part == 1 and s >= 1:
                    n0, w = CH[s - 1][0] * P, CH[s - 1][1] * P
                    act.wait_ge(enc2_product, s)
                    nc.scalar.activation(HT[:, n0:n0 + w], PS[EC2][:, 0:w], ACT.Identity, bias=bias[:, B_E2:B_E2 + 1]
                                         ).then_inc(state_encoded, 1)
                if part == 2 and s < NC:
                    w = CH[s][1] * P
                    act.wait_ge(enc1_product, s + 1)
                    if s == 0:
                        act.wait_ge(weights_loaded, 14 * 16)
                    else:
                        act.wait_ge(enc2_product, s)
                    nc.scalar.activation(rS[:, 0:w], PS[EC1][:, 0:w], ACT.Relu, bias=bias[:, B_E1:B_E1 + 1]
                                         ).then_inc(enc1_relu, 1)
                if part == 3 and s >= 1:
                    t0, nt = CH[s - 1]
                    act.wait_ge(encoded_transposed, s)
                    if s >= 2:
                        act.wait_ge(encoded_lo, s - 1)
                    nc.scalar.activation(yS[0:P, 0:nt * F], PS[EB][0:P, 0:nt * F], ACT.Copy, scale=S0).then_inc(encoded_copied, 1)

            act.wait_ge(keys_copied, 1)
            act.sem_inc(window_bank_free, BANKS)
            def aggregated(q):
                w = CH[q % NC][1] * P
                act.wait_ge(sum_ready, q + 1)
                if q >= 1:
                    act.wait_ge(input_product, q)
                nc.scalar.activation(aggS[:, 0:w], agg_bank(q)[:, 0:w], ACT.Copy, scale=1.0 / S0).then_inc(sum_copied, 1)

            for b in range(NBT):
                windows(b)
                if b < ENC:
                    encoder(*divmod(b, 4))
                if b in COMB:
                    act.wait_ge(comb_product, COMB.index(b) + 1)
                    nc.scalar.activation(combS[:, COMB.index(b), :], PS[EB][:, 0:G], ACT.Copy).then_inc(comb_copied, 1)
                if b == ENC + 4:
                    aggregated(0)
            act.wait_ge(gate_biases, 1)
            for l in range(L):
                for c in range(NC + 2):
                    q = l * NC + c
                    if c < NC:
                        for m in cgroups(q):
                            if m % 2 == 1:
                                evac_block_group(act, m)
                        if 0 <= q - 3 < T:
                            degree(q - 3)
                        if q >= 1:
                            aggregated(q)
                    if 1 <= c <= NC:
                        w = CH[c - 1][1] * P
                        act.wait_ge(reset_product, q)
                        if q >= 2:
                            act.wait_ge(new_gate, q - 1)
                        nc.scalar.activation(rS[:, 0:w], PS[RB][:, 0:w], ACT.Sigmoid, bias=bias[:, B_R:B_R + 1]
                                             ).then_inc(reset_gate, 1)
                        act.wait_ge(update_product, q)
                        if q >= 2:
                            act.wait_ge(state_ready, q - 1)
                        nc.scalar.activation(zS[:, 0:w], PS[ZB][:, 0:w], ACT.Sigmoid, bias=bias[:, B_Z:B_Z + 1]
                                             ).then_inc(update_gate, 1)
                    if l == L - 1 and NC - 1 <= c <= NC:
                        second_input(2 * (c - NC + 1))
                    if c >= 2 and l < L - 1:
                        t0, nt = CH[c - 2]
                        act.wait_ge(state_transposed, q - 1)
                        nc.scalar.activation(H16[0:P, (l + 1) % 2, t0:t0 + nt, 0, :],
                                             PS[TB][0:P, 0:nt * F].rearrange("p (t f) -> p t f", t=nt),
                                             ACT.Copy, scale=S0).then_inc(state_hi, 1)
                    if 1 <= c <= NC:
                        act.wait_ge(new_input, q)
                        nc.scalar.activation(nS[:, 0:w], rS[:, 0:w], ACT.Tanh, bias=bias[:, B_IN:B_IN + 1]
                                             ).then_inc(new_gate, 1)
                    if l == L - 1 and c == NC - 1:
                        second_input(1)
                    if l == L - 1 and c >= 2:
                        n0, w = CH[c - 2][0] * P, CH[c - 2][1] * P
                        act.wait_ge(dec1_product, c - 1)
                        nc.scalar.activation(HT[:, n0:n0 + w], PS[TB][:, 0:w], ACT.Relu, bias=bias[:, B_D1:B_D1 + 1]
                                             ).then_inc(dec1_relu, 1)
                    if l == L - 1 and c >= 3:
                        decode_sig(c - 3)
                    if l == L - 1 and c >= NC:
                        second_input(3 + c - NC)
                        for k in range(2 * (c - NC), 2 * (c - NC) + 2):
                            column_scales(k)
            decode_sig(NC - 1)
            second_input(5)
            column_scales(4)
            column_scales(5)
            second_input(6)
            column_scales(6)
            for c in range(1, NC + 2):
                if c <= NC:
                    w = CH[c - 1][1] * P
                    for k in range(HID // F):
                        act.wait_ge(expand_product, 2 * (c - 1) + k + 1)
                        if c >= 2:
                            act.wait_ge(project_product, c - 1)
                        nc.scalar.activation((rS, zS)[k][:, 0:w], PS[RB + k][:, 0:w], ACT.Relu,
                                             bias=bias[:, B_L1 + k:B_L1 + k + 1]).then_inc(expand_relu, 1)
                if c >= 1 and c <= NC:
                    t0, nt = CH[c - 1]
                    act.wait_ge(project_product, c)
                    for j in range(nt):
                        last = nc.scalar.activation(Z16[:, t0 + j, 0, :], PS[IB][0:P, j * F:j * F + F], ACT.Copy,
                                                    scale=dinvs[0:P, t0 + j:t0 + j + 1])
                    last.then_inc(projected_hi, 1)
            for c in range(NC):
                w = CH[c][1] * P
                act.wait_ge(sum2_ready, c + 1)
                if c >= 1:
                    act.wait_ge(sum2_transposed, c)
                nc.scalar.activation(aggS[:, 0:w], PS[AGG[c % 2]][:, 0:w], ACT.Copy, scale=1.0 / S0
                                     ).then_inc(sum2_copied, 1)
            act.wait_ge(flag_ready, 1)
            with act.If(act.value_load(flag[0:1, 0:1], min_val=0, max_val=1000) > 0):
                general_scalar(act)


_IN = ['x', 'src', 'dst', 'enc_w1T', 'enc_b1', 'enc_w2T', 'enc_b2', 'conv_wT', 'gru_wihT', 'gru_whhT',
       'gru_bih', 'gru_bhh', 'dec_w1T', 'dec_b1', 'dec_w2T', 'dec_b2', 'l1_w1T', 'l1_b1', 'l1_w2T', 'l1_b2']


def layout(inputs):
    import numpy as np
    a = {k: np.asarray(v) for k, v in inputs.items()}
    g = lambda n: a['L0_gnn_' + n]
    f = lambda n: a['L1_gnn_' + n]
    c = np.ascontiguousarray
    H = g('gru_whh').shape[1]
    return {
        'x': c(a['x']), 'src': c(a['src']), 'dst': c(a['dst']),
        'enc_w1T': c(g('enc_w1').T), 'enc_b1': c(g('enc_b1').reshape(-1, 1)),
        'enc_w2T': c(g('enc_w2').T), 'enc_b2': c(g('enc_b2').reshape(-1, 1)),
        'conv_wT': c(g('conv_w').transpose(0, 2, 1)),
        'gru_wihT': c(g('gru_wih').T), 'gru_whhT': c(g('gru_whh').T),
        'gru_bih': c(g('gru_bih').reshape(3, H).T), 'gru_bhh': c(g('gru_bhh').reshape(3, H).T),
        'dec_w1T': c(g('dec_w1').T), 'dec_b1': c(g('dec_b1').reshape(-1, 1)),
        'dec_w2T': c(g('dec_w2').T), 'dec_b2': c(g('dec_b2').reshape(1, -1)),
        'l1_w1T': c(f('W1').T), 'l1_b1': c(f('b1').reshape(2, -1).T),
        'l1_w2T': c(f('W2').T.reshape(2, H, -1).transpose(1, 0, 2)), 'l1_b2': c(f('b2').reshape(1, -1)),
    }


def kernel(**inputs):
    import numpy as np
    import concourse.bacc as bacc
    from concourse.bass_utils import run_bass_kernel_spmd

    nc = bacc.Bacc("TRN2", target_bir_lowering=False, num_devices=1)
    arrays = layout(inputs)
    args = [nc.dram_tensor(f"in_{n}", arrays[n].shape, mybir.dt.from_np(arrays[n].dtype),
                           kind="ExternalInput").ap() for n in _IN]
    out = nc.dram_tensor("out", inputs['x'].shape, mybir.dt.float32, kind="ExternalOutput").ap()
    gnn_kernel(nc, *args, out)
    r = run_bass_kernel_spmd(nc, [{f"in_{n}": arrays[n] for n in _IN}], core_ids=[0])
    return np.asarray(r.results[0]["out"])
```
